# Optimizing a Trainium2 kernel written in Bass

```python
import numpy as np
import jax
import jax.numpy as jnp

def _softmax(x, axis=-1):
    return jax.nn.softmax(x, axis=axis)

def _gelu(x):
    return jax.nn.gelu(x, approximate=True)

def _silu(x):
    return jax.nn.silu(x)

def _sigmoid(x):
    return jax.nn.sigmoid(x)

def _layernorm(x, axis=-1, eps=1e-05):
    m = jnp.mean(x, axis=axis, keepdims=True)
    v = jnp.var(x, axis=axis, keepdims=True)
    return (x - m) / jnp.sqrt(v + eps)

def _scatter_add(tgt, idx, src, axis=0):
    return tgt.at[idx].add(src)

def _segment_sum(src, seg, n):
    return jax.ops.segment_sum(src, seg, n)
kernel_name = 'mk_gnn_resnorm_d4_gnn_r8_476dd4'

def setup_inputs(seed: int=0):
    np.random.seed(seed)
    _w = jnp.asarray

    def _rec_inputs():
        import jax
        import jax.numpy as jnp
        _gk = jax.random.key(seed)
        x = -0.0005121 + 1.001 * jax.random.normal(jax.random.fold_in(_gk, 1), (12500, 32), jnp.float32)
        src = jax.random.randint(jax.random.fold_in(_gk, 2), (400000,), 0, 12500, jnp.int32)
        dst = jax.random.randint(jax.random.fold_in(_gk, 3), (400000,), 0, 12500, jnp.int32)
        _o = jnp.argsort(dst, stable=True)
        src = src[_o]
        dst = dst[_o]
        edge_attr_2 = jax.random.uniform(jax.random.fold_in(_gk, 12), (400000, 2), jnp.float32, 0.0, 1)
        edge_attr_32 = 0.000196303 + 1.00016 * jax.random.normal(jax.random.fold_in(_gk, 13), (400000, 32), jnp.float32)
        edge_type_4 = jax.random.randint(jax.random.fold_in(_gk, 15), (400000,), 0, 4, jnp.int32)
        return (x, src, dst, edge_attr_2, edge_attr_32, edge_type_4)
    x, src, dst, edge_attr_2, edge_attr_32, edge_type_4 = _rec_inputs()

    def _L0_gnn_setup():
        import jax, jax.numpy as jnp
        import numpy as np
        N_NODES = 12500
        IN_DIM = 32
        ENC_HID = 64
        OUT_DIM = 32
        N_EDGES = 200000

        def _gcn_forward(node_features, W1, b1, W2, b2, Wg, bg, src, dst):
            h0 = jax.nn.relu(node_features @ W1 + b1)
            h0 = jax.nn.relu(h0 @ W2 + b2)
            n = node_features.shape[0]
            loop = jnp.arange(n, dtype=src.dtype)
            s = jnp.concatenate([src, loop])
            d = jnp.concatenate([dst, loop])
            ones = jnp.ones(s.shape[0], dtype=h0.dtype)
            deg_out = jax.ops.segment_sum(ones, s, num_segments=n)
            deg_in = jax.ops.segment_sum(ones, d, num_segments=n)
            norm_src = jax.lax.rsqrt(jnp.clip(deg_out, 1.0))
            norm_dst = jax.lax.rsqrt(jnp.clip(deg_in, 1.0))
            m = (h0 * norm_src[:, None])[s]
            agg = jax.ops.segment_sum(m, d, num_segments=n)
            h1 = agg * norm_dst[:, None] @ Wg + bg
            h1 = jax.nn.relu(h1)
            return h0 + h1
        key = jax.random.key(seed)
        ks = jax.random.split(key, 10)
        node_features = jax.random.normal(ks[0], (N_NODES, IN_DIM), dtype=jnp.float32)
        edge_src = jax.random.randint(ks[1], (N_EDGES,), 0, N_NODES, dtype=jnp.int32)
        edge_dst = jax.random.randint(ks[2], (N_EDGES,), 0, N_NODES, dtype=jnp.int32)
        edgetypes = jax.random.randint(ks[3], (N_EDGES,), 0, 4, dtype=jnp.int32)
        s1 = 1.0 / np.sqrt(IN_DIM)
        s2 = 1.0 / np.sqrt(ENC_HID)
        W1 = jax.random.uniform(ks[4], (IN_DIM, ENC_HID), jnp.float32, -s1, s1)
        b1 = jax.random.uniform(ks[5], (ENC_HID,), jnp.float32, -s1, s1)
        W2 = jax.random.uniform(ks[6], (ENC_HID, OUT_DIM), jnp.float32, -s2, s2)
        b2 = jax.random.uniform(ks[7], (OUT_DIM,), jnp.float32, -s2, s2)
        g = np.sqrt(6.0 / (OUT_DIM + OUT_DIM))
        Wg = jax.random.uniform(ks[8], (OUT_DIM, OUT_DIM), jnp.float32, -g, g)
        bg = jnp.zeros((OUT_DIM,), dtype=jnp.float32)
        return dict(node_features=node_features, W1=W1, b1=b1, W2=W2, b2=b2, Wg=Wg, bg=bg, edge_src=edge_src, edge_dst=edge_dst, edgetypes=edgetypes)
    _L0_gnn_all = _L0_gnn_setup()
    _L0_gnn_in = {k: v for k, v in _L0_gnn_all.items() if k in ('W1', 'b1', 'W2', 'b2', 'Wg', 'bg')}
    del _L0_gnn_all

    def _L1_gnn_setup():
        import jax, jax.numpy as jnp
        import numpy as np
        N_NODES = 12500
        N_EDGES = 400000
        IN_CH = 32
        OUT_CH = 32
        DIM = 2
        KSIZE = 3

        def _basis(pseudo):
            p = jnp.clip(pseudo, 0.0, 1.0)
            grid = jnp.linspace(0.0, 1.0, KSIZE, dtype=p.dtype)
            dist = jnp.abs(p[:, :, None] - grid[None, None, :])
            b = jnp.maximum(1.0 - dist * (KSIZE - 1), 0.0)
            basis = jnp.einsum('ea,eb->eab', b[:, 0], b[:, 1])
            return basis.reshape(p.shape[0], -1)
        key = jax.random.key(seed)
        k1, k2, k3, k4, k5, k6 = jax.random.split(key, 6)
        x = jax.random.normal(k1, (N_NODES, IN_CH), dtype=jnp.float32)
        pseudo = jax.random.uniform(k2, (N_EDGES, DIM), dtype=jnp.float32)
        weight = jax.random.normal(k3, (KSIZE * KSIZE, IN_CH, OUT_CH), dtype=jnp.float32) / np.sqrt(IN_CH)
        root_w = jax.random.normal(k4, (OUT_CH, IN_CH), dtype=jnp.float32) / np.sqrt(IN_CH)
        root_b = jax.random.normal(k5, (OUT_CH,), dtype=jnp.float32) * 0.01
        edge_index = jax.random.randint(k6, (2, N_EDGES), 0, N_NODES, dtype=jnp.int64)
        return {'x': x, 'pseudo': pseudo, 'weight': weight, 'root_w': root_w, 'root_b': root_b, 'edge_index': edge_index}
    _L1_gnn_all = _L1_gnn_setup()
    _L1_gnn_in = {k: v for k, v in _L1_gnn_all.items() if k in ('weight', 'root_w', 'root_b')}
    del _L1_gnn_all

    def _L2_gnn_setup():
        import jax, jax.numpy as jnp
        import numpy as np
        N_NODES = 12500
        N_EDGES = 200000
        IN_FEAT = 32
        OUT_FEAT = 32

        def _gna_forward(feat, src, dst, w1_W, w1_b, w2_W, w2_b, a):
            n = feat.shape[0]
            h_src = feat[src]
            h_dst = feat[dst]
            dt = h_dst - h_src
            a_vec = a[0]
            aij = dt @ (w2_W.T @ a_vec) + jnp.dot(a_vec, w2_b)
            ss = h_src @ w2_W.T + w2_b
            m = jax.ops.segment_max(aij, dst, num_segments=n)
            aexp = jnp.exp(aij - m[dst])
            denom = jax.ops.segment_sum(aexp, dst, num_segments=n)
            alpha = aexp / denom[dst]
            res = jax.ops.segment_sum(alpha[:, None] * ss, dst, num_segments=n)
            out = res + feat @ w1_W.T + w1_b
            return out
        key = jax.random.key(seed)
        k = jax.random.split(key, 8)
        feat = jax.random.normal(k[0], (N_NODES, IN_FEAT), dtype=jnp.float32)
        src = jax.random.randint(k[1], (N_EDGES,), 0, N_NODES, dtype=jnp.int64)
        dst = jax.random.randint(k[2], (N_EDGES,), 0, N_NODES, dtype=jnp.int64)
        s1 = 1.0 / np.sqrt(IN_FEAT)
        w1_W = jax.random.uniform(k[3], (OUT_FEAT, IN_FEAT), jnp.float32, -s1, s1)
        w1_b = jax.random.uniform(k[4], (OUT_FEAT,), jnp.float32, -s1, s1)
        w2_W = jax.random.uniform(k[5], (OUT_FEAT, IN_FEAT), jnp.float32, -s1, s1)
        w2_b = jax.random.uniform(k[6], (OUT_FEAT,), jnp.float32, -s1, s1)
        a = jax.random.normal(k[7], (1, OUT_FEAT), dtype=jnp.float32)
        return {'feat': feat, 'src': src, 'dst': dst, 'w1_W': w1_W, 'w1_b': w1_b, 'w2_W': w2_W, 'w2_b': w2_b, 'a': a}
    _L2_gnn_all = _L2_gnn_setup()
    _L2_gnn_in = {k: v for k, v in _L2_gnn_all.items() if k in ('w1_W', 'w1_b', 'w2_W', 'w2_b', 'a')}
    del _L2_gnn_all

    def _L3_gnn_setup():
        import jax, jax.numpy as jnp
        import numpy as np
        N_NODES = 6250
        N_EDGES = 100000
        X_DIM = 32
        E_DIM = 32
        HID = 64
        OUT = 32
        key = jax.random.key(seed)
        ks = jax.random.split(key, 6)
        x = jax.random.normal(ks[0], (N_NODES, X_DIM), dtype=jnp.float32)
        edge_index = jax.random.randint(ks[1], (2, N_EDGES), 0, N_NODES, dtype=jnp.int64)
        edge_attr = jax.random.normal(ks[2], (N_EDGES, E_DIM), dtype=jnp.float32)
        in_dim = 2 * X_DIM + E_DIM
        W1 = jax.random.normal(ks[3], (in_dim, HID), dtype=jnp.float32) * (1.0 / np.sqrt(in_dim))
        b1 = jnp.zeros((HID,), dtype=jnp.float32)
        W2 = jax.random.normal(ks[4], (HID, OUT), dtype=jnp.float32) * (1.0 / np.sqrt(HID))
        b2 = jnp.zeros((OUT,), dtype=jnp.float32)
        return {'x': x, 'edge_index': edge_index, 'edge_attr': edge_attr, 'W1': W1, 'b1': b1, 'W2': W2, 'b2': b2}
    _L3_gnn_all = _L3_gnn_setup()
    _L3_gnn_in = {k: v for k, v in _L3_gnn_all.items() if k in ('W1', 'b1', 'W2', 'b2')}
    del _L3_gnn_all
    return {'x': x, 'src': src, 'dst': dst, 'edge_attr_2': edge_attr_2, 'edge_attr_32': edge_attr_32, 'edge_type_4': edge_type_4, 'L0_gnn_W1': _L0_gnn_in['W1'], 'L0_gnn_b1': _L0_gnn_in['b1'], 'L0_gnn_W2': _L0_gnn_in['W2'], 'L0_gnn_b2': _L0_gnn_in['b2'], 'L0_gnn_Wg': _L0_gnn_in['Wg'], 'L0_gnn_bg': _L0_gnn_in['bg'], 'L1_gnn_weight': _L1_gnn_in['weight'], 'L1_gnn_root_w': _L1_gnn_in['root_w'], 'L1_gnn_root_b': _L1_gnn_in['root_b'], 'L2_gnn_w1_W': _L2_gnn_in['w1_W'], 'L2_gnn_w1_b': _L2_gnn_in['w1_b'], 'L2_gnn_w2_W': _L2_gnn_in['w2_W'], 'L2_gnn_w2_b': _L2_gnn_in['w2_b'], 'L2_gnn_a': _L2_gnn_in['a'], 'L3_gnn_W1': _L3_gnn_in['W1'], 'L3_gnn_b1': _L3_gnn_in['b1'], 'L3_gnn_W2': _L3_gnn_in['W2'], 'L3_gnn_b2': _L3_gnn_in['b2']}

def reference(x, src, dst, edge_attr_2, edge_attr_32, edge_type_4, L0_gnn_W1, L0_gnn_b1, L0_gnn_W2, L0_gnn_b2, L0_gnn_Wg, L0_gnn_bg, L1_gnn_weight, L1_gnn_root_w, L1_gnn_root_b, L2_gnn_w1_W, L2_gnn_w1_b, L2_gnn_w2_W, L2_gnn_w2_b, L2_gnn_a, L3_gnn_W1, L3_gnn_b1, L3_gnn_W2, L3_gnn_b2):
    import jax
    import jax.numpy as jnp

    def _L0_gnn_ref(node_features, W1, b1, W2, b2, Wg, bg, edge_src, edge_dst, edgetypes):
        import jax, jax.numpy as jnp
        import numpy as np
        N_NODES = 12500
        IN_DIM = 32
        ENC_HID = 64
        OUT_DIM = 32
        N_EDGES = 200000

        def _gcn_forward(node_features, W1, b1, W2, b2, Wg, bg, src, dst):
            h0 = jax.nn.relu(node_features @ W1 + b1)
            h0 = jax.nn.relu(h0 @ W2 + b2)
            n = node_features.shape[0]
            loop = jnp.arange(n, dtype=src.dtype)
            s = jnp.concatenate([src, loop])
            d = jnp.concatenate([dst, loop])
            ones = jnp.ones(s.shape[0], dtype=h0.dtype)
            deg_out = jax.ops.segment_sum(ones, s, num_segments=n)
            deg_in = jax.ops.segment_sum(ones, d, num_segments=n)
            norm_src = jax.lax.rsqrt(jnp.clip(deg_out, 1.0))
            norm_dst = jax.lax.rsqrt(jnp.clip(deg_in, 1.0))
            m = (h0 * norm_src[:, None])[s]
            agg = jax.ops.segment_sum(m, d, num_segments=n)
            h1 = agg * norm_dst[:, None] @ Wg + bg
            h1 = jax.nn.relu(h1)
            return h0 + h1
        return _gcn_forward(node_features, W1, b1, W2, b2, Wg, bg, edge_src, edge_dst)

    def _L1_gnn_ref(x, pseudo, weight, root_w, root_b, edge_index):
        import jax, jax.numpy as jnp
        import numpy as np
        N_NODES = 12500
        N_EDGES = 400000
        IN_CH = 32
        OUT_CH = 32
        DIM = 2
        KSIZE = 3

        def _basis(pseudo):
            p = jnp.clip(pseudo, 0.0, 1.0)
            grid = jnp.linspace(0.0, 1.0, KSIZE, dtype=p.dtype)
            dist = jnp.abs(p[:, :, None] - grid[None, None, :])
            b = jnp.maximum(1.0 - dist * (KSIZE - 1), 0.0)
            basis = jnp.einsum('ea,eb->eab', b[:, 0], b[:, 1])
            return basis.reshape(p.shape[0], -1)
        row, col = (edge_index[0], edge_index[1])
        basis = _basis(pseudo)
        messages = jnp.einsum('ek,ei,kio->eo', basis, x[row], weight)
        out = jnp.zeros((x.shape[0], weight.shape[2]), dtype=x.dtype).at[col].add(messages)
        degree = jnp.zeros((x.shape[0],), dtype=x.dtype).at[col].add(jnp.ones_like(col, dtype=x.dtype))
        out = out / jnp.maximum(degree, 1.0)[:, None]
        out = out + x @ root_w.T + root_b
        return out

    def _L2_gnn_ref(feat, src, dst, w1_W, w1_b, w2_W, w2_b, a):
        import jax, jax.numpy as jnp
        import numpy as np
        N_NODES = 12500
        N_EDGES = 200000
        IN_FEAT = 32
        OUT_FEAT = 32

        def _gna_forward(feat, src, dst, w1_W, w1_b, w2_W, w2_b, a):
            n = feat.shape[0]
            h_src = feat[src]
            h_dst = feat[dst]
            dt = h_dst - h_src
            a_vec = a[0]
            aij = dt @ (w2_W.T @ a_vec) + jnp.dot(a_vec, w2_b)
            ss = h_src @ w2_W.T + w2_b
            m = jax.ops.segment_max(aij, dst, num_segments=n)
            aexp = jnp.exp(aij - m[dst])
            denom = jax.ops.segment_sum(aexp, dst, num_segments=n)
            alpha = aexp / denom[dst]
            res = jax.ops.segment_sum(alpha[:, None] * ss, dst, num_segments=n)
            out = res + feat @ w1_W.T + w1_b
            return out
        return _gna_forward(feat, src, dst, w1_W, w1_b, w2_W, w2_b, a)

    def _L3_gnn_ref(x, edge_index, edge_attr, W1, b1, W2, b2):
        import jax, jax.numpy as jnp
        import numpy as np
        N_NODES = 6250
        N_EDGES = 100000
        X_DIM = 32
        E_DIM = 32
        HID = 64
        OUT = 32
        num_nodes = x.shape[0]
        rol, col = (edge_index[0], edge_index[1])
        e_feat = jnp.concatenate([x[rol], x[col], edge_attr], axis=-1)
        h = jax.nn.relu(e_feat @ W1 + b1)
        v = h @ W2 + b2
        x_cand = jax.ops.segment_max(v, col, num_segments=num_nodes)
        return jnp.maximum(x_cand, x[:, -v.shape[-1]:])
    edge_index = jnp.stack([src, dst])
    x = _layernorm(x + _L0_gnn_ref(x, L0_gnn_W1, L0_gnn_b1, L0_gnn_W2, L0_gnn_b2, L0_gnn_Wg, L0_gnn_bg, src, dst, edge_type_4), axis=-1)
    x = _layernorm(x + _L1_gnn_ref(x, edge_attr_2, L1_gnn_weight, L1_gnn_root_w, L1_gnn_root_b, edge_index), axis=-1)
    x = _layernorm(x + _L2_gnn_ref(x, src, dst, L2_gnn_w1_W, L2_gnn_w1_b, L2_gnn_w2_W, L2_gnn_w2_b, L2_gnn_a), axis=-1)
    x = _layernorm(x + _L3_gnn_ref(x, edge_index, edge_attr_32, L3_gnn_W1, L3_gnn_b1, L3_gnn_W2, L3_gnn_b2), axis=-1)
    return x

_drawn_inputs = setup_inputs


def setup_inputs(seed=0):
    import zlib

    import numpy as np

    out = dict(_drawn_inputs(seed))
    spreads = {'L0_gnn_bg': (0.0, 0.1), 'L3_gnn_b1': (0.0, 0.1), 'L3_gnn_b2': (0.0, 0.1)}
    factors = {'L1_gnn_root_b': 8.0}
    for name, (base, spread) in spreads.items():
        noise = np.random.default_rng([zlib.crc32(name.encode()), seed]).standard_normal(out[name].shape)
        drawn = base * np.exp(spread * noise) if base else spread * noise
        out[name] = jnp.asarray(drawn.astype(out[name].dtype))
    for name, factor in factors.items():
        out[name] = (out[name] * factor).astype(out[name].dtype)
    return out
```

```python
from contextlib import ExitStack

import concourse.bass as bass
from concourse import mybir

F32 = mybir.dt.float32
I32 = mybir.dt.int32
BF16 = mybir.dt.bfloat16
ALU = mybir.AluOpType
ACT = mybir.ActivationFunctionType
AX = mybir.AxisListType

N, E, D, H = 12500, 400000, 32, 64
P = 128
EPP = E // P
NP, NJ = 125, 100
T = 25
SLOTS = 5
LOOPS = EPP // (T * SLOTS)
T1 = 5
LOOPS1 = EPP // (T1 * SLOTS)
K1 = 9
GJ = 4
UNROLL = 5
NLOOPS = NJ // (GJ * UNROLL)
BIG = 1e38
MAGIC = 12582912.0
EPS = 1e-5


def repeat(eng, count):
    def build(body):
        body(0)
        with eng.Fori(1, count) as i:
            body(i)
    return build


def wait(eng, sem, value):
    if not isinstance(value, int) or value > 0:
        eng.wait_ge(sem, value)


class Chain:

    def __init__(self, eng, sem):
        self.eng, self.sem, self.n, self.base = eng, sem, 0, None

    def __call__(self, ins):
        ins.then_inc(self.sem, 1)
        self.n += 1
        self.eng.wait_ge(self.sem, self.n if self.base is None else self.base + self.n)

    def loop(self, i, per_iteration):
        if self.base is None:
            self.start = self.n
        self.n, self.per = 0, per_iteration
        self.base = i * per_iteration + self.start

    def end_loop(self, iterations):
        assert self.n == self.per, (self.n, self.per)
        self.n, self.base = self.start + iterations * self.per, None


class Pools:

    live = []

    def __init__(self, nc, stack, tag):
        self.nc, self.stack, self.tag = nc, stack, tag

    def sb(self, name, shape, dt=F32):
        return self.stack.enter_context(self.nc.sbuf_tensor(f"{self.tag}_{name}", shape, dt))

    def ps(self, name, shape):
        return self.stack.enter_context(self.nc.psum_tensor(f"{self.tag}_{name}", shape, F32))

    def sem(self, name):
        self.live.append(self.nc.alloc_semaphore(name=f"{self.tag}_{name}"))
        return self.live[-1]

    def sems(self, name, n=SLOTS):
        return [self.sem(f"{name}{k}") for k in range(n)]


def clear_semaphores(nc):
    nc.clear_and_free_semaphores(Pools.live)
    nc.all_engine_barrier()
    Pools.live.clear()


def by_partition(ap, parts=P):
    return ap.rearrange("(p t) f -> p t f", p=parts)


def spread(ap, shape):
    return ap.to_broadcast(shape)




def stage_indices(act, src, idx, idx_ready, gathered, tiles, loops):
    @repeat(act, loops)
    def _(i):
        for b in range(SLOTS):
            wait(act, gathered[b], i * (16 * tiles))
            act.activation(idx[:, b, :], src[:, bass.ds(i * (SLOTS * tiles) + b * tiles, tiles)],
                           ACT.Copy).then_inc(idx_ready[b], 1)


def stage_ahead(act, g, idx, idx_ready, tiles, i, b):
    act.activation(idx[:, b, :], g.src[:, bass.ds(i * (SLOTS * tiles) + b * tiles, tiles)],
                   ACT.Copy).then_inc(idx_ready[b], 1)


def gather_rows(pool, table, rows, idx, idx_ready, slot_free, gathered, tiles, loops):
    @repeat(pool, loops)
    def _(i):
        for b in range(SLOTS):
            wait(pool, idx_ready[b], i + 1)
            pool.nop(nofuse=True)
            wait(pool, slot_free[b], i)
            pool.nop(nofuse=True)
            for t in range(tiles):
                pool.indirect_dma_start(
                    rows[:, b, t, :], None, table, bass.IndirectOffsetOnAxis(ap=idx[:, b, t:t + 1], axis=0)
                ).then_inc(gathered[b], 16)


def store_running(sp, running, run_rows, scanned, stored, loops):
    @repeat(sp, loops)
    def _(i):
        for b in range(SLOTS):
            wait(sp, scanned[b], i + 1)
            sp.dma_start(run_rows[:, bass.ds(i * (SLOTS * T) + b * T, T), :], running[:, b]).then_inc(stored[b], 16)


def finish_stores(sp, stored, loops):
    for b in range(SLOTS):
        sp.wait_ge(stored[b], 16 * loops)


def layer_norm(dve, act, chain, x, tmp, stat, sem_var, sem_std):
    wide = [NP, NJ, D]
    chain(dve.tensor_reduce(stat[:, 0, :], x[:, :, :], AX.X, ALU.add))
    chain(dve.tensor_scalar(stat[:, 0, :], stat[:, 0, :], 1.0 / D, None, ALU.mult))
    chain(dve.tensor_tensor(x[:, :, :], x[:, :, :], spread(stat[:, 0, :, None], wide), ALU.subtract))
    chain(dve.tensor_tensor(tmp[:, :, :], x[:, :, :], x[:, :, :], ALU.mult))
    chain(dve.tensor_reduce(stat[:, 1, :], tmp[:, :, :], AX.X, ALU.add))
    dve.tensor_scalar(stat[:, 1, :], stat[:, 1, :], 1.0 / D, EPS, ALU.mult, ALU.add).then_inc(sem_var, 1)
    dve.wait_ge(sem_std, 1)
    chain(dve.reciprocal(stat[:, 1, :], stat[:, 1, :]))
    chain(dve.tensor_tensor(x[:, :, :], x[:, :, :], spread(stat[:, 1, :, None], wide), ALU.mult))


def norm_root(act, stat, sem_var, sem_std):
    act.wait_ge(sem_var, 1)
    act.activation(stat[:, 1, :], stat[:, 1, :], ACT.Sqrt).then_inc(sem_std, 1)


def node_linear(nc, tag, ident, terms, width, sink, table=None):
    with ExitStack() as stack:
        m = Pools(nc, stack, tag)
        nt = len(terms)
        bank = 512
        stage = m.sb("stage", [NP, 2, nt, GJ * D])
        turned = m.sb("turned", [P, 2, nt, NP])
        turn_ps = m.ps("turn_ps", [P, 2, bank])
        out_w = bank if width > 128 else width
        nslot = 1 if width > 128 else 2
        out_all = m.ps("out_ps", [NP, nslot, GJ * out_w if width > 128 else bank])
        out_ps = out_all[:, :, 0:GJ * out_w].rearrange("p s (q w) -> p s q w", q=GJ)
        staged, turned_ps, turned_sb = m.sem("staged"), m.sem("turned_ps"), m.sem("turned_sb")
        product, taken, sent = m.sem("product"), m.sem("taken"), m.sems("sent", 2)
        chain_sem = m.sem("chain")
        row_stage = m.sb("row_stage", [NP, 2, GJ, table[1]]) if table else None
        sends = {0: 3, 1: 2}

        with nc.Block() as block:
            @block.scalar
            def _(act):
                @repeat(act, NLOOPS)
                def _(i):
                    def put(b):
                        if b >= 2:
                            wait(act, turned_ps, i * UNROLL + b - 1)
                        else:
                            wait(act, turned_ps, i * UNROLL)
                        for k, (rows, _) in enumerate(terms):
                            last = act.activation(
                                stage[:, b % 2, k, :].rearrange("p (j f) -> p j f", f=D),
                                rows[:, bass.ds(i * (GJ * UNROLL) + b * GJ, GJ), :], ACT.Copy)
                        last.then_inc(staged, 1)

                    put(0)
                    for b in range(UNROLL):
                        if b + 1 < UNROLL:
                            put(b + 1)
                        wait(act, turned_ps, i * UNROLL + b + 1)
                        wait(act, product, i * UNROLL + max(b - 1, 0))
                        act.activation(
                            turned[:, b % 2, :, :],
                            turn_ps[:, b % 2, 0:nt * NP].rearrange("p (k n) -> p k n", n=NP),
                            ACT.Copy).then_inc(turned_sb, 1)

            @block.tensor
            def _(pe):
                @repeat(pe, NLOOPS)
                def _(i):
                    def turn(b):
                        wait(pe, staged, i * UNROLL + b + 1)
                        wait(pe, turned_sb, i * UNROLL + max(b - 1, 0))
                        for k in range(nt):
                            last = pe.transpose(turn_ps[:, b % 2, k * NP:(k + 1) * NP], stage[:, b % 2, k, :],
                                                ident[0:NP, 0:NP])
                        last.then_inc(turned_ps, 1)

                    turn(0)
                    for b in range(UNROLL):
                        if b + 1 < UNROLL:
                            turn(b + 1)
                        wait(pe, turned_sb, i * UNROLL + b + 1)
                        wait(pe, taken, i * UNROLL + (b if nslot == 1 else max(b - 1, 0)))
                        per = 1 if width > 128 else GJ
                        for q in range(0, GJ, per):
                            for k, (_, w) in enumerate(terms):
                                last = pe.matmul(out_ps[:, b % nslot, q:q + per, 0:width], turned[:, b % 2, k, :],
                                                 w[:, q:q + per, :], start=(k == 0), stop=(k == nt - 1))
                        last.then_inc(product, 1)

            @block.vector
            def _(dve):
                @repeat(dve, NLOOPS)
                def _(i):
                    for b in range(UNROLL):
                        wait(dve, product, i * UNROLL + b + 1)
                        if table:
                            n = len([c for c in range(b) if c % 2 == b % 2])
                            wait(dve, sent[b % 2], (i * sends[b % 2] + n) * 16)
                        sink(dve, out_ps[:, b % nslot, :, 0:width], i * (GJ * UNROLL) + b * GJ,
                             row_stage[:, b % 2] if table else None).then_inc(taken, 1)

            if table:
                @block.sync
                def _(sp):
                    rows = by_partition(table[0], NP)
                    @repeat(sp, NLOOPS)
                    def _(i):
                        for b in range(UNROLL):
                            wait(sp, taken, i * UNROLL + b + 1)
                            sp.dma_start(rows[:, bass.ds(i * (GJ * UNROLL) + b * GJ, GJ), :],
                                         row_stage[:, b % 2]).then_inc(sent[b % 2], 16)
                    for s in range(2):
                        sp.wait_ge(sent[s], 16 * NLOOPS * sends[s])


def carry(nc, g, kind, run_dram, tail, node_rows):
    w = {"sum": D, "max": D, "softmax": D + 2}[kind]
    r = {"sum": D, "max": D, "softmax": D + 1}[kind]
    with ExitStack() as stack:
        m = Pools(nc, stack, f"carry{g.phase}")
        g.phase += 1
        ps = m.ps("ps", [P, 4, 512])
        tail_t, state = m.sb("tail_t", [r, P]), m.sb("state", [r, P + 1])
        head = m.sb("head", [P, w])
        tail_max, max_t = m.sb("tail_max", [P, r]), m.sb("max_t", [r, P])
        max_state, drift = m.sb("max_state", [r, P + 1]), m.sb("drift", [r, 2, P])
        new_max, fade = m.sb("new_max", [P, 1]), m.sb("fade", [P, 2])
        turned, scanned, back, exp_in, exp_out = (
            m.sem(x) for x in ("turned", "scanned", "back", "exp_in", "exp_out"))
        prepared, head_in, head_ok, head_out, fetched, link = (
            m.sem(x) for x in ("prepared", "head_in", "head_ok", "head_out", "fetched", "link"))
        soft = kind == "softmax"

        with nc.Block() as block:
            @block.tensor
            def _(pe):
                if soft:
                    pe.wait_ge(prepared, 1)
                    pe.transpose(ps[0:r, 1, 0:P], tail_max[:, :], g.ident[:, :])
                pe.transpose(ps[0:r, 0, 0:P], tail[:, 0:r], g.ident[:, :]).then_inc(turned, 1)
                pe.wait_ge(scanned, 1)
                if soft:
                    pe.transpose(ps[:, 3, 0:r], max_state[:, 0:P], g.ident[0:r, 0:r])
                pe.transpose(ps[:, 2, 0:r], state[:, 0:P], g.ident[0:r, 0:r]).then_inc(back, 1)

            @block.scalar
            def _(act):
                if soft:
                    act.wait_ge(exp_in, 1)
                    act.activation(drift[:, :, :], drift[:, :, :], ACT.Exp).then_inc(exp_out, 1)
                    act.wait_ge(exp_in, 2)
                    act.activation(fade[:, :], fade[:, :], ACT.Exp).then_inc(exp_out, 1)

            @block.vector
            def _(dve):
                chain = Chain(dve, link)
                chain(dve.memset(state[:, 0:1], -BIG if kind == "max" else 0.0))
                if soft:
                    chain(dve.memset(max_state[:, 0:1], -BIG))
                    dve.tensor_copy(tail_max[:, :], spread(tail[:, D + 1:D + 2], [P, r])).then_inc(prepared, 1)
                dve.wait_ge(turned, 1)
                chain(dve.tensor_copy(tail_t[:, :], ps[0:r, 0, 0:P]))
                if kind == "sum":
                    dve.tensor_tensor_scan(state[:, 1:P + 1], g.keep_row[0:r, :], tail_t[:, :], 0.0,
                                           ALU.mult, ALU.add).then_inc(scanned, 1)
                elif kind == "max":
                    dve.tensor_tensor_scan(state[:, 1:P + 1], g.pen_row[0:r, :], tail_t[:, :], -BIG,
                                           ALU.add, ALU.max).then_inc(scanned, 1)
                else:
                    chain(dve.tensor_copy(max_t[:, :], ps[0:r, 1, 0:P]))
                    chain(dve.tensor_tensor_scan(max_state[:, 1:P + 1], g.pen_row[0:r, :], max_t[:, :], -BIG,
                                                 ALU.add, ALU.max))
                    chain(dve.tensor_tensor(drift[:, 0, :], max_state[:, 0:P], g.pen_row[0:r, :], ALU.add))
                    chain(dve.tensor_tensor(drift[:, 0, :], drift[:, 0, :], max_state[:, 1:P + 1], ALU.subtract))
                    dve.tensor_tensor(drift[:, 1, :], max_t[:, :], max_state[:, 1:P + 1],
                                      ALU.subtract).then_inc(exp_in, 1)
                    dve.wait_ge(exp_out, 1)
                    chain(dve.tensor_tensor(tail_t[:, :], tail_t[:, :], drift[:, 1, :], ALU.mult))
                    dve.tensor_tensor_scan(state[:, 1:P + 1], drift[:, 0, :], tail_t[:, :], 0.0,
                                           ALU.mult, ALU.add).then_inc(scanned, 1)
                dve.wait_ge(back, 1)
                dve.wait_ge(head_in, 16)
                if kind == "sum":
                    dve.tensor_tensor(head[:, :], head[:, :], ps[:, 2, 0:r], ALU.add).then_inc(head_ok, 1)
                elif kind == "max":
                    dve.tensor_tensor(head[:, :], head[:, :], ps[:, 2, 0:r], ALU.max).then_inc(head_ok, 1)
                else:
                    chain(dve.tensor_tensor(new_max[:, :], head[:, D + 1:D + 2], ps[:, 3, 0:1], ALU.max))
                    chain(dve.tensor_tensor(fade[:, 0:1], head[:, D + 1:D + 2], new_max[:, :], ALU.subtract))
                    dve.tensor_tensor(fade[:, 1:2], ps[:, 3, 0:1], new_max[:, :], ALU.subtract).then_inc(exp_in, 1)
                    dve.wait_ge(exp_out, 2)
                    chain(dve.tensor_scalar(head[:, 0:r], head[:, 0:r], fade[:, 0:1], None, ALU.mult))
                    chain(dve.tensor_copy(head[:, D + 1:D + 2], new_max[:, :]))
                    dve.scalar_tensor_tensor(head[:, 0:r], ps[:, 2, 0:r], fade[:, 1:2], head[:, 0:r],
                                             ALU.mult, ALU.add).then_inc(head_ok, 1)

            @block.gpsimd
            def _(pool):
                rows = run_dram[0:E + P, 0:w]
                pool.indirect_dma_start(head[:, :], None, rows, bass.IndirectOffsetOnAxis(
                    ap=g.head_idx[:, 0:1], axis=0)).then_inc(head_in, 16)
                pool.wait_ge(head_ok, 1)
                pool.indirect_dma_start(rows, bass.IndirectOffsetOnAxis(ap=g.head_idx[:, 0:1], axis=0),
                                        head[:, :], None).then_inc(head_out, 16)
                pool.wait_ge(head_out, 16)
                for j in range(NJ):
                    pool.indirect_dma_start(node_rows[:, j, :], None, rows, bass.IndirectOffsetOnAxis(
                        ap=g.end_idx[:, j:j + 1], axis=0)).then_inc(fetched, 16)
                pool.wait_ge(fetched, 16 * NJ)




def digits(dve, chain, ids, high, low, scratch):
    chain(dve.tensor_scalar(scratch[:, :], ids, 0.5, 1.0 / NJ, ALU.add, ALU.mult))
    chain(dve.tensor_scalar(scratch[:, :], scratch[:, :], -0.5, None, ALU.add))
    chain(dve.tensor_scalar(scratch[:, :], scratch[:, :], MAGIC, None, ALU.add))
    chain(dve.tensor_scalar(scratch[:, :], scratch[:, :], -MAGIC, None, ALU.add))
    chain(dve.tensor_copy(high[:, :], scratch[:, :]))
    chain(dve.scalar_tensor_tensor(low[:, :], scratch[:, :], -float(NJ), ids, ALU.mult, ALU.add))


def mark(dve, hot, b, steps, high, low, at):
    dve.tensor_tensor(hot[:, b, 0:NP, :], steps[:, :, :],
                      spread(high[:, None, bass.ds(at, T)], [P, NP, T]), ALU.is_equal)
    return dve.tensor_tensor(hot[:, b, NP:NP + NJ, :], steps[:, 0:NJ, :],
                             spread(low[:, None, bass.ds(at, T)], [P, NJ, T]), ALU.is_equal)


def count(pe, counts, hot, b):
    for t in range(T):
        last = pe.matmul(counts, hot[:, b, 0:NP, t], hot[:, b, NP:NP + NJ, t], start=False, stop=False,
                         skip_group_check=True)
    return last




def prepare(nc, g, a):
    with ExitStack() as stack:
        m = Pools(nc, stack, "prep")
        dst_i, dst_f, scratch, next_i = g.dst_i, g.dst_f, g.scratch, g.next_i
        hot = m.sb("hot", [P, 2, NP + NJ, T], BF16)
        nothing = m.sb("nothing", [P, NP], BF16)
        step_i, step_f = m.sb("step_i", [P, NP], I32), m.sb("step_f", [P, NP])
        w1, w2b, b1 = m.sb("w1", [P, GJ, H]), m.sb("w2b", [H + 1, D]), m.sb("b1", [H, 1])
        avec, w2l2 = m.sb("avec", [D, 1]), m.sb("w2l2", [D, D])
        acol = m.sb("acol", [D, P])
        stage, turned, hid = m.sb("stage", [NP, GJ * D]), m.sb("turned", [P, NP]), m.sb("hid", [H + 1, GJ * NP])
        counts = m.ps("counts", [NP, 512])
        turn_ps, hid_ps, h0_ps, small_ps = (m.ps(n, [P, 512]) for n in ("turn_ps", "hid_ps", "h0_ps", "small_ps"))
        names = ("src_in dst_in border x_in w_in filled link consts hid_one nothing_ok staged turned_ps "
                 "turned_sb hid_ready hid_sb h0_ready h0_out counted trash_ok rows_ok rows_ps ab_ok ab_ps root root_in "
                 "zero_out edges score_sb weights_zero").split()
        s = {n: m.sem(n) for n in names}
        marked, used = m.sems("marked", 2), m.sems("used", 2)

        with nc.Block() as block:
            @block.sync
            def _(sp):
                sp.dma_start(g.src[:, 0:EPP], a["src"].rearrange("(p t) -> p t", p=P)).then_inc(s["src_in"], 16)
                sp.dma_start(dst_i[:, 1:EPP + 1], a["dst"].rearrange("(p t) -> p t", p=P)).then_inc(s["dst_in"], 16)
                sp.wait_ge(s["filled"], 1)
                col = a["dst"].rearrange("(p t) -> p t", p=P)
                sp.dma_start(dst_i[1:P, 0:1], col[0:P - 1, EPP - 1:EPP],
                             allow_slow_non_contiguous=True).then_inc(s["border"], 16)
                sp.dma_start(next_i[0:P - 1, :], col[1:P, 0:1],
                             allow_slow_non_contiguous=True).then_inc(s["border"], 16)
                sp.dma_start(g.x[:, :, :], by_partition(a["x"], NP)).then_inc(s["x_in"], 16)
                sp.wait_ge(s["nothing_ok"], 1)
                sp.dma_start(g.run[E:E + P, 0:D + 2], g.zeros[:, 0:D + 2]).then_inc(s["zero_out"], 16)
                sp.wait_ge(s["zero_out"], 16)
                sp.wait_ge(s["dst_in"], 16)
                sp.wait_ge(s["border"], 32)

            @block.scalar
            def _(act):
                n = 0
                act.wait_ge(s["weights_zero"], 1)
                for q in range(GJ):
                    rows = slice(D * q, D * q + D)
                    for dst_w, src_w in ((w1[rows, q, :], a["L0_gnn_W1"]), (g.wg[rows, q, :], a["L0_gnn_Wg"]),
                                         (g.w_p[rows, q, :], a["L3_gnn_W1"][0:D, :]),
                                         (g.w_d[rows, q, :], a["L3_gnn_W1"][D:2 * D, :]),
                                         (g.w_e[rows, q, :], a["L3_gnn_W1"][2 * D:3 * D, :]),
                                         (g.w_y[rows, q, 0:K1 * D].rearrange("i (k o) -> i k o", k=K1),
                                          a["L1_gnn_weight"].rearrange("k i o -> i k o")),
                                         (g.w_y[rows, q, K1 * D:K1 * D + D], a["L1_gnn_root_w"].rearrange("o i -> i o")),
                                         (g.w_s[rows, q, :], a["L2_gnn_w1_W"].rearrange("o i -> i o")),
                                         (g.w_a[rows, q, :], a["L2_gnn_w2_W"].rearrange("o i -> i o"))):
                        act.dma_start(dst_w, src_w, allow_slow_non_contiguous=True).then_inc(s["w_in"], 16)
                        n += 1
                for q in range(2):
                    act.dma_start(g.w_v[H * q:H * q + H, q, :], a["L3_gnn_W2"]).then_inc(s["w_in"], 16)
                    n += 1
                for dst_w, src_w in ((w2b[0:H, :], a["L0_gnn_W2"]), (w2b[H:H + 1, :], a["L0_gnn_b2"][None, :]),
                                     (b1[:, :], a["L0_gnn_b1"][:, None]), (avec[:, :], a["L2_gnn_a"].rearrange("z i -> i z")),
                                     (w2l2[:, :], a["L2_gnn_w2_W"])):
                    act.dma_start(dst_w, src_w, allow_slow_non_contiguous=True).then_inc(s["w_in"], 16)
                    n += 1
                for k, (v, width) in enumerate(((a["L0_gnn_bg"], D), (a["L1_gnn_root_b"], D), (a["L2_gnn_w1_b"], D),
                                                (a["L2_gnn_w2_b"], D), (a["L3_gnn_b2"], D), (a["L3_gnn_b1"], H))):
                    act.dma_start(g.bias[:, k, 0:width], v[None, :].to_broadcast([P, width])).then_inc(s["w_in"], 16)
                    n += 1
                act.wait_ge(s["w_in"], 16 * n)
                act.wait_ge(s["x_in"], 16)
                act.wait_ge(s["hid_one"], 1)
                @repeat(act, NJ // GJ)
                def _(i):
                    wait(act, s["turned_ps"], i)
                    act.activation(stage[:, :].rearrange("p (j f) -> p j f", f=D),
                                   g.x[:, bass.ds(i * GJ, GJ), :], ACT.Copy).then_inc(s["staged"], 1)
                    wait(act, s["turned_ps"], i + 1)
                    act.activation(turned[:, :], turn_ps[:, 0:NP], ACT.Copy).then_inc(s["turned_sb"], 1)
                    wait(act, s["hid_ready"], i + 1)
                    act.activation(hid[0:H, :], hid_ps[0:H, 0:GJ * NP], ACT.Relu, bias=b1[:, 0:1]).then_inc(s["hid_sb"], 1)
                    wait(act, s["h0_ready"], i + 1)
                    act.activation(g.h0[:, bass.ds(i * GJ, GJ), :],
                                   h0_ps[0:NP, 0:GJ * D].rearrange("p (j f) -> p j f", f=D),
                                   ACT.Relu).then_inc(s["h0_out"], 1)
                act.wait_ge(s["root_in"], 1)
                act.activation(g.norm_src[:, :], g.norm_src[:, :], ACT.Sqrt).then_inc(s["root"], 1)

            @block.gpsimd
            def _(pool):
                pool.memset(g.ident[:, :], 0.0).then_inc(s["edges"], 1)
                pool.iota(step_i[:, :], [[1, NP]], base=0, channel_multiplier=0).then_inc(s["consts"], 1)
                pool.iota(g.spare_row[:, :], [[1, 1]], base=E, channel_multiplier=1).then_inc(s["trash_ok"], 1)
                pool.iota(g.iota_e[:, :], [[0, 1]], base=0, channel_multiplier=EPP).then_inc(s["trash_ok"], 1)
                pool.iota(g.node_id[:, :], [[1, NJ]], base=0, channel_multiplier=NJ).then_inc(s["trash_ok"], 1)
                pool.wait_ge(s["trash_ok"], 3)
                pool.wait_ge(s["edges"], 1)
                pool.affine_select(out=g.ident[:, :], in_=g.ident[:, :], compare_op=ALU.not_equal, fill=1.0,
                                   base=0, pattern=[[-1, P]], channel_multiplier=1).then_inc(s["consts"], 1)

            @block.tensor
            def _(pe):
                pe.wait_ge(s["nothing_ok"], 1)
                pe.matmul(counts[:, 0:NJ], nothing[:, 0:NP], nothing[:, 0:NJ], start=True, stop=False,
                          skip_group_check=True)
                pe.wait_ge(s["consts"], 2)
                pe.wait_ge(s["w_in"], 16 * (4 * 9 + 2 + 5 + 6))
                pe.wait_ge(s["hid_one"], 1)
                @repeat(pe, NJ // GJ)
                def _(i):
                    for b in range(SLOTS):
                        k = b % 2
                        n = b // 2
                        wait(pe, marked[k], i * (3 - k) + n + 1)
                        count(pe, counts[:, 0:NJ], hot, k).then_inc(used[k], 1)
                        if b == 0:
                            wait(pe, s["staged"], i + 1)
                            pe.transpose(turn_ps[:, 0:NP], stage[:, :], g.ident[0:NP, 0:NP]).then_inc(s["turned_ps"], 1)
                        if b == 1:
                            wait(pe, s["turned_sb"], i + 1)
                            for q in range(GJ):
                                last = pe.matmul(hid_ps[0:H, q * NP:q * NP + NP], w1[:, q, :],
                                                 turned[:, :], start=True, stop=True)
                            last.then_inc(s["hid_ready"], 1)
                        if b == 3:
                            wait(pe, s["hid_sb"], i + 1)
                            for q in range(GJ):
                                last = pe.matmul(h0_ps[0:NP, q * D:q * D + D], hid[:, q * NP:q * NP + NP],
                                                 w2b[:, :], start=True, stop=True)
                            last.then_inc(s["h0_ready"], 1)
                pe.matmul(counts[:, 0:NJ], nothing[:, 0:NP], nothing[:, 0:NJ], start=False, stop=True,
                          skip_group_check=True).then_inc(s["counted"], 1)
                pe.wait_ge(s["ab_ok"], 1)
                pe.matmul(small_ps[:, 0:D], acol[:, :], w2l2[:, :], start=True, stop=True).then_inc(s["ab_ps"], 1)

            @block.vector
            def _(dve):
                chain = Chain(dve, s["link"])
                for w in (w1, g.wg, g.w_p, g.w_d, g.w_e, g.w_s, g.w_a, g.w_v):
                    dve.memset(w[:, :, :], 0.0)
                dve.memset(g.w_y[:, :, :], 0.0).then_inc(s["weights_zero"], 1)
                chain(dve.memset(dst_i[:, 0:1], -1))
                dve.memset(next_i[:, :], -1).then_inc(s["filled"], 1)
                chain(dve.memset(g.src[:, EPP:EPP + SLOTS * T], 0))
                chain(dve.memset(nothing[:, :], 0.0))
                dve.memset(g.zeros[:, :], 0.0).then_inc(s["nothing_ok"], 1)
                dve.memset(hid[H:H + 1, :], 1.0).then_inc(s["hid_one"], 1)
                dve.wait_ge(s["consts"], 2)
                chain(dve.tensor_copy(step_f[:, :], step_i[:, :]))
                chain(dve.tensor_copy(g.steps[:, :, :], spread(step_f[:, :, None], [P, NP, T])))
                dve.wait_ge(s["src_in"], 16)
                chain(dve.tensor_copy(dst_f[:, 0:EPP], g.src[:, 0:EPP]))
                digits(dve, chain, dst_f[:, 0:EPP], g.high, g.low, scratch)
                @repeat(dve, EPP // (T * SLOTS))
                def _(i):
                    for b in range(SLOTS):
                        k, n = b % 2, b // 2
                        wait(dve, used[k], i * (3 - k) + n if n else i * (3 - k))
                        mark(dve, hot, k, g.steps, g.high, g.low, i * (SLOTS * T) + b * T).then_inc(marked[k], 1)
                dve.wait_ge(s["w_in"], 16 * (4 * 9 + 2 + 5 + 6))
                dve.tensor_copy(acol[:, :], spread(avec[:, :], [D, P])).then_inc(s["ab_ok"], 1)
                dve.wait_ge(s["ab_ps"], 1)
                dve.tensor_copy(g.score_w[:, :], small_ps[:, 0:D]).then_inc(s["score_sb"], 1)
                dve.wait_ge(s["counted"], 1)
                dve.tensor_scalar(g.norm_src[:, :], counts[:, 0:NJ], 1.0, None, ALU.add).then_inc(s["root_in"], 1)
                dve.wait_ge(s["root"], 1)
                chain(dve.reciprocal(g.norm_src[:, :], g.norm_src[:, :]))
                dve.wait_ge(s["h0_out"], NJ // GJ)
                chain(dve.tensor_tensor(g.m0[:, :, :], g.h0[:, :, :], spread(g.norm_src[:, :, None], [NP, NJ, D]), ALU.mult))


def write_rows(nc, tag, pairs):
    with ExitStack() as stack:
        m = Pools(nc, stack, tag)
        sent = m.sem("sent")
        with nc.Block() as block:
            @block.sync
            def _(sp):
                for dram, rows in pairs:
                    sp.dma_start(by_partition(dram, NP), rows).then_inc(sent, 16)
                sp.wait_ge(sent, 16 * len(pairs))


def gcn_edges(nc, g):
    with ExitStack() as stack:
        m = Pools(nc, stack, "gcn")
        idx = m.sb("idx", [P, SLOTS, T], I32)
        rows, running = m.sb("rows", [P, SLOTS, T, D]), m.sb("running", [P, SLOTS, T, D])
        hot, nothing = m.sb("hot", [P, 2, NP + NJ, T], BF16), m.sb("nothing", [P, NP], BF16)
        zero_slot = m.sb("zero_slot", [P, T * D])
        idx_ready, gathered, scanned, stored = (m.sems(n) for n in ("idx_ready", "gathered", "scanned", "stored"))
        marked, used = m.sems("marked", 2), m.sems("used", 2)
        prepared, counted, zeroed, link, ends_in = (m.sem(n) for n in ("prepared", "counted", "zeroed", "link", "ends_in"))
        tot, tot_ps = m.sb("tot", [NP, 1]), m.ps("tot_ps", [NP, 512])
        below, cum = m.sb("below", [NP, NP]), m.sb("cum", [NP, NJ])
        below_ok, tot_ok, based = m.sem("below_ok"), m.sem("tot_ok"), m.sem("based")
        counts = m.ps("counts", [NP, 512])
        work = m.sb("work", [NP, NJ])
        next_f, edge, rows33 = m.sb("next_f", [P, 1]), m.sb("edge", [P, 8]), m.sb("rows33", [P, 2, D + 2])
        row_ps, rows_ok, rows_ps = m.ps("row_ps", [P, 512]), m.sem("rows_ok"), m.sem("rows_ps_ok")

        with nc.Block() as block:
            @block.scalar
            def _(act):
                stage_indices(act, g.src, idx, idx_ready, gathered, T, LOOPS)

            @block.gpsimd
            def _(pool):
                pool.memset(below[:, :], 1.0).then_inc(below_ok, 1)
                pool.wait_ge(below_ok, 1)
                pool.affine_select(out=below[:, :], in_=below[:, :], compare_op=ALU.is_gt, fill=0.0,
                                   base=0, pattern=[[1, NP]], channel_multiplier=-1).then_inc(below_ok, 1)
                gather_rows(pool, g.table[:, 0:D], rows, idx, idx_ready, scanned, gathered, T, LOOPS)

            @block.sync
            def _(sp):
                sp.wait_ge(prepared, 1)
                fill = g.fill_rows[0:E, :].rearrange("(p t) f -> p (t f)", p=P)
                run_rows = by_partition(g.run[0:E, 0:D])
                @repeat(sp, LOOPS)
                def _(i):
                    for b in range(SLOTS):
                        sp.dma_start(fill[:, bass.ds(i * (SLOTS * T * D) + b * T * D, T * D)],
                                     zero_slot[:, :]).then_inc(zeroed, 16)
                        wait(sp, scanned[b], i + 1)
                        sp.dma_start(run_rows[:, bass.ds(i * (SLOTS * T) + b * T, T), :],
                                     running[:, b]).then_inc(stored[b], 16)
                finish_stores(sp, stored, LOOPS)
                sp.wait_ge(zeroed, 16 * LOOPS * SLOTS)

            @block.tensor
            def _(pe):
                pe.wait_ge(prepared, 1)
                pe.matmul(counts[:, 0:NJ], nothing[:, 0:NP], nothing[:, 0:NJ], start=True, stop=False,
                          skip_group_check=True)
                @repeat(pe, LOOPS)
                def _(i):
                    for b in range(SLOTS):
                        k, n = b % 2, b // 2
                        wait(pe, marked[k], i * (3 - k) + n + 1)
                        count(pe, counts[:, 0:NJ], hot, k).then_inc(used[k], 1)
                pe.matmul(counts[:, 0:NJ], nothing[:, 0:NP], nothing[:, 0:NJ], start=False, stop=True,
                          skip_group_check=True).then_inc(counted, 1)
                pe.wait_ge(rows_ok, 1)
                pe.transpose(row_ps[0:D + 2, 0:P], rows33[:, 0, :], g.ident[:, :])
                pe.transpose(row_ps[0:D + 2, P:2 * P], rows33[:, 1, :], g.ident[:, :]).then_inc(rows_ps, 1)
                pe.wait_ge(below_ok, 2)
                pe.wait_ge(tot_ok, 1)
                pe.matmul(tot_ps[:, 0:1], below[:, :], tot[:, :], start=True, stop=True).then_inc(based, 1)

            @block.vector
            def _(dve):
                chain = Chain(dve, link)
                chain(dve.memset(nothing[:, :], 0.0))
                chain(dve.memset(running[:, SLOTS - 1, T - 1, :], 0.0))
                dve.memset(zero_slot[:, :], 0.0).then_inc(prepared, 1)
                chain(dve.tensor_copy(g.dst_f[:, :], g.dst_i[:, :]))
                chain(dve.tensor_copy(next_f[:, :], g.next_i[:, :]))
                chain(dve.tensor_tensor(g.keep[:, :], g.dst_f[:, 1:EPP + 1], g.dst_f[:, 0:EPP], ALU.is_equal))
                chain(dve.tensor_scalar(g.pen[:, :], g.keep[:, :], BIG, -BIG, ALU.mult, ALU.add))
                digits(dve, chain, g.dst_f[:, 1:EPP + 1], g.high, g.low, g.scratch)
                chain(dve.tensor_copy(g.first_dst[:, :], g.dst_i[:, 1:2]))

                @repeat(dve, LOOPS)
                def _(i):
                    for b in range(SLOTS):
                        at = i * (SLOTS * T) + b * T
                        k, n = b % 2, b // 2
                        wait(dve, used[k], i * (3 - k) + n)
                        mark(dve, hot, k, g.steps, g.high, g.low, at).then_inc(marked[k], 1)
                        wait(dve, gathered[b], (i + 1) * (16 * T))
                        wait(dve, stored[b], i * 16)
                        before = (b - 1) % SLOTS
                        wait(dve, scanned[before], i + 1 if b else i)
                        for f in range(D):
                            last = dve.tensor_tensor_scan(
                                running[:, b, :, f], g.keep[:, bass.ds(at, T)], rows[:, b, :, f],
                                running[:, before, T - 1, f:f + 1], ALU.mult, ALU.add)
                        last.then_inc(scanned[b], 1)
                dve.wait_ge(scanned[SLOTS - 1], LOOPS)
                chain(dve.tensor_copy(g.tail[:, 0:D], running[:, SLOTS - 1, T - 1, :]))
                chain(dve.tensor_tensor(edge[:, 0:1], g.dst_f[:, EPP:EPP + 1], next_f[:, :], ALU.is_equal))
                chain(dve.tensor_tensor(edge[:, 1:2], g.dst_f[:, 1:2], g.dst_f[:, EPP:EPP + 1], ALU.is_equal))
                chain(dve.tensor_copy(edge[:, 2:3], g.keep[:, 0:1]))
                chain(dve.tensor_scalar(g.scratch[:, :], g.dst_f[:, 1:EPP + 1], g.dst_f[:, 1:2], None, ALU.is_equal))
                chain(dve.tensor_reduce(edge[:, 3:4], g.scratch[:, :], AX.X, ALU.add))
                chain(dve.tensor_tensor(edge[:, 4:5], edge[:, 0:1], edge[:, 1:2], ALU.mult))
                chain(dve.tensor_scalar(edge[:, 4:5], edge[:, 4:5], -1.0, 1.0, ALU.mult, ALU.add))
                chain(dve.tensor_tensor(edge[:, 4:5], edge[:, 4:5], edge[:, 2:3], ALU.mult))
                chain(dve.tensor_copy(edge[:, 5:6], g.iota_e[:, :]))
                chain(dve.tensor_copy(edge[:, 6:7], g.spare_row[:, :]))
                chain(dve.scalar_tensor_tensor(edge[:, 5:6], edge[:, 5:6], -1.0, edge[:, 3:4], ALU.add, ALU.add))
                chain(dve.tensor_tensor(edge[:, 5:6], edge[:, 5:6], edge[:, 6:7], ALU.subtract))
                chain(dve.tensor_tensor(edge[:, 5:6], edge[:, 5:6], edge[:, 4:5], ALU.mult))
                chain(dve.tensor_tensor(edge[:, 5:6], edge[:, 5:6], edge[:, 6:7], ALU.add))
                chain(dve.tensor_copy(g.head_idx[:, :], edge[:, 5:6]))
                chain(dve.tensor_tensor(edge[:, 7:8], edge[:, 1:2], edge[:, 2:3], ALU.mult))
                chain(dve.tensor_copy(rows33[:, 0, :], spread(edge[:, 7:8], [P, D + 2])))
                dve.tensor_scalar(rows33[:, 1, :], rows33[:, 0, :], BIG, -BIG, ALU.mult, ALU.add).then_inc(rows_ok, 1)
                dve.wait_ge(rows_ps, 1)
                chain(dve.tensor_copy(g.keep_row[:, :], row_ps[0:D + 2, 0:P]))
                chain(dve.tensor_copy(g.pen_row[:, :], row_ps[0:D + 2, P:2 * P]))
                dve.wait_ge(counted, 1)
                chain(dve.tensor_copy(g.deg[:, :], counts[:, 0:NJ]))
                chain(dve.tensor_scalar(g.mask[:, :], g.deg[:, :], 0.0, None, ALU.is_gt))
                chain(dve.tensor_scalar(g.pen_node[:, :], g.mask[:, :], BIG, -BIG, ALU.mult, ALU.add))
                chain(dve.memset(work[:, :], 1.0))
                chain(dve.tensor_tensor_scan(cum[:, :], work[:, :], g.deg[:, :], 0.0, ALU.mult, ALU.add))
                dve.tensor_copy(tot[:, :], cum[:, NJ - 1:NJ]).then_inc(tot_ok, 1)
                dve.wait_ge(based, 1)
                chain(dve.tensor_copy(tot[:, :], tot_ps[:, 0:1]))
                chain(dve.tensor_scalar(cum[:, :], cum[:, :], tot[:, 0:1], None, ALU.add))
                chain(dve.tensor_scalar(work[:, :], cum[:, :], -1.0, 0.0, ALU.add, ALU.max))
                chain(dve.tensor_copy(g.end_idx[:, :], work[:, :]))
                chain(dve.tensor_copy(work[:, :], g.node_id[:, :]))
                chain(dve.tensor_scalar(work[:, :], work[:, :], float(E), None, ALU.add))
                chain(dve.tensor_tensor(cum[:, :], cum[:, :], g.deg[:, :], ALU.subtract))
                chain(dve.tensor_tensor(cum[:, :], cum[:, :], work[:, :], ALU.subtract))
                chain(dve.tensor_tensor(cum[:, :], cum[:, :], g.mask[:, :], ALU.mult))
                chain(dve.tensor_tensor(cum[:, :], cum[:, :], work[:, :], ALU.add))
                chain(dve.tensor_copy(g.start_idx[:, :], cum[:, :]))


def gcn_nodes(nc, g):
    wide = [NP, NJ, D]
    with ExitStack() as stack:
        m = Pools(nc, stack, "gcn_n")
        agg, out = m.sb("agg", wide), m.sb("out", wide)
        carry(nc, g, "sum", g.run, g.tail, agg)
        link, root_in, root = m.sem("link"), m.sem("root_in"), m.sem("root")
        with nc.Block() as block:
            @block.vector
            def _(dve):
                chain = Chain(dve, link)
                dve.tensor_scalar(g.stat[:, 0, :], g.deg[:, :], 1.0, None, ALU.add).then_inc(root_in, 1)
                chain(dve.tensor_tensor(agg[:, :, :], agg[:, :, :], spread(g.mask[:, :, None], wide), ALU.mult))
                chain(dve.tensor_tensor(agg[:, :, :], agg[:, :, :], g.m0[:, :, :], ALU.add))
                dve.wait_ge(root, 1)
                chain(dve.reciprocal(g.stat[:, 0, :], g.stat[:, 0, :]))
                chain(dve.tensor_tensor(agg[:, :, :], agg[:, :, :], spread(g.stat[:, 0, :, None], wide), ALU.mult))

            @block.scalar
            def _(act):
                act.wait_ge(root_in, 1)
                act.activation(g.stat[:, 0, :], g.stat[:, 0, :], ACT.Sqrt).then_inc(root, 1)

        def to_out(dve, ps, at, _):
            return dve.tensor_tensor(out[:, bass.ds(at, GJ), :], ps, spread(g.bias[0:NP, 0:1, 0:D], [NP, GJ, D]), ALU.add)

        node_linear(nc, "gcn_lin", g.ident, [(agg, g.wg)], D, to_out)
        link2, var, std = m.sem("link2"), m.sem("var"), m.sem("std")
        with nc.Block() as block:
            @block.vector
            def _(dve):
                chain = Chain(dve, link2)
                chain(dve.scalar_tensor_tensor(out[:, :, :], out[:, :, :], 0.0, g.h0[:, :, :], ALU.max, ALU.add))
                chain(dve.tensor_tensor(g.x[:, :, :], g.x[:, :, :], out[:, :, :], ALU.add))
                layer_norm(dve, None, chain, g.x, agg, g.stat, var, std)

            @block.scalar
            def _(act):
                norm_root(act, g.stat, var, std)
    spline_table(nc, g)


def spline_table(nc, g):
    def to_table(dve, ps, at, rows):
        dve.tensor_copy(rows, ps[:, :, 0:K1 * D])
        return dve.tensor_copy(g.rooted[:, bass.ds(at, GJ), :], ps[:, :, K1 * D:K1 * D + D])

    node_linear(nc, "spl_tab", g.ident, [(g.x, g.w_y)], (K1 + 1) * D, to_table, (g.spline_rows, K1 * D))


def spline_edges(nc, g, a):
    with ExitStack() as stack:
        m = Pools(nc, stack, "spln")
        idx = m.sb("idx", [P, SLOTS, T1], I32)
        rows = m.sb("rows", [P, SLOTS, T1, K1 * D])
        halves = m.sb("halves", [P, SLOTS, T1, 2, 3 * D])
        third, part = m.sb("third", [P, 2, T1, 3 * D]), m.sb("part", [P, T, 3 * D])
        msg3, msg, running = m.sb("msg3", [P, T, 3, D]), m.sb("msg", [P, T, D]), m.sb("running", [P, 2, T, D])
        place = m.sb("place", [P, EPP + T, 2])
        coef = m.sb("coef", [P, T, 2, 3])
        placed, link, scanned, stored, based, halved = (
            m.sem(n) for n in ("placed", "link", "scanned", "stored", "based", "halved"))
        idx_ready, gathered, slot_free = (m.sems(n) for n in ("idx_ready", "gathered", "slot_free"))

        with nc.Block() as block:
            @block.scalar
            def _(act):
                for b in range(SLOTS):
                    stage_ahead(act, g, idx, idx_ready, T1, 0, b)

                @repeat(act, LOOPS1)
                def _(i):
                    wait(act, based, i + 1)
                    for b in range(SLOTS):
                        wait(act, gathered[b], (i + 1) * (16 * T1))
                        stage_ahead(act, g, idx, idx_ready, T1, i + 1, b)
                        wait(act, slot_free[b], i)
                        for t in range(T1):
                            for c in range(2):
                                last = act.activation(
                                    halves[:, b, t, c, :], rows[:, b, t, c * 3 * D:(c + 1) * 3 * D], ACT.Copy,
                                    scale=coef[:, b * T1 + t, 0, c:c + 1])
                        last.then_inc(halved, 1)

            @block.gpsimd
            def _(pool):
                gather_rows(pool, g.spline_rows, rows, idx, idx_ready, slot_free, gathered, T1, LOOPS1)

            @block.sync
            def _(sp):
                sp.dma_start(place[:, 0:EPP, :],
                             a["edge_attr_2"].rearrange("(p t) c -> p t c", p=P)).then_inc(placed, 16)
                run_rows = by_partition(g.run[0:E, 0:D])

                @repeat(sp, LOOPS1)
                def _(i):
                    wait(sp, scanned, i + 1)
                    sp.dma_start(run_rows[:, bass.ds(i * T, T), :], running[:, 0]).then_inc(stored, 16)
                sp.wait_ge(stored, 16 * LOOPS1)

            @block.vector
            def _(dve):
                chain = Chain(dve, link)

                def basis(i):
                    chain(dve.tensor_scalar(coef[:, :, :, 1], place[:, bass.ds(i * T, T), :], 0.0, 1.0,
                                            ALU.max, ALU.min))
                    dve.tensor_scalar(coef[:, :, :, 0], coef[:, :, :, 1], -2.0, 1.0, ALU.mult, ALU.add)
                    chain(dve.tensor_scalar(coef[:, :, :, 2], coef[:, :, :, 1], 2.0, -1.0, ALU.mult, ALU.add))
                    chain(dve.tensor_tensor(coef[:, :, :, 1], coef[:, :, :, 0], coef[:, :, :, 2], ALU.max))
                    dve.tensor_scalar(coef[:, :, :, 1], coef[:, :, :, 1], -1.0, 1.0, ALU.mult, ALU.add)
                    dve.tensor_scalar(coef[:, :, :, 0], coef[:, :, :, 0], 0.0, None, ALU.max)
                    dve.tensor_scalar(coef[:, :, :, 2], coef[:, :, :, 2], 0.0, None, ALU.max).then_inc(based, 1)

                chain(dve.memset(running[:, 1, T - 1, :], 0.0))
                chain(dve.memset(place[:, EPP:EPP + T, :], 0.0))
                dve.wait_ge(placed, 16)
                basis(0)

                @repeat(dve, LOOPS1)
                def _(i):
                    chain.loop(i, 2 * SLOTS + 1 + 3 + 2 + 1)
                    wait(dve, based, i + 1)
                    for b in range(SLOTS):
                        wait(dve, gathered[b], (i + 1) * (16 * T1))
                        edges = slice(b * T1, b * T1 + T1)
                        chain(dve.tensor_tensor(third[:, b % 2], rows[:, b, :, 6 * D:9 * D],
                                                spread(coef[:, edges, 0, 2:3], [P, T1, 3 * D]), ALU.mult))
                        wait(dve, halved, i * SLOTS + b + 1)
                        chain(dve.tensor_tensor(part[:, edges, :], halves[:, b, :, 0, :], halves[:, b, :, 1, :], ALU.add))
                        dve.tensor_tensor(part[:, edges, :], part[:, edges, :], third[:, b % 2],
                                          ALU.add).then_inc(slot_free[b], 1)
                    wait(dve, slot_free[SLOTS - 1], i + 1)
                    chain(dve.tensor_tensor(msg3[:, :, :, :], part[:, :, :].rearrange("p t (a f) -> p t a f", a=3),
                                            spread(coef[:, :, 1, :, None], [P, T, 3, D]), ALU.mult))
                    basis(i + 1)
                    chain(dve.tensor_tensor(msg[:, :, :], msg3[:, :, 0, :], msg3[:, :, 1, :], ALU.add))
                    chain(dve.tensor_tensor(msg[:, :, :], msg[:, :, :], msg3[:, :, 2, :], ALU.add))
                    wait(dve, stored, i * 16)
                    for f in range(D):
                        last = dve.tensor_tensor_scan(
                            running[:, 0, :, f], g.keep[:, bass.ds(i * T, T)], msg[:, :, f],
                            running[:, 1, T - 1, f:f + 1], ALU.mult, ALU.add)
                    last.then_inc(scanned, 1)
                    wait(dve, scanned, i + 1)
                    chain(dve.tensor_copy(running[:, 1, T - 1, :], running[:, 0, T - 1, :]))
                chain.end_loop(LOOPS1)
                chain(dve.tensor_copy(g.tail[:, 0:D], running[:, 1, T - 1, :]))


def spline_nodes(nc, g):
    wide = [NP, NJ, D]
    with ExitStack() as stack:
        m = Pools(nc, stack, "spl_n")
        agg = m.sb("agg", wide)
        carry(nc, g, "sum", g.run, g.tail, agg)
        link, var, std = m.sem("link"), m.sem("var"), m.sem("std")
        table = m.sb("table", [NP, NJ, D + 1])
        with nc.Block() as block:
            @block.vector
            def _(dve):
                chain = Chain(dve, link)
                chain(dve.tensor_scalar(g.stat[:, 0, :], g.deg[:, :], 1.0, None, ALU.max))
                chain(dve.reciprocal(g.stat[:, 0, :], g.stat[:, 0, :]))
                chain(dve.tensor_tensor(g.stat[:, 0, :], g.stat[:, 0, :], g.mask[:, :], ALU.mult))
                chain(dve.tensor_tensor(agg[:, :, :], agg[:, :, :], spread(g.stat[:, 0, :, None], wide), ALU.mult))
                chain(dve.tensor_tensor(agg[:, :, :], agg[:, :, :], g.rooted[:, :, :], ALU.add))
                chain(dve.tensor_tensor(agg[:, :, :], agg[:, :, :], spread(g.bias[0:NP, 1:2, 0:D], wide), ALU.add))
                chain(dve.tensor_tensor(g.x[:, :, :], g.x[:, :, :], agg[:, :, :], ALU.add))
                layer_norm(dve, None, chain, g.x, agg, g.stat, var, std)
                chain(dve.tensor_copy(table[:, :, 0:D], g.x[:, :, :]))
                chain(dve.tensor_tensor(agg[:, :, :], g.x[:, :, :], spread(g.score_w[0:NP, None, :], wide), ALU.mult))
                chain(dve.tensor_reduce(table[:, :, D:D + 1], agg[:, :, :], AX.X, ALU.add))

            @block.scalar
            def _(act):
                norm_root(act, g.stat, var, std)
        write_rows(nc, "att_tab", [(g.att_rows, table[:, :, :])])


def attention_edges(nc, g):
    with ExitStack() as stack:
        m = Pools(nc, stack, "attn")
        idx = m.sb("idx", [P, SLOTS, T], I32)
        rows, running = m.sb("rows", [P, SLOTS, T, D + 1]), m.sb("running", [P, SLOTS, T, D + 2])
        top, drift, weighted = m.sb("top", [P, T + 1]), m.sb("drift", [P, 2, T]), m.sb("weighted", [P, T, D + 1])
        score = m.sb("score", [P, T])
        idx_ready, gathered, scanned, stored = (m.sems(n) for n in ("idx_ready", "gathered", "scanned", "stored"))
        link, exp_in, exp_out = m.sem("link"), m.sem("exp_in"), m.sem("exp_out")

        with nc.Block() as block:
            @block.scalar
            def _(act):
                for b in range(SLOTS):
                    stage_ahead(act, g, idx, idx_ready, T, 0, b)

                @repeat(act, LOOPS)
                def _(i):
                    for b in range(SLOTS):
                        wait(act, gathered[b], (i + 1) * (16 * T))
                        stage_ahead(act, g, idx, idx_ready, T, i + 1, b)
                        wait(act, exp_in, i * SLOTS + b + 1)
                        act.activation(drift[:, :, :], drift[:, :, :], ACT.Exp).then_inc(exp_out, 1)

            @block.gpsimd
            def _(pool):
                gather_rows(pool, g.att_rows, rows, idx, idx_ready, scanned, gathered, T, LOOPS)

            @block.sync
            def _(sp):
                store_running(sp, running, by_partition(g.run[0:E, 0:D + 2]), scanned, stored, LOOPS)
                finish_stores(sp, stored, LOOPS)

            @block.vector
            def _(dve):
                chain = Chain(dve, link)
                chain(dve.memset(running[:, SLOTS - 1, T - 1, 0:D + 1], 0.0))
                chain(dve.memset(top[:, T:T + 1], -BIG))
                chain(dve.memset(drift[:, :, :], 0.0))
                @repeat(dve, LOOPS)
                def _(i):
                    chain.loop(i, 8 * SLOTS)
                    for b in range(SLOTS):
                        at = i * (SLOTS * T) + b * T
                        before = (b - 1) % SLOTS
                        chain(dve.tensor_copy(top[:, 0:1], top[:, T:T + 1]))
                        wait(dve, gathered[b], (i + 1) * (16 * T))
                        chain(dve.tensor_scalar(score[:, :], rows[:, b, :, D], -1.0, None, ALU.mult))
                        chain(dve.tensor_tensor_scan(top[:, 1:T + 1], g.pen[:, bass.ds(at, T)], score[:, :],
                                                     top[:, 0:1], ALU.add, ALU.max))
                        chain(dve.tensor_tensor(drift[:, 0, :], top[:, 0:T], g.pen[:, bass.ds(at, T)], ALU.add))
                        chain(dve.tensor_tensor(drift[:, 0, :], drift[:, 0, :], top[:, 1:T + 1], ALU.subtract))
                        dve.tensor_tensor(drift[:, 1, :], score[:, :], top[:, 1:T + 1],
                                          ALU.subtract).then_inc(exp_in, 1)
                        wait(dve, exp_out, i * SLOTS + b + 1)
                        chain(dve.tensor_tensor(weighted[:, :, 0:D], rows[:, b, :, 0:D],
                                                spread(drift[:, 1, :, None], [P, T, D]), ALU.mult))
                        chain(dve.tensor_copy(weighted[:, :, D], drift[:, 1, :]))
                        wait(dve, stored[b], i * 16)
                        wait(dve, scanned[before], i + 1 if b else i)
                        chain(dve.tensor_copy(running[:, b, :, D + 1], top[:, 1:T + 1]))
                        for f in range(D + 1):
                            last = dve.tensor_tensor_scan(
                                running[:, b, :, f], drift[:, 0, :], weighted[:, :, f],
                                running[:, before, T - 1, f:f + 1], ALU.mult, ALU.add)
                        last.then_inc(scanned[b], 1)
                        wait(dve, scanned[b], i + 1)
                chain.end_loop(LOOPS)
                chain(dve.tensor_copy(g.tail[:, :], running[:, SLOTS - 1, T - 1, :]))


def attention_nodes(nc, g):
    wide = [NP, NJ, D]
    with ExitStack() as stack:
        m = Pools(nc, stack, "att_n")
        state, agg, out = m.sb("state", [NP, NJ, D + 2]), m.sb("agg", wide), m.sb("out", wide)
        carry(nc, g, "softmax", g.run, g.tail, state)
        link, link2, var, std = (m.sem(n) for n in ("link", "link2", "var", "std"))
        with nc.Block() as block:
            @block.vector
            def _(dve):
                chain = Chain(dve, link)
                chain(dve.tensor_tensor(g.stat[:, 0, :], state[:, :, D], g.mask[:, :], ALU.mult))
                chain(dve.scalar_tensor_tensor(g.stat[:, 0, :], g.stat[:, 0, :], 1.0, g.mask[:, :],
                                               ALU.add, ALU.subtract))
                chain(dve.reciprocal(g.stat[:, 0, :], g.stat[:, 0, :]))
                chain(dve.tensor_tensor(g.stat[:, 0, :], g.stat[:, 0, :], g.mask[:, :], ALU.mult))
                chain(dve.tensor_tensor(agg[:, :, :], state[:, :, 0:D], spread(g.stat[:, 0, :, None], wide), ALU.mult))

        def to_out(dve, ps, at, _):
            return dve.tensor_tensor(out[:, bass.ds(at, GJ), :], ps, spread(g.bias[0:NP, 2:3, 0:D], [NP, GJ, D]), ALU.add)

        node_linear(nc, "att_lin", g.ident, [(agg, g.w_a), (g.x, g.w_s)], D, to_out)
        with nc.Block() as block:
            @block.vector
            def _(dve):
                chain = Chain(dve, link2)
                chain(dve.tensor_tensor(agg[:, :, :], spread(g.mask[:, :, None], wide),
                                        spread(g.bias[0:NP, 3:4, 0:D], wide), ALU.mult))
                chain(dve.tensor_tensor(out[:, :, :], out[:, :, :], agg[:, :, :], ALU.add))
                chain(dve.tensor_tensor(g.x[:, :, :], g.x[:, :, :], out[:, :, :], ALU.add))
                layer_norm(dve, None, chain, g.x, agg, g.stat, var, std)

            @block.scalar
            def _(act):
                norm_root(act, g.stat, var, std)

    def to_table(dve, ps, at, rows):
        return dve.tensor_tensor(rows, ps, spread(g.bias[0:NP, 5:6, 0:H], [NP, GJ, H]), ALU.add)

    node_linear(nc, "mlp_tab", g.ident, [(g.x, g.w_p)], H, to_table, (g.mlp_rows, H))
    with ExitStack() as stack:
        m = Pools(nc, stack, "mlp_spread")
        placed, sent = m.sem("placed"), m.sem("sent")
        with nc.Block() as block:
            @block.gpsimd
            def _(pool):
                for j in range(NJ):
                    pool.indirect_dma_start(
                        g.fill_rows, bass.IndirectOffsetOnAxis(ap=g.start_idx[:, j:j + 1], axis=0),
                        g.x[:, j, :], None).then_inc(placed, 16)
                pool.wait_ge(placed, 16 * NJ)

            @block.sync
            def _(sp):
                sp.dma_start(by_partition(g.table[:, 0:D], NP), g.x[:, :, :]).then_inc(sent, 16)
                sp.wait_ge(sent, 16)


def mlp_edges(nc, g, a):
    GE = 5
    PER = T // GE
    GROUPS = SLOTS * PER
    with ExitStack() as stack:
        m = Pools(nc, stack, "edge_mlp")
        idx = m.sb("idx", [P, SLOTS, T], I32)
        rows = m.sb("rows", [P, SLOTS, T, H])
        first_rows, attr, x_dst = (m.sb(n, [P, SLOTS, T, D]) for n in ("first_rows", "attr", "x_dst"))
        value, running = m.sb("value", [P, 2, T, D]), m.sb("running", [P, SLOTS, T, D])
        in_t, hid = m.sb("in_t", [P, 2, 4, P]), m.sb("hid", [P, 2, GE * H])
        hid_t = m.sb("hid_t", [P, 2, 3, P])
        in_ps, hid_ps, hid_t_ps, val_ps = (m.ps(n, [P, 2, 512]) for n in ("in_ps", "hid_ps", "hid_t_ps", "val_ps"))
        idx_ready, gathered, scanned, stored = (m.sems(n) for n in ("idx_ready", "gathered", "scanned", "stored"))
        loaded, spread_ok = m.sems("loaded"), m.sems("spread_ok")
        (started, turned, turned_sb, product, summed, hid_turned, hid_turned_sb, valued, value_sb, first) = (
            m.sem(n) for n in ("started turned turned_sb product summed hid_turned hid_turned_sb valued value_sb "
                               "first").split())

        with nc.Block() as block:
            @block.sync
            def _(sp):
                places = by_partition(g.fill_rows[0:E, :])
                attrs = by_partition(a["edge_attr_32"])
                run_rows = by_partition(g.run[0:E, 0:D])

                def load(i, b, at):
                    sp.dma_start(first_rows[:, b], places[:, bass.ds(at, T), :]).then_inc(loaded[b], 16)
                    sp.dma_start(attr[:, b], attrs[:, bass.ds(at, T), :]).then_inc(loaded[b], 16)

                for b in range(SLOTS):
                    load(0, b, b * T)
                @repeat(sp, LOOPS - 1)
                def _(i):
                    for b in range(SLOTS):
                        wait(sp, scanned[b], i + 1)
                        sp.dma_start(run_rows[:, bass.ds(i * (SLOTS * T) + b * T, T), :],
                                     running[:, b]).then_inc(stored[b], 16)
                        load(i, b, (i + 1) * (SLOTS * T) + b * T)
                for b in range(SLOTS):
                    sp.wait_ge(scanned[b], LOOPS)
                    at = (LOOPS - 1) * SLOTS * T + b * T
                    sp.dma_start(run_rows[:, at:at + T, :], running[:, b]).then_inc(stored[b], 16)
                finish_stores(sp, stored, LOOPS)

            @block.gpsimd
            def _(pool):
                pool.indirect_dma_start(x_dst[:, SLOTS - 1, T - 1, :], None, g.table[:, 0:D],
                                        bass.IndirectOffsetOnAxis(ap=g.first_dst[:, 0:1], axis=0)).then_inc(first, 16)
                gather_rows(pool, g.mlp_rows, rows, idx, idx_ready, scanned, gathered, T, LOOPS)

            @block.scalar
            def _(act):
                for b in range(SLOTS):
                    stage_ahead(act, g, idx, idx_ready, T, 0, b)

                @repeat(act, LOOPS)
                def _(i):
                    n = i * GROUPS
                    for s in range(GROUPS + 3):
                        if s < GROUPS:
                            k = s % 2
                            wait(act, turned, n + s + 1)
                            wait(act, product, n + max(s - 1, 0))
                            act.activation(in_t[:, k, 0:2, :], in_ps[:, k, 0:2 * P].rearrange("p (c e) -> p c e", e=P),
                                           ACT.Copy)
                            act.activation(in_t[0:D, k, 2:4, :],
                                           in_ps[0:D, k, 2 * P:4 * P].rearrange("p (c e) -> p c e", e=P),
                                           ACT.Copy).then_inc(turned_sb, 1)
                        if 0 <= s - 2 < GROUPS:
                            u = s - 2
                            k = u % 2
                            wait(act, hid_turned, n + u + 1)
                            wait(act, valued, n + max(u - 1, 0))
                            act.activation(hid_t[:, k, 0:2, :], hid_t_ps[:, k, 0:2 * P].rearrange("p (c e) -> p c e", e=P),
                                           ACT.Relu)
                            act.activation(hid_t[0:H, k, 2, :], hid_t_ps[0:H, k, 2 * P:3 * P],
                                           ACT.Relu).then_inc(hid_turned_sb, 1)
                            if u % PER == 0:
                                wait(act, gathered[u // PER], (i + 1) * (16 * T))
                                stage_ahead(act, g, idx, idx_ready, T, i + 1, u // PER)
                        if 0 <= s - 3 < GROUPS:
                            u = s - 3
                            b, c = u // PER, u % PER
                            wait(act, valued, n + u + 1)
                            if c == 0 and b >= 2:
                                wait(act, scanned[b - 2], i + 1)
                            elif c == 0:
                                wait(act, scanned[SLOTS - 1], i)
                            act.activation(value[:, b % 2, c * GE:c * GE + GE, :],
                                           val_ps[:, u % 2, 0:GE * D].rearrange("p (t f) -> p t f", f=D),
                                           ACT.Copy).then_inc(value_sb, 1)

            @block.tensor
            def _(pe):
                @repeat(pe, LOOPS)
                def _(i):
                    n = i * GROUPS

                    def turn(s):
                        b, at, k = s // PER, s % PER * GE, s % 2
                        if s % PER == 0:
                            wait(pe, loaded[b], (i + 1) * 32)
                            wait(pe, spread_ok[b], i + 1)
                        wait(pe, turned_sb, n + max(s - 1, 0))
                        for c, (tile, lo, hi) in enumerate(((attr, 0, 4), (x_dst, 0, 4), (attr, 4, 5), (x_dst, 4, 5))):
                            last = pe.transpose(in_ps[0:(hi - lo) * D, k, c * P:c * P + P],
                                                tile[:, b, at + lo:at + hi, :].rearrange("p t f -> p (t f)"), g.ident[:, :])
                        last.then_inc(turned, 1)

                    def first_product(s):
                        k = s % 2
                        wait(pe, turned_sb, n + s + 1)
                        wait(pe, summed, n + max(s - 1, 0))
                        for lanes, t, c in ((slice(0, P), 0, 0), (slice(0, D), 4, 2)):
                            out = hid_ps[:, k, t * H:(t + 4) * H] if t == 0 else hid_ps[:, k, t * H:t * H + H]
                            wide = slice(0, 4 if t == 0 else 1)
                            pe.matmul(out, in_t[lanes, k, c, :], g.w_e[lanes, wide, :], start=True, stop=False)
                            last = pe.matmul(out, in_t[lanes, k, c + 1, :], g.w_d[lanes, wide, :],
                                             start=False, stop=True)
                        last.then_inc(product, 1)

                    def turn_hidden(s):
                        k = s % 2
                        wait(pe, summed, n + s + 1)
                        wait(pe, hid_turned_sb, n + max(s - 1, 0))
                        for c in range(3):
                            w = 2 * H if c < 2 else H
                            last = pe.transpose(hid_t_ps[0:w, k, c * P:c * P + P], hid[:, k, c * 2 * H:c * 2 * H + w],
                                                g.ident[:, :])
                        last.then_inc(hid_turned, 1)

                    def second_product(s):
                        k = s % 2
                        wait(pe, hid_turned_sb, n + s + 1)
                        wait(pe, value_sb, n + max(s - 1, 0))
                        for c in range(3):
                            lanes, wide = (slice(0, P), slice(0, 2)) if c < 2 else (slice(0, H), slice(0, 1))
                            at = 2 * c * D
                            last = pe.matmul(val_ps[:, k, at:at + (2 * D if c < 2 else D)], hid_t[lanes, k, c, :],
                                             g.w_v[lanes, wide, :], start=True, stop=True)
                        last.then_inc(valued, 1)

                    for s in range(GROUPS + 3):
                        for lag, stage in enumerate((turn, first_product, turn_hidden, second_product)):
                            if 0 <= s - lag < GROUPS:
                                stage(s - lag)

            @block.vector
            def _(dve):
                dve.memset(running[:, SLOTS - 1, T - 1, :], -BIG).then_inc(started, 1)
                dve.wait_ge(started, 1)
                dve.wait_ge(first, 16)
                @repeat(dve, LOOPS)
                def _(i):
                    n = i * GROUPS

                    def spread_rows(b):
                        at, before = i * (SLOTS * T) + b * T, (b - 1) % SLOTS
                        wait(dve, loaded[b], (i + 1) * 32)
                        wait(dve, spread_ok[before], i + 1 if b else i)
                        for f in range(D):
                            last = dve.tensor_tensor_scan(
                                x_dst[:, b, :, f], g.keep[:, bass.ds(at, T)], first_rows[:, b, :, f],
                                x_dst[:, before, T - 1, f:f + 1], ALU.mult, ALU.add)
                        last.then_inc(spread_ok[b], 1)

                    def add_source(s):
                        b, at, k = s // PER, s % PER * GE, s % 2
                        if s % PER == 0:
                            wait(dve, gathered[b], (i + 1) * (16 * T))
                        wait(dve, product, n + s + 1)
                        wait(dve, hid_turned, n + max(s - 1, 0))
                        dve.tensor_tensor(hid[:, k, :], hid_ps[:, k, 0:GE * H],
                                          rows[:, b, at:at + GE, :].rearrange("p t f -> p (t f)"),
                                          ALU.add).then_inc(summed, 1)

                    def maximum(b):
                        at, before = i * (SLOTS * T) + b * T, (b - 1) % SLOTS
                        wait(dve, value_sb, n + (b + 1) * PER)
                        wait(dve, stored[b], i * 16)
                        wait(dve, scanned[before], i + 1 if b else i)
                        for f in range(D):
                            last = dve.tensor_tensor_scan(
                                running[:, b, :, f], g.pen[:, bass.ds(at, T)], value[:, b % 2, :, f],
                                running[:, before, T - 1, f:f + 1], ALU.add, ALU.max)
                        last.then_inc(scanned[b], 1)

                    spread_rows(0)
                    for s in range(GROUPS + 5):
                        if s % PER == 0 and s // PER + 1 < SLOTS:
                            spread_rows(s // PER + 1)
                        if 0 <= s - 1 < GROUPS:
                            add_source(s - 1)
                        if 0 <= s - 5 < GROUPS and (s - 5) % PER == PER - 1:
                            maximum((s - 5) // PER)
                dve.wait_ge(scanned[SLOTS - 1], LOOPS)
                dve.tensor_copy(g.tail[:, 0:D], running[:, SLOTS - 1, T - 1, :])


def mlp_nodes(nc, g, out):
    wide = [NP, NJ, D]
    with ExitStack() as stack:
        m = Pools(nc, stack, "mlp_n")
        top = m.sb("top", wide)
        carry(nc, g, "max", g.run, g.tail, top)
        link, var, std = m.sem("link"), m.sem("var"), m.sem("std")
        with nc.Block() as block:
            @block.vector
            def _(dve):
                chain = Chain(dve, link)
                chain(dve.tensor_tensor(top[:, :, :], top[:, :, :], spread(g.mask[:, :, None], wide), ALU.mult))
                chain(dve.tensor_tensor(top[:, :, :], top[:, :, :], spread(g.pen_node[:, :, None], wide), ALU.add))
                chain(dve.tensor_tensor(top[:, :, :], top[:, :, :], spread(g.bias[0:NP, 4:5, 0:D], wide), ALU.add))
                chain(dve.tensor_tensor(top[:, :, :], top[:, :, :], g.x[:, :, :], ALU.max))
                chain(dve.tensor_tensor(g.x[:, :, :], g.x[:, :, :], top[:, :, :], ALU.add))
                layer_norm(dve, None, chain, g.x, top, g.stat, var, std)

            @block.scalar
            def _(act):
                norm_root(act, g.stat, var, std)
        write_rows(nc, "result", [(out, g.x[:, :, :])])


class Globals:
    pass


def graph_layers(nc, a, out, stop=99):
    g = Globals()
    g.phase = 0
    Pools.live.clear()
    with ExitStack() as stack:
        m = Pools(nc, stack, "g")
        g.src = m.sb("src", [P, EPP + SLOTS * T], I32)
        g.keep, g.pen = m.sb("keep", [P, EPP]), m.sb("pen", [P, EPP])
        g.ident = m.sb("ident", [P, P])
        g.x = m.sb("x", [NP, NJ, D])
        g.rooted = m.sb("rooted", [NP, NJ, D])
        g.end_idx, g.start_idx, g.node_id = (m.sb(n, [NP, NJ], I32) for n in ("end_idx", "start_idx", "node_id"))
        g.mask, g.pen_node, g.deg = (m.sb(n, [NP, NJ]) for n in ("mask", "pen_node", "deg"))
        g.norm_src = m.sb("norm_src", [NP, NJ])
        g.stat = m.sb("stat", [NP, 2, NJ])
        g.head_idx, g.first_dst, g.iota_e = (m.sb(n, [P, 1], I32) for n in ("head_idx", "first_dst", "iota_e"))
        g.keep_row, g.pen_row = m.sb("keep_row", [D + 2, P]), m.sb("pen_row", [D + 2, P])
        g.tail = m.sb("tail", [P, D + 2])
        g.zeros = m.sb("zeros", [P, D + 2])
        g.score_w = m.sb("score_w", [P, D])
        g.bias = m.sb("bias", [P, 6, H])
        g.wg, g.w_s, g.w_a = (m.sb(n, [P, GJ, D]) for n in ("wg", "w_s", "w_a"))
        g.w_p, g.w_d, g.w_e = (m.sb(n, [P, GJ, H]) for n in ("w_p", "w_d", "w_e"))
        g.w_v = m.sb("w_v", [P, 2, D])
        g.w_y = m.sb("w_y", [P, GJ, (K1 + 1) * D])
        dram = lambda name, shape: nc.dram_tensor(name, shape, F32, kind="Internal").ap()
        g.table = dram("node_rows", (N, D))
        g.spline_rows = dram("spline_rows", (N, K1 * D))
        g.att_rows = dram("att_rows", (N, D + 1))
        g.mlp_rows = dram("mlp_rows", (N, H))
        g.fill_rows = dram("fill_rows", (E + N, D))
        runs = {w: dram(f"run{w}", (E + P, w)) for w in (D, D + 2)}
        with ExitStack() as first:
            f = Pools(nc, first, "f")
            g.h0 = f.sb("h0", [NP, NJ, D])
            g.m0 = g.rooted
            g.high, g.low = f.sb("high", [P, EPP], BF16), f.sb("low", [P, EPP], BF16)
            g.dst_i, g.dst_f = f.sb("dst_i", [P, EPP + 1], I32), f.sb("dst_f", [P, EPP + 1])
            g.scratch, g.next_i, g.spare_row = f.sb("scratch", [P, EPP]), f.sb("next_i", [P, 1], I32), f.sb("spare_row", [P, 1], I32)
            g.steps = f.sb("steps", [P, NP, T], BF16)
            g.run = runs[D + 2]
            prepare(nc, g, a)
            write_rows(nc, "m0", [(g.table, g.m0[:, :, :]), ])
            g.run = runs[D]
            spare_rows(nc, g)
            gcn_edges(nc, g)
            gcn_nodes(nc, g)
        clear_semaphores(nc)
        if stop > 1:
            spline_edges(nc, g, a)
            spline_nodes(nc, g)
        if stop > 2:
            g.run = runs[D + 2]
            attention_edges(nc, g)
            attention_nodes(nc, g)
        clear_semaphores(nc)
        if stop > 3:
            g.run = runs[D]
            mlp_edges(nc, g, a)
            mlp_nodes(nc, g, out)
        else:
            write_rows(nc, "result", [(out, g.x[:, :, :])])


def spare_rows(nc, g):
    with ExitStack() as stack:
        sent = Pools(nc, stack, "spare").sem("sent")
        with nc.Block() as block:
            @block.sync
            def _(sp):
                sp.dma_start(g.run[E:E + P, :], g.zeros[:, 0:D]).then_inc(sent, 16)
                sp.wait_ge(sent, 16)


_INS = ['x', 'src', 'dst', 'edge_attr_2', 'edge_attr_32', 'L0_gnn_W1', 'L0_gnn_b1', 'L0_gnn_W2', 'L0_gnn_b2',
        'L0_gnn_Wg', 'L0_gnn_bg', 'L1_gnn_weight', 'L1_gnn_root_w', 'L1_gnn_root_b', 'L2_gnn_w1_W', 'L2_gnn_w1_b',
        'L2_gnn_w2_W', 'L2_gnn_w2_b', 'L2_gnn_a', 'L3_gnn_W1', 'L3_gnn_b1', 'L3_gnn_W2', 'L3_gnn_b2']


def kernel(**inputs):
    import numpy as _np
    import concourse.bacc as _bacc
    from concourse.bass_utils import run_bass_kernel_spmd as _run

    nc = _bacc.Bacc("TRN2", target_bir_lowering=False, num_devices=1)
    arrays, aps = {}, {}
    for name in _INS:
        v = _np.ascontiguousarray(inputs[name])
        arrays[f"in_{name}"] = v
        aps[name] = nc.dram_tensor(f"in_{name}", v.shape, mybir.dt.from_np(v.dtype), kind="ExternalInput").ap()
    out = nc.dram_tensor("out_x", (N, D), F32, kind="ExternalOutput").ap()
    graph_layers(nc, aps, out)
    r = _run(nc, [arrays], core_ids=[0])
    return r.results[0]["out_x"]
```

```python
from contextlib import ExitStack

import concourse.bass as bass
from concourse import mybir

F32 = mybir.dt.float32
I32 = mybir.dt.int32
BF16 = mybir.dt.bfloat16
ALU = mybir.AluOpType
ACT = mybir.ActivationFunctionType
AX = mybir.AxisListType

N, E, D, H = 12500, 400000, 32, 64
P = 128
EPP = E // P
NP, NJ = 125, 100
T = 25
SLOTS = 5
LOOPS = EPP // (T * SLOTS)
T1 = 5
LOOPS1 = EPP // (T1 * SLOTS)
K1 = 9
HOT = 3
USES = [len(range(k, SLOTS, HOT)) for k in range(HOT)]
GJ = 4
CHUNKS = 5
CJ = NJ // CHUNKS
GROUPS = CJ // GJ
BIG = 1e38
MAGIC = 12582912.0
EPS = 1e-5


def repeat(eng, count):
    def build(body):
        body(0)
        with eng.Fori(1, count) as i:
            body(i)
    return build


def wait(eng, sem, value):
    if not isinstance(value, int) or value > 0:
        eng.wait_ge(sem, value)


class Chain:

    def __init__(self, eng, sem):
        self.eng, self.sem, self.n, self.base = eng, sem, 0, None

    def __call__(self, ins):
        ins.then_inc(self.sem, 1)
        self.n += 1
        self.eng.wait_ge(self.sem, self.n if self.base is None else self.base + self.n)

    def loop(self, i, per_iteration):
        if self.base is None:
            self.start = self.n
        self.n, self.per = 0, per_iteration
        self.base = i * per_iteration + self.start

    def end_loop(self, iterations):
        assert self.n == self.per, (self.n, self.per)
        self.n, self.base = self.start + iterations * self.per, None


class Pools:

    live = []

    def __init__(self, nc, stack, tag):
        self.nc, self.stack, self.tag = nc, stack, tag

    def sb(self, name, shape, dt=F32):
        return self.stack.enter_context(self.nc.sbuf_tensor(f"{self.tag}_{name}", shape, dt))

    def ps(self, name, shape):
        return self.stack.enter_context(self.nc.psum_tensor(f"{self.tag}_{name}", shape, F32))

    def sem(self, name):
        self.live.append(self.nc.alloc_semaphore(name=f"{self.tag}_{name}"))
        return self.live[-1]

    def sems(self, name, n=SLOTS):
        return [self.sem(f"{name}{k}") for k in range(n)]


def clear_semaphores(nc):
    nc.clear_and_free_semaphores(Pools.live)
    nc.all_engine_barrier()
    Pools.live.clear()


def by_partition(ap, parts=P):
    return ap.rearrange("(p t) f -> p t f", p=parts)


def spread(ap, shape):
    return ap.to_broadcast(shape)




def stage_indices(act, src, idx, idx_ready, gathered, tiles, loops):
    @repeat(act, loops)
    def _(i):
        for b in range(SLOTS):
            wait(act, gathered[b], i * (16 * tiles))
            act.activation(idx[:, b, :], src[:, bass.ds(i * (SLOTS * tiles) + b * tiles, tiles)],
                           ACT.Copy).then_inc(idx_ready[b], 1)


def stage_ahead(act, g, idx, idx_ready, tiles, i, b):
    act.activation(idx[:, b, :], g.src[:, bass.ds(i * (SLOTS * tiles) + b * tiles, tiles)],
                   ACT.Copy).then_inc(idx_ready[b], 1)


def gather_rows(pool, table, rows, idx, idx_ready, slot_free, gathered, tiles, loops):
    @repeat(pool, loops)
    def _(i):
        for b in range(SLOTS):
            wait(pool, idx_ready[b], i + 1)
            pool.nop(nofuse=True)
            wait(pool, slot_free[b], i)
            pool.nop(nofuse=True)
            for t in range(tiles):
                pool.indirect_dma_start(
                    rows[:, b, t, :], None, table, bass.IndirectOffsetOnAxis(ap=idx[:, b, t:t + 1], axis=0)
                ).then_inc(gathered[b], 16)


def store_running(sp, running, run_rows, scanned, stored, loops):
    @repeat(sp, loops)
    def _(i):
        for b in range(SLOTS):
            wait(sp, scanned[b], i + 1)
            sp.dma_start(run_rows[:, bass.ds(i * (SLOTS * T) + b * T, T), :], running[:, b]).then_inc(stored[b], 16)


def finish_stores(sp, stored, loops):
    for b in range(SLOTS):
        sp.wait_ge(stored[b], 16 * loops)


def layer_norm(dve, chain, g, cols, tmp, var_ok, std_ok, n, done):
    wide = [NP, CJ, D]
    x, mean, var = g.x[:, cols, :], g.stat[:, 0, cols], g.stat[:, 1, cols]
    chain(dve.tensor_reduce(mean, x, AX.X, ALU.add))
    chain(dve.tensor_scalar(mean, mean, 1.0 / D, None, ALU.mult))
    chain(dve.tensor_tensor(x, x, spread(g.stat[:, 0, cols, None], wide), ALU.subtract))
    chain(dve.tensor_tensor(tmp[:, cols, 0:D], x, x, ALU.mult))
    chain(dve.tensor_reduce(var, tmp[:, cols, 0:D], AX.X, ALU.add))
    dve.tensor_scalar(var, var, 1.0 / D, EPS, ALU.mult, ALU.add).then_inc(var_ok, 1)
    dve.wait_ge(std_ok, n + 1)
    chain(dve.reciprocal(var, var))
    dve.tensor_tensor(x, x, spread(g.stat[:, 1, cols, None], wide), ALU.mult).then_inc(done, 1)


class Linear:

    def __init__(self, terms, width):
        self.terms, self.width, self.wide = terms, width, width * GJ > 512


def node_phase(nc, g, tag, run_rows, rows, before, linear, take, after, finish=None, table=None, sends=(),
               root_first=None, place=None):
    with ExitStack() as stack:
        m = Pools(nc, stack, tag)
        fetched, row_sent = m.sems("fetched", CHUNKS), m.sems("row_sent", 2)
        (link, made, var_ok, std_ok, normed, finished, staged, turned_ps, turned_sb, product, taken, taken_act,
         sent, root_in, root, placed, half) = (m.sem(n) for n in (
             "link made var_ok std_ok normed finished staged turned_ps turned_sb product taken taken_act "
             "sent root_in root placed half").split())
        kinds = [k for k in (linear, table and table[0]) if k]
        nt = max([len(k.terms) for k in kinds], default=1)
        if kinds:
            stage, turned = m.sb("stage", [NP, 2, nt, GJ * D]), m.sb("turned", [P, 2, nt, NP])
            turn_ps, small_ps = m.ps("turn_ps", [P, 2, 512]), m.ps("small_ps", [NP, 2, 512])
        if table:
            row_stage = m.sb("row_stage", [NP, 2, GJ, table[1].shape[1]])
        if table and table[0].wide:
            wide_ps = m.ps("wide_ps", [NP, GJ, 512])
        turns = []
        for c in range(CHUNKS):
            turns += [(c, linear)] if linear else []
            turns += [(c - 1, table[0])] if table and c else []
        turns += [(CHUNKS - 1, table[0])] if table else []
        jobs = [(c, k, u) for c, k in turns for u in range(GROUPS)]

        def batch(c, kind):
            return [n for n, (c_, k, _) in enumerate(jobs) if c_ == c and k is kind]

        def cols_of(n):
            c, _, u = jobs[n]
            return slice(c * CJ + u * GJ, c * CJ + (u + 1) * GJ)

        def before_of(n, wide):
            return sum(1 for _, k, _ in jobs[:n] if k.wide == wide)

        def result(n):
            k = jobs[n][1]
            if k.wide:
                return wide_ps[:, :, 0:k.width]
            return small_ps[:, before_of(n, False) % 2, 0:GJ * k.width].rearrange("p (q w) -> p q w", q=GJ)

        def table_number(n):
            return sum(1 for _, k, _ in jobs[:n] if table and k is table[0])

        with nc.Block() as block:
            @block.gpsimd
            def _(pool):
                for c in range(CHUNKS):
                    for j in range(c * CJ, (c + 1) * CJ):
                        pool.indirect_dma_start(rows[:, j, :], None, run_rows, bass.IndirectOffsetOnAxis(
                            ap=g.end_idx[:, j:j + 1], axis=0)).then_inc(fetched[c], 16)
                if place is not None:
                    for c in range(CHUNKS):
                        pool.wait_ge(normed, c + 1)
                        for j in range(c * CJ, (c + 1) * CJ):
                            pool.indirect_dma_start(
                                place, bass.IndirectOffsetOnAxis(ap=g.start_idx[:, j:j + 1], axis=0),
                                g.x[:, j, :], None).then_inc(placed, 16)
                    pool.wait_ge(placed, 16 * NJ)

            @block.scalar
            def _(act):
                if root_first:
                    act.wait_ge(root_in, 1)
                    act.activation(root_first, root_first, ACT.Sqrt).then_inc(root, 1)

                def put(n):
                    act.wait_ge(turned_ps, n - 1) if n > 1 else None
                    for k, (tile, _) in enumerate(jobs[n][1].terms):
                        last = act.activation(stage[:, n % 2, k, :].rearrange("p (j f) -> p j f", f=D),
                                              tile[:, cols_of(n), :], ACT.Copy)
                    last.then_inc(staged, 1)

                def take_wide(n):
                    act.wait_ge(product, n + 1)
                    b = table_number(n)
                    if b >= 2:
                        act.wait_ge(row_sent[b % 2], 16 * (b // 2))
                    act.activation(row_stage[:, b % 2, 2:4, :], wide_ps[:, 2:4, 0:K1 * D], ACT.Copy)
                    at = cols_of(n).start
                    act.activation(g.rooted[:, at + 2:at + 4, :], wide_ps[:, 2:4, K1 * D:K1 * D + D],
                                   ACT.Copy).then_inc(taken_act, 1)

                def turn_rows(c, kind):
                    ns = batch(c, kind)
                    put(ns[0])
                    for n in ns:
                        if n + 1 in ns:
                            put(n + 1)
                        act.wait_ge(turned_ps, n + 1)
                        act.wait_ge(product, n - 1) if n > 1 else None
                        k = len(kind.terms)
                        act.activation(turned[:, n % 2, 0:k, :],
                                       turn_ps[:, n % 2, 0:k * NP].rearrange("p (k n) -> p k n", n=NP),
                                       ACT.Copy).then_inc(turned_sb, 1)
                        if kind.wide and n > ns[0]:
                            take_wide(n - 1)
                    if kind.wide:
                        take_wide(ns[-1])

                for c in range(CHUNKS):
                    if linear:
                        act.wait_ge(made, c + 1)
                        turn_rows(c, linear)
                    act.wait_ge(var_ok, c + 1)
                    cols = slice(c * CJ, (c + 1) * CJ)
                    act.activation(g.stat[:, 1, cols], g.stat[:, 1, cols], ACT.Sqrt).then_inc(std_ok, 1)
                    if table and c:
                        act.wait_ge(normed, c)
                        turn_rows(c - 1, table[0])
                if table:
                    act.wait_ge(normed, CHUNKS)
                    turn_rows(CHUNKS - 1, table[0])

            @block.tensor
            def _(pe):
                def turn(n):
                    pe.wait_ge(staged, n + 1)
                    pe.wait_ge(turned_sb, n - 1) if n > 1 else None
                    for k in range(len(jobs[n][1].terms)):
                        last = pe.transpose(turn_ps[:, n % 2, k * NP:(k + 1) * NP], stage[:, n % 2, k, :],
                                            g.ident[0:NP, 0:NP])
                    last.then_inc(turned_ps, 1)

                for c, kind in turns:
                    ns = batch(c, kind)
                    turn(ns[0])
                    for n in ns:
                        if n + 1 in ns:
                            turn(n + 1)
                        pe.wait_ge(turned_sb, n + 1)
                        b = before_of(n, kind.wide)
                        last_term = len(kind.terms) - 1
                        if kind.wide:
                            for q in range(GJ):
                                if b and q == 0:
                                    pe.wait_ge(taken, n)
                                if b and q == 2:
                                    pe.wait_ge(taken_act, b)
                                lanes = slice(D * q, D * q + D)
                                for k, (_, w) in enumerate(kind.terms):
                                    last = pe.matmul(wide_ps[:, q, 0:kind.width], turned[lanes, n % 2, k, :],
                                                     w[lanes, q, :], start=(k == 0), stop=(k == last_term))
                                if q == 1:
                                    last.then_inc(half, 1)
                        else:
                            if b >= 2:
                                pe.wait_ge(taken, n - 1)
                            for k, (_, w) in enumerate(kind.terms):
                                last = pe.matmul(result(n), turned[:, n % 2, k, :], w[:, :, :],
                                                 start=(k == 0), stop=(k == last_term))
                        last.then_inc(product, 1)

            @block.vector
            def _(dve):
                chain = Chain(dve, link)
                if root_first:
                    dve.tensor_scalar(root_first, g.deg[:, :], 1.0, None, ALU.add).then_inc(root_in, 1)
                    dve.wait_ge(root, 1)
                    chain(dve.reciprocal(root_first, root_first))

                def tables(c):
                    for n in batch(c, table[0]):
                        b = table_number(n)
                        if table[0].wide:
                            dve.wait_ge(half, b + 1)
                        else:
                            dve.wait_ge(product, n + 1)
                        if b >= 2:
                            dve.wait_ge(row_sent[b % 2], 16 * (b // 2))
                        if table[0].wide:
                            dve.tensor_copy(row_stage[:, b % 2, 0:2, :], wide_ps[:, 0:2, 0:K1 * D])
                            at = cols_of(n).start
                            last = dve.tensor_copy(g.rooted[:, at:at + 2, :], wide_ps[:, 0:2, K1 * D:K1 * D + D])
                        else:
                            last = dve.tensor_tensor(row_stage[:, b % 2], result(n),
                                                     spread(table[2], [NP, GJ, table[0].width]), ALU.add)
                        last.then_inc(taken, 1)

                for c in range(CHUNKS):
                    cols = slice(c * CJ, (c + 1) * CJ)
                    dve.wait_ge(fetched[c], 16 * CJ)
                    before(dve, chain, cols, made)
                    if linear:
                        for n in batch(c, linear):
                            dve.wait_ge(product, n + 1)
                            take(dve, result(n), cols_of(n)).then_inc(taken, 1)
                        dve.wait_ge(taken, batch(c, linear)[-1] + 1)
                    after(dve, chain, cols)
                    layer_norm(dve, chain, g, cols, rows, var_ok, std_ok, c, normed)
                    if finish:
                        dve.wait_ge(normed, c + 1)
                        finish(dve, chain, cols).then_inc(finished, 1)
                    if table and c:
                        tables(c - 1)
                if table:
                    tables(CHUNKS - 1)

            @block.sync
            def _(sp):
                def tables(c):
                    for n in batch(c, table[0]):
                        b = table_number(n)
                        sp.wait_ge(taken, n + 1)
                        if table[0].wide:
                            sp.wait_ge(taken_act, b + 1)
                        sp.dma_start(by_partition(table[1], NP)[:, cols_of(n), :],
                                     row_stage[:, b % 2]).then_inc(row_sent[b % 2], 16)

                for c in range(CHUNKS):
                    cols = slice(c * CJ, (c + 1) * CJ)
                    sp.wait_ge(finished if finish else normed, c + 1)
                    for dram, tile in sends:
                        sp.dma_start(by_partition(dram, NP)[:, cols, :], tile[:, cols, :]).then_inc(sent, 16)
                    if table:
                        tables(c - 1) if c else None
                if table:
                    tables(CHUNKS - 1)
                if sends:
                    sp.wait_ge(sent, 16 * CHUNKS * len(sends))
                if table:
                    total = CHUNKS * GROUPS
                    sp.wait_ge(row_sent[0], 16 * ((total + 1) // 2))
                    sp.wait_ge(row_sent[1], 16 * (total // 2))


def carry(nc, g, kind, run_dram, tail):
    w = {"sum": D, "max": D, "softmax": D + 2}[kind]
    r = {"sum": D, "max": D, "softmax": D + 1}[kind]
    with ExitStack() as stack:
        m = Pools(nc, stack, f"carry{g.phase}")
        g.phase += 1
        ps = m.ps("ps", [P, 4, 512])
        tail_t, state = m.sb("tail_t", [r, P]), m.sb("state", [r, P + 1])
        head = m.sb("head", [P, w])
        tail_max, max_t = m.sb("tail_max", [P, r]), m.sb("max_t", [r, P])
        max_state, drift = m.sb("max_state", [r, P + 1]), m.sb("drift", [r, 2, P])
        new_max, fade = m.sb("new_max", [P, 1]), m.sb("fade", [P, 2])
        turned, scanned, back, exp_in, exp_out = (
            m.sem(x) for x in ("turned", "scanned", "back", "exp_in", "exp_out"))
        prepared, head_in, head_ok, head_out, link = (
            m.sem(x) for x in ("prepared", "head_in", "head_ok", "head_out", "link"))
        soft = kind == "softmax"

        with nc.Block() as block:
            @block.tensor
            def _(pe):
                if soft:
                    pe.wait_ge(prepared, 1)
                    pe.transpose(ps[0:r, 1, 0:P], tail_max[:, :], g.ident[:, :])
                pe.transpose(ps[0:r, 0, 0:P], tail[:, 0:r], g.ident[:, :]).then_inc(turned, 1)
                pe.wait_ge(scanned, 1)
                if soft:
                    pe.transpose(ps[:, 3, 0:r], max_state[:, 0:P], g.ident[0:r, 0:r])
                pe.transpose(ps[:, 2, 0:r], state[:, 0:P], g.ident[0:r, 0:r]).then_inc(back, 1)

            @block.scalar
            def _(act):
                if soft:
                    act.wait_ge(exp_in, 1)
                    act.activation(drift[:, :, :], drift[:, :, :], ACT.Exp).then_inc(exp_out, 1)
                    act.wait_ge(exp_in, 2)
                    act.activation(fade[:, :], fade[:, :], ACT.Exp).then_inc(exp_out, 1)

            @block.vector
            def _(dve):
                chain = Chain(dve, link)
                chain(dve.memset(state[:, 0:1], -BIG if kind == "max" else 0.0))
                if soft:
                    chain(dve.memset(max_state[:, 0:1], -BIG))
                    dve.tensor_copy(tail_max[:, :], spread(tail[:, D + 1:D + 2], [P, r])).then_inc(prepared, 1)
                dve.wait_ge(turned, 1)
                chain(dve.tensor_copy(tail_t[:, :], ps[0:r, 0, 0:P]))
                if kind == "sum":
                    dve.tensor_tensor_scan(state[:, 1:P + 1], g.keep_row[0:r, :], tail_t[:, :], 0.0,
                                           ALU.mult, ALU.add).then_inc(scanned, 1)
                elif kind == "max":
                    dve.tensor_tensor_scan(state[:, 1:P + 1], g.pen_row[0:r, :], tail_t[:, :], -BIG,
                                           ALU.add, ALU.max).then_inc(scanned, 1)
                else:
                    chain(dve.tensor_copy(max_t[:, :], ps[0:r, 1, 0:P]))
                    chain(dve.tensor_tensor_scan(max_state[:, 1:P + 1], g.pen_row[0:r, :], max_t[:, :], -BIG,
                                                 ALU.add, ALU.max))
                    chain(dve.tensor_tensor(drift[:, 0, :], max_state[:, 0:P], g.pen_row[0:r, :], ALU.add))
                    chain(dve.tensor_tensor(drift[:, 0, :], drift[:, 0, :], max_state[:, 1:P + 1], ALU.subtract))
                    dve.tensor_tensor(drift[:, 1, :], max_t[:, :], max_state[:, 1:P + 1],
                                      ALU.subtract).then_inc(exp_in, 1)
                    dve.wait_ge(exp_out, 1)
                    chain(dve.tensor_tensor(tail_t[:, :], tail_t[:, :], drift[:, 1, :], ALU.mult))
                    dve.tensor_tensor_scan(state[:, 1:P + 1], drift[:, 0, :], tail_t[:, :], 0.0,
                                           ALU.mult, ALU.add).then_inc(scanned, 1)
                dve.wait_ge(back, 1)
                dve.wait_ge(head_in, 16)
                if kind == "sum":
                    dve.tensor_tensor(head[:, :], head[:, :], ps[:, 2, 0:r], ALU.add).then_inc(head_ok, 1)
                elif kind == "max":
                    dve.tensor_tensor(head[:, :], head[:, :], ps[:, 2, 0:r], ALU.max).then_inc(head_ok, 1)
                else:
                    chain(dve.tensor_tensor(new_max[:, :], head[:, D + 1:D + 2], ps[:, 3, 0:1], ALU.max))
                    chain(dve.tensor_tensor(fade[:, 0:1], head[:, D + 1:D + 2], new_max[:, :], ALU.subtract))
                    dve.tensor_tensor(fade[:, 1:2], ps[:, 3, 0:1], new_max[:, :], ALU.subtract).then_inc(exp_in, 1)
                    dve.wait_ge(exp_out, 2)
                    chain(dve.tensor_scalar(head[:, 0:r], head[:, 0:r], fade[:, 0:1], None, ALU.mult))
                    chain(dve.tensor_copy(head[:, D + 1:D + 2], new_max[:, :]))
                    dve.scalar_tensor_tensor(head[:, 0:r], ps[:, 2, 0:r], fade[:, 1:2], head[:, 0:r],
                                             ALU.mult, ALU.add).then_inc(head_ok, 1)

            @block.gpsimd
            def _(pool):
                rows = run_dram[0:E + P, 0:w]
                pool.indirect_dma_start(head[:, :], None, rows, bass.IndirectOffsetOnAxis(
                    ap=g.head_idx[:, 0:1], axis=0)).then_inc(head_in, 16)
                pool.wait_ge(head_ok, 1)
                pool.indirect_dma_start(rows, bass.IndirectOffsetOnAxis(ap=g.head_idx[:, 0:1], axis=0),
                                        head[:, :], None).then_inc(head_out, 16)
                pool.wait_ge(head_out, 16)




def digits(dve, chain, ids, high, low, scratch):
    chain(dve.tensor_scalar(scratch[:, :], ids, 0.5, 1.0 / NJ, ALU.add, ALU.mult))
    chain(dve.tensor_scalar(scratch[:, :], scratch[:, :], -0.5, MAGIC, ALU.add, ALU.add))
    chain(dve.tensor_scalar(high[:, :], scratch[:, :], -MAGIC, None, ALU.add))
    chain(dve.scalar_tensor_tensor(low[:, :], high[:, :], -float(NJ), ids, ALU.mult, ALU.add))


def mark(dve, hot, b, steps, high, low, at):
    dve.tensor_tensor(hot[:, b, 0:NP, :], steps[:, :, :],
                      spread(high[:, None, bass.ds(at, T)], [P, NP, T]), ALU.is_equal)
    return dve.tensor_tensor(hot[:, b, NP:NP + NJ, :], steps[:, 0:NJ, :],
                             spread(low[:, None, bass.ds(at, T)], [P, NJ, T]), ALU.is_equal)


def count(pe, counts, hot, b):
    for t in range(T):
        last = pe.matmul(counts, hot[:, b, 0:NP, t], hot[:, b, NP:NP + NJ, t], start=False, stop=False,
                         skip_group_check=True)
    return last




def prepare(nc, g, a, spare):
    with ExitStack() as stack:
        m = Pools(nc, stack, "prep")
        dst_i, next_i = g.dst_i, g.next_i
        hot = m.sb("hot", [P, HOT, NP + NJ, T], BF16)
        nothing = m.sb("nothing", [P, NP], BF16)
        step_i, step_f = m.sb("step_i", [P, NP], I32), m.sb("step_f", [P, NP])
        w1, w2b, b1 = m.sb("w1", [P, GJ, H]), m.sb("w2b", [H + 1, D]), m.sb("b1", [H, 1])
        avec, w2l2 = m.sb("avec", [D, 1]), m.sb("w2l2", [D, D])
        acol = m.sb("acol", [D, P])
        stage, turned, hid = m.sb("stage", [NP, GJ * D]), m.sb("turned", [P, NP]), m.sb("hid", [H + 1, GJ * NP])
        counts = m.ps("counts", [NP, 512])
        turn_ps, hid_ps, h0_ps, small_ps = (m.ps(n, [P, 512]) for n in ("turn_ps", "hid_ps", "h0_ps", "small_ps"))
        names = ("src_in dst_in border x_in enc_in w_in filled link consts hid_one nothing_ok staged turned_ps "
                 "turned_sb hid_ready hid_sb h0_ready h0_out counted trash_ok rows_ok rows_ps ab_ok ab_ps root root_in "
                 "zero_out edges score_sb weights_zero table_ok table_out").split()
        s = {n: m.sem(n) for n in names}
        marked, used = m.sems("marked", HOT), m.sems("used", HOT)

        across = [(q, slice(D * q, D * q + D)) for q in range(GJ)]
        encoder = [(w1[r, q, :], a["L0_gnn_W1"]) for q, r in across]
        encoder += [(w2b[0:H, :], a["L0_gnn_W2"]), (w2b[H:H + 1, :], a["L0_gnn_b2"][None, :]),
                    (b1[:, :], a["L0_gnn_b1"][:, None])]
        others = [(avec[:, :], a["L2_gnn_a"].rearrange("z i -> i z")), (w2l2[:, :], a["L2_gnn_w2_W"])]
        for q, r in across:
            others += [(g.wg[r, q, :], a["L0_gnn_Wg"]),
                       (g.w_p[r, q, :], a["L3_gnn_W1"][0:D, :]),
                       (g.w_d[r, q, :], a["L3_gnn_W1"][D:2 * D, :]),
                       (g.w_e[r, q, :], a["L3_gnn_W1"][2 * D:3 * D, :]),
                       (g.w_y[r, q, 0:K1 * D].rearrange("i (k o) -> i k o", k=K1),
                        a["L1_gnn_weight"].rearrange("k i o -> i k o")),
                       (g.w_y[r, q, K1 * D:K1 * D + D], a["L1_gnn_root_w"].rearrange("o i -> i o")),
                       (g.w_s[r, q, :], a["L2_gnn_w1_W"].rearrange("o i -> i o")),
                       (g.w_a[r, q, :], a["L2_gnn_w2_W"].rearrange("o i -> i o"))]
        others += [(g.w_v[H * q:H * q + H, q, :], a["L3_gnn_W2"]) for q in range(2)]
        others += [(g.bias[:, k, 0:v.shape[0]], v[None, :].to_broadcast([P, v.shape[0]])) for k, v in enumerate(
            a[n] for n in ("L0_gnn_bg", "L1_gnn_root_b", "L2_gnn_w1_b", "L2_gnn_w2_b", "L3_gnn_b2", "L3_gnn_b1"))]

        with nc.Block() as block:
            @block.sync
            def _(sp):
                sp.dma_start(g.src[:, 0:EPP], a["src"].rearrange("(p t) -> p t", p=P)).then_inc(s["src_in"], 16)
                sp.dma_start(dst_i[:, 1:EPP + 1], a["dst"].rearrange("(p t) -> p t", p=P)).then_inc(s["dst_in"], 16)
                sp.wait_ge(s["filled"], 1)
                col = a["dst"].rearrange("(p t) -> p t", p=P)
                sp.dma_start(dst_i[1:P, 0:1], col[0:P - 1, EPP - 1:EPP],
                             allow_slow_non_contiguous=True).then_inc(s["border"], 16)
                sp.dma_start(next_i[0:P - 1, :], col[1:P, 0:1],
                             allow_slow_non_contiguous=True).then_inc(s["border"], 16)
                sp.dma_start(g.x[:, :, :], by_partition(a["x"], NP)).then_inc(s["x_in"], 16)
                sp.wait_ge(s["weights_zero"], 1)
                for tile, dram in encoder:
                    sp.dma_start(tile, dram, allow_slow_non_contiguous=True).then_inc(s["enc_in"], 16)
                for tile, dram in others:
                    sp.dma_start(tile, dram, allow_slow_non_contiguous=True).then_inc(s["w_in"], 16)
                sp.wait_ge(s["nothing_ok"], 1)
                for run in spare:
                    sp.dma_start(run[E:E + P, :], g.zeros[:, 0:run.shape[1]]).then_inc(s["zero_out"], 16)
                sp.wait_ge(s["zero_out"], 16 * len(spare))
                sp.wait_ge(s["dst_in"], 16)
                sp.wait_ge(s["border"], 32)
                sp.wait_ge(s["table_ok"], 1)
                sp.dma_start(by_partition(g.table, NP), g.m0[:, :, :]).then_inc(s["table_out"], 16)
                sp.wait_ge(s["table_out"], 16)

            @block.scalar
            def _(act):
                act.wait_ge(s["enc_in"], 16 * len(encoder))
                act.wait_ge(s["x_in"], 16)
                act.wait_ge(s["hid_one"], 1)
                @repeat(act, NJ // GJ)
                def _(i):
                    wait(act, s["turned_ps"], i)
                    act.activation(stage[:, :].rearrange("p (j f) -> p j f", f=D),
                                   g.x[:, bass.ds(i * GJ, GJ), :], ACT.Copy).then_inc(s["staged"], 1)
                    wait(act, s["turned_ps"], i + 1)
                    act.activation(turned[:, :], turn_ps[:, 0:NP], ACT.Copy).then_inc(s["turned_sb"], 1)
                    wait(act, s["hid_ready"], i + 1)
                    act.activation(hid[0:H, :], hid_ps[0:H, 0:GJ * NP], ACT.Relu, bias=b1[:, 0:1]).then_inc(s["hid_sb"], 1)
                    wait(act, s["h0_ready"], i + 1)
                    act.activation(g.h0[:, bass.ds(i * GJ, GJ), :],
                                   h0_ps[0:NP, 0:GJ * D].rearrange("p (j f) -> p j f", f=D),
                                   ACT.Relu).then_inc(s["h0_out"], 1)
                act.wait_ge(s["root_in"], 1)
                act.activation(g.norm_src[:, :], g.norm_src[:, :], ACT.Sqrt).then_inc(s["root"], 1)

            @block.gpsimd
            def _(pool):
                pool.memset(g.ident[:, :], 0.0).then_inc(s["edges"], 1)
                pool.iota(step_i[:, :], [[1, NP]], base=0, channel_multiplier=0).then_inc(s["consts"], 1)
                pool.iota(g.spare_row[:, :], [[1, 1]], base=E, channel_multiplier=1).then_inc(s["trash_ok"], 1)
                pool.iota(g.iota_e[:, :], [[0, 1]], base=0, channel_multiplier=EPP).then_inc(s["trash_ok"], 1)
                pool.iota(g.node_id[:, :], [[1, NJ]], base=0, channel_multiplier=NJ).then_inc(s["trash_ok"], 1)
                pool.wait_ge(s["trash_ok"], 3)
                pool.wait_ge(s["edges"], 1)
                pool.affine_select(out=g.ident[:, :], in_=g.ident[:, :], compare_op=ALU.not_equal, fill=1.0,
                                   base=0, pattern=[[-1, P]], channel_multiplier=1).then_inc(s["consts"], 1)

            @block.tensor
            def _(pe):
                pe.wait_ge(s["nothing_ok"], 1)
                pe.matmul(counts[:, 0:NJ], nothing[:, 0:NP], nothing[:, 0:NJ], start=True, stop=False,
                          skip_group_check=True)
                pe.wait_ge(s["consts"], 2)
                @repeat(pe, NJ // GJ)
                def _(i):
                    for b in range(SLOTS):
                        k, n = b % HOT, b // HOT
                        wait(pe, marked[k], i * USES[k] + n + 1)
                        count(pe, counts[:, 0:NJ], hot, k).then_inc(used[k], 1)
                        if b == 0:
                            wait(pe, s["staged"], i + 1)
                            pe.transpose(turn_ps[:, 0:NP], stage[:, :], g.ident[0:NP, 0:NP]).then_inc(s["turned_ps"], 1)
                        if b == 1:
                            wait(pe, s["turned_sb"], i + 1)
                            for q in range(GJ):
                                last = pe.matmul(hid_ps[0:H, q * NP:q * NP + NP], w1[:, q, :],
                                                 turned[:, :], start=True, stop=True)
                            last.then_inc(s["hid_ready"], 1)
                        if b == 3:
                            wait(pe, s["hid_sb"], i + 1)
                            for q in range(GJ):
                                last = pe.matmul(h0_ps[0:NP, q * D:q * D + D], hid[:, q * NP:q * NP + NP],
                                                 w2b[:, :], start=True, stop=True)
                            last.then_inc(s["h0_ready"], 1)
                pe.matmul(counts[:, 0:NJ], nothing[:, 0:NP], nothing[:, 0:NJ], start=False, stop=True,
                          skip_group_check=True).then_inc(s["counted"], 1)
                pe.wait_ge(s["w_in"], 16 * len(others))
                pe.wait_ge(s["ab_ok"], 1)
                pe.matmul(small_ps[:, 0:D], acol[:, :], w2l2[:, :], start=True, stop=True).then_inc(s["ab_ps"], 1)

            @block.vector
            def _(dve):
                chain = Chain(dve, s["link"])
                for w in (w1, g.wg, g.w_p, g.w_d, g.w_e, g.w_s, g.w_a, g.w_v):
                    dve.memset(w[:, :, :], 0.0)
                dve.memset(g.w_y[:, :, :], 0.0).then_inc(s["weights_zero"], 1)
                chain(dve.memset(dst_i[:, 0:1], -1))
                dve.memset(next_i[:, :], -1).then_inc(s["filled"], 1)
                chain(dve.memset(g.src[:, EPP:EPP + SLOTS * T], 0))
                chain(dve.memset(nothing[:, :], 0.0))
                dve.memset(g.zeros[:, :], 0.0).then_inc(s["nothing_ok"], 1)
                dve.memset(hid[H:H + 1, :], 1.0).then_inc(s["hid_one"], 1)
                dve.wait_ge(s["consts"], 2)
                chain(dve.tensor_copy(step_f[:, :], step_i[:, :]))
                chain(dve.tensor_copy(g.steps[:, :, :], spread(step_f[:, :, None], [P, NP, T])))
                dve.wait_ge(s["src_in"], 16)
                digits(dve, chain, g.src[:, 0:EPP], g.high, g.low, g.pen)
                @repeat(dve, EPP // (T * SLOTS))
                def _(i):
                    for b in range(SLOTS):
                        k, n = b % HOT, b // HOT
                        wait(dve, used[k], i * USES[k] + n)
                        mark(dve, hot, k, g.steps, g.high, g.low, i * (SLOTS * T) + b * T).then_inc(marked[k], 1)
                dve.wait_ge(s["w_in"], 16 * len(others))
                dve.tensor_copy(acol[:, :], spread(avec[:, :], [D, P])).then_inc(s["ab_ok"], 1)
                dve.wait_ge(s["ab_ps"], 1)
                dve.tensor_copy(g.score_w[:, :], small_ps[:, 0:D]).then_inc(s["score_sb"], 1)
                dve.wait_ge(s["counted"], 1)
                dve.tensor_scalar(g.norm_src[:, :], counts[:, 0:NJ], 1.0, None, ALU.add).then_inc(s["root_in"], 1)
                dve.wait_ge(s["root"], 1)
                chain(dve.reciprocal(g.norm_src[:, :], g.norm_src[:, :]))
                dve.wait_ge(s["h0_out"], NJ // GJ)
                dve.tensor_tensor(g.m0[:, :, :], g.h0[:, :, :], spread(g.norm_src[:, :, None], [NP, NJ, D]),
                                  ALU.mult).then_inc(s["table_ok"], 1)


def write_rows(nc, tag, pairs):
    with ExitStack() as stack:
        m = Pools(nc, stack, tag)
        sent = m.sem("sent")
        with nc.Block() as block:
            @block.sync
            def _(sp):
                for dram, rows in pairs:
                    sp.dma_start(by_partition(dram, NP), rows).then_inc(sent, 16)
                sp.wait_ge(sent, 16 * len(pairs))


def gcn_edges(nc, g):
    with ExitStack() as stack:
        m = Pools(nc, stack, "gcn")
        idx = m.sb("idx", [P, SLOTS, T], I32)
        rows, running = m.sb("rows", [P, SLOTS, T, D]), m.sb("running", [P, SLOTS, T, D])
        hot, nothing = m.sb("hot", [P, HOT, NP + NJ, T], BF16), m.sb("nothing", [P, NP], BF16)
        zero_slot = m.sb("zero_slot", [P, T * D])
        idx_ready, gathered, scanned, stored = (m.sems(n) for n in ("idx_ready", "gathered", "scanned", "stored"))
        marked, used = m.sems("marked", HOT), m.sems("used", HOT)
        prepared, counted, zeroed, link, ends_in = (m.sem(n) for n in ("prepared", "counted", "zeroed", "link", "ends_in"))
        tot, tot_ps = m.sb("tot", [NP, 1]), m.ps("tot_ps", [NP, 512])
        below, cum = m.sb("below", [NP, NP]), m.sb("cum", [NP, NJ])
        below_ok, tot_ok, based = m.sem("below_ok"), m.sem("tot_ok"), m.sem("based")
        counts = m.ps("counts", [NP, 512])
        work = m.sb("work", [NP, NJ])
        next_f, edge, rows33 = m.sb("next_f", [P, 1]), m.sb("edge", [P, 8]), m.sb("rows33", [P, 2, D + 2])
        row_ps, rows_ok, rows_ps = m.ps("row_ps", [P, 512]), m.sem("rows_ok"), m.sem("rows_ps_ok")

        with nc.Block() as block:
            @block.scalar
            def _(act):
                stage_indices(act, g.src, idx, idx_ready, gathered, T, LOOPS)

            @block.gpsimd
            def _(pool):
                pool.memset(below[:, :], 1.0).then_inc(below_ok, 1)
                pool.wait_ge(below_ok, 1)
                pool.affine_select(out=below[:, :], in_=below[:, :], compare_op=ALU.is_gt, fill=0.0,
                                   base=0, pattern=[[1, NP]], channel_multiplier=-1).then_inc(below_ok, 1)
                gather_rows(pool, g.table[:, 0:D], rows, idx, idx_ready, scanned, gathered, T, LOOPS)

            @block.sync
            def _(sp):
                sp.wait_ge(prepared, 1)
                fill = g.fill_rows[0:E, :].rearrange("(p t) f -> p (t f)", p=P)
                run_rows = by_partition(g.run[0:E, 0:D])
                @repeat(sp, LOOPS)
                def _(i):
                    for b in range(SLOTS):
                        sp.dma_start(fill[:, bass.ds(i * (SLOTS * T * D) + b * T * D, T * D)],
                                     zero_slot[:, :]).then_inc(zeroed, 16)
                        wait(sp, scanned[b], i + 1)
                        sp.dma_start(run_rows[:, bass.ds(i * (SLOTS * T) + b * T, T), :],
                                     running[:, b]).then_inc(stored[b], 16)
                finish_stores(sp, stored, LOOPS)
                sp.wait_ge(zeroed, 16 * LOOPS * SLOTS)

            @block.tensor
            def _(pe):
                pe.wait_ge(prepared, 1)
                pe.matmul(counts[:, 0:NJ], nothing[:, 0:NP], nothing[:, 0:NJ], start=True, stop=False,
                          skip_group_check=True)
                @repeat(pe, LOOPS)
                def _(i):
                    for b in range(SLOTS):
                        k, n = b % HOT, b // HOT
                        wait(pe, marked[k], i * USES[k] + n + 1)
                        count(pe, counts[:, 0:NJ], hot, k).then_inc(used[k], 1)
                pe.matmul(counts[:, 0:NJ], nothing[:, 0:NP], nothing[:, 0:NJ], start=False, stop=True,
                          skip_group_check=True).then_inc(counted, 1)
                pe.wait_ge(rows_ok, 1)
                pe.transpose(row_ps[0:D + 2, 0:P], rows33[:, 0, :], g.ident[:, :])
                pe.transpose(row_ps[0:D + 2, P:2 * P], rows33[:, 1, :], g.ident[:, :]).then_inc(rows_ps, 1)
                pe.wait_ge(below_ok, 2)
                pe.wait_ge(tot_ok, 1)
                pe.matmul(tot_ps[:, 0:1], below[:, :], tot[:, :], start=True, stop=True).then_inc(based, 1)

            @block.vector
            def _(dve):
                chain = Chain(dve, link)
                chain(dve.memset(nothing[:, :], 0.0))
                chain(dve.memset(running[:, SLOTS - 1, T - 1, :], 0.0))
                dve.memset(zero_slot[:, :], 0.0).then_inc(prepared, 1)
                chain(dve.tensor_copy(g.dst_f[:, :], g.dst_i[:, :]))
                chain(dve.tensor_copy(next_f[:, :], g.next_i[:, :]))
                chain(dve.tensor_tensor(g.keep[:, :], g.dst_f[:, 1:EPP + 1], g.dst_f[:, 0:EPP], ALU.is_equal))
                digits(dve, chain, g.dst_f[:, 1:EPP + 1], g.high, g.low, g.pen)
                chain(dve.tensor_scalar(g.pen[:, :], g.dst_f[:, 1:EPP + 1], g.dst_f[:, 1:2], None, ALU.is_equal))
                chain(dve.tensor_reduce(edge[:, 3:4], g.pen[:, :], AX.X, ALU.add))
                chain(dve.tensor_scalar(g.pen[:, :], g.keep[:, :], BIG, -BIG, ALU.mult, ALU.add))
                chain(dve.tensor_copy(g.first_dst[:, :], g.dst_i[:, 1:2]))

                @repeat(dve, LOOPS)
                def _(i):
                    for b in range(SLOTS):
                        at = i * (SLOTS * T) + b * T
                        k, n = b % HOT, b // HOT
                        wait(dve, used[k], i * USES[k] + n)
                        mark(dve, hot, k, g.steps, g.high, g.low, at).then_inc(marked[k], 1)
                        wait(dve, gathered[b], (i + 1) * (16 * T))
                        wait(dve, stored[b], i * 16)
                        before = (b - 1) % SLOTS
                        wait(dve, scanned[before], i + 1 if b else i)
                        for f in range(D):
                            last = dve.tensor_tensor_scan(
                                running[:, b, :, f], g.keep[:, bass.ds(at, T)], rows[:, b, :, f],
                                running[:, before, T - 1, f:f + 1], ALU.mult, ALU.add)
                        last.then_inc(scanned[b], 1)
                dve.wait_ge(scanned[SLOTS - 1], LOOPS)
                chain(dve.tensor_copy(g.tail[:, 0:D], running[:, SLOTS - 1, T - 1, :]))
                chain(dve.tensor_tensor(edge[:, 0:1], g.dst_f[:, EPP:EPP + 1], next_f[:, :], ALU.is_equal))
                chain(dve.tensor_tensor(edge[:, 1:2], g.dst_f[:, 1:2], g.dst_f[:, EPP:EPP + 1], ALU.is_equal))
                chain(dve.tensor_copy(edge[:, 2:3], g.keep[:, 0:1]))
                chain(dve.tensor_tensor(edge[:, 4:5], edge[:, 0:1], edge[:, 1:2], ALU.mult))
                chain(dve.tensor_scalar(edge[:, 4:5], edge[:, 4:5], -1.0, 1.0, ALU.mult, ALU.add))
                chain(dve.tensor_tensor(edge[:, 4:5], edge[:, 4:5], edge[:, 2:3], ALU.mult))
                chain(dve.tensor_copy(edge[:, 5:6], g.iota_e[:, :]))
                chain(dve.tensor_copy(edge[:, 6:7], g.spare_row[:, :]))
                chain(dve.scalar_tensor_tensor(edge[:, 5:6], edge[:, 5:6], -1.0, edge[:, 3:4], ALU.add, ALU.add))
                chain(dve.tensor_tensor(edge[:, 5:6], edge[:, 5:6], edge[:, 6:7], ALU.subtract))
                chain(dve.tensor_tensor(edge[:, 5:6], edge[:, 5:6], edge[:, 4:5], ALU.mult))
                chain(dve.tensor_tensor(edge[:, 5:6], edge[:, 5:6], edge[:, 6:7], ALU.add))
                chain(dve.tensor_copy(g.head_idx[:, :], edge[:, 5:6]))
                chain(dve.tensor_tensor(edge[:, 7:8], edge[:, 1:2], edge[:, 2:3], ALU.mult))
                chain(dve.tensor_copy(rows33[:, 0, :], spread(edge[:, 7:8], [P, D + 2])))
                dve.tensor_scalar(rows33[:, 1, :], rows33[:, 0, :], BIG, -BIG, ALU.mult, ALU.add).then_inc(rows_ok, 1)
                dve.wait_ge(rows_ps, 1)
                chain(dve.tensor_copy(g.keep_row[:, :], row_ps[0:D + 2, 0:P]))
                chain(dve.tensor_copy(g.pen_row[:, :], row_ps[0:D + 2, P:2 * P]))
                dve.wait_ge(counted, 1)
                chain(dve.tensor_copy(g.deg[:, :], counts[:, 0:NJ]))
                chain(dve.tensor_scalar(g.mask[:, :], g.deg[:, :], 0.0, None, ALU.is_gt))
                chain(dve.tensor_scalar(g.pen_node[:, :], g.mask[:, :], BIG, -BIG, ALU.mult, ALU.add))
                chain(dve.memset(work[:, :], 1.0))
                chain(dve.tensor_tensor_scan(cum[:, :], work[:, :], g.deg[:, :], 0.0, ALU.mult, ALU.add))
                dve.tensor_copy(tot[:, :], cum[:, NJ - 1:NJ]).then_inc(tot_ok, 1)
                dve.wait_ge(based, 1)
                chain(dve.tensor_copy(tot[:, :], tot_ps[:, 0:1]))
                chain(dve.tensor_scalar(cum[:, :], cum[:, :], tot[:, 0:1], None, ALU.add))
                chain(dve.tensor_scalar(work[:, :], cum[:, :], -1.0, 0.0, ALU.add, ALU.max))
                chain(dve.tensor_copy(g.end_idx[:, :], work[:, :]))
                chain(dve.tensor_copy(work[:, :], g.node_id[:, :]))
                chain(dve.tensor_scalar(work[:, :], work[:, :], float(E), None, ALU.add))
                chain(dve.tensor_tensor(cum[:, :], cum[:, :], g.deg[:, :], ALU.subtract))
                chain(dve.tensor_tensor(cum[:, :], cum[:, :], work[:, :], ALU.subtract))
                chain(dve.tensor_tensor(cum[:, :], cum[:, :], g.mask[:, :], ALU.mult))
                chain(dve.tensor_tensor(cum[:, :], cum[:, :], work[:, :], ALU.add))
                chain(dve.tensor_copy(g.start_idx[:, :], cum[:, :]))


def gcn_nodes(nc, g):
    with ExitStack() as stack:
        m = Pools(nc, stack, "gcn_n")
        agg, out = m.sb("agg", [NP, NJ, D]), m.sb("out", [NP, NJ, D])
        norm_dst = m.sb("norm_dst", [NP, NJ])
        wide = [NP, CJ, D]
        carry(nc, g, "sum", g.run, g.tail)

        def before(dve, chain, cols, made):
            chain(dve.tensor_tensor(agg[:, cols, :], agg[:, cols, :], spread(g.mask[:, cols, None], wide), ALU.mult))
            chain(dve.tensor_tensor(agg[:, cols, :], agg[:, cols, :], g.m0[:, cols, :], ALU.add))
            dve.tensor_tensor(agg[:, cols, :], agg[:, cols, :], spread(norm_dst[:, cols, None], wide),
                              ALU.mult).then_inc(made, 1)

        def take(dve, ps, cols):
            return dve.tensor_tensor(out[:, cols, :], ps, spread(g.bias[0:NP, 0:1, 0:D], [NP, GJ, D]), ALU.add)

        def after(dve, chain, cols):
            chain(dve.scalar_tensor_tensor(out[:, cols, :], out[:, cols, :], 0.0, g.h0[:, cols, :], ALU.max, ALU.add))
            chain(dve.tensor_tensor(g.x[:, cols, :], g.x[:, cols, :], out[:, cols, :], ALU.add))

        node_phase(nc, g, "gcn_node", g.run[0:E + P, 0:D], agg, before, Linear([(agg, g.wg)], D), take, after,
                   table=(Linear([(g.x, g.w_y)], (K1 + 1) * D), g.spline_rows, None), root_first=norm_dst[:, :])


def spline_edges(nc, g, a):
    with ExitStack() as stack:
        m = Pools(nc, stack, "spln")
        idx = m.sb("idx", [P, SLOTS, T1], I32)
        rows = m.sb("rows", [P, SLOTS, T1, K1 * D])
        halves = m.sb("halves", [P, SLOTS, T1, 2, 3 * D])
        third, part = m.sb("third", [P, 2, T1, 3 * D]), m.sb("part", [P, T, 3 * D])
        msg3, msg, running = m.sb("msg3", [P, T, 3, D]), m.sb("msg", [P, T, D]), m.sb("running", [P, 2, T, D])
        place = m.sb("place", [P, EPP + T, 2])
        coef = m.sb("coef", [P, T, 2, 3])
        placed, link, scanned, stored, based, halved = (
            m.sem(n) for n in ("placed", "link", "scanned", "stored", "based", "halved"))
        idx_ready, gathered, slot_free = (m.sems(n) for n in ("idx_ready", "gathered", "slot_free"))

        with nc.Block() as block:
            @block.scalar
            def _(act):
                for b in range(SLOTS):
                    stage_ahead(act, g, idx, idx_ready, T1, 0, b)

                @repeat(act, LOOPS1)
                def _(i):
                    wait(act, based, i + 1)
                    for b in range(SLOTS):
                        wait(act, gathered[b], (i + 1) * (16 * T1))
                        stage_ahead(act, g, idx, idx_ready, T1, i + 1, b)
                        wait(act, slot_free[b], i)
                        for t in range(T1):
                            for c in range(2):
                                last = act.activation(
                                    halves[:, b, t, c, :], rows[:, b, t, c * 3 * D:(c + 1) * 3 * D], ACT.Copy,
                                    scale=coef[:, b * T1 + t, 0, c:c + 1])
                        last.then_inc(halved, 1)

            @block.gpsimd
            def _(pool):
                gather_rows(pool, g.spline_rows, rows, idx, idx_ready, slot_free, gathered, T1, LOOPS1)

            @block.sync
            def _(sp):
                sp.dma_start(place[:, 0:EPP, :],
                             a["edge_attr_2"].rearrange("(p t) c -> p t c", p=P)).then_inc(placed, 16)
                run_rows = by_partition(g.run[0:E, 0:D])

                @repeat(sp, LOOPS1)
                def _(i):
                    wait(sp, scanned, i + 1)
                    sp.dma_start(run_rows[:, bass.ds(i * T, T), :], running[:, 0]).then_inc(stored, 16)
                sp.wait_ge(stored, 16 * LOOPS1)

            @block.vector
            def _(dve):
                chain = Chain(dve, link)

                def basis(i):
                    chain(dve.tensor_scalar(coef[:, :, :, 1], place[:, bass.ds(i * T, T), :], 0.0, 1.0,
                                            ALU.max, ALU.min))
                    dve.tensor_scalar(coef[:, :, :, 0], coef[:, :, :, 1], -2.0, 1.0, ALU.mult, ALU.add)
                    chain(dve.tensor_scalar(coef[:, :, :, 2], coef[:, :, :, 1], 2.0, -1.0, ALU.mult, ALU.add))
                    chain(dve.tensor_tensor(coef[:, :, :, 1], coef[:, :, :, 0], coef[:, :, :, 2], ALU.max))
                    dve.tensor_scalar(coef[:, :, :, 1], coef[:, :, :, 1], -1.0, 1.0, ALU.mult, ALU.add)
                    dve.tensor_scalar(coef[:, :, :, 0], coef[:, :, :, 0], 0.0, None, ALU.max)
                    dve.tensor_scalar(coef[:, :, :, 2], coef[:, :, :, 2], 0.0, None, ALU.max).then_inc(based, 1)

                chain(dve.memset(running[:, 1, T - 1, :], 0.0))
                chain(dve.memset(place[:, EPP:EPP + T, :], 0.0))
                dve.wait_ge(placed, 16)
                basis(0)

                @repeat(dve, LOOPS1)
                def _(i):
                    chain.loop(i, 2 * SLOTS + 1 + 3 + 2 + 1)
                    wait(dve, based, i + 1)
                    for b in range(SLOTS):
                        wait(dve, gathered[b], (i + 1) * (16 * T1))
                        edges = slice(b * T1, b * T1 + T1)
                        chain(dve.tensor_tensor(third[:, b % 2], rows[:, b, :, 6 * D:9 * D],
                                                spread(coef[:, edges, 0, 2:3], [P, T1, 3 * D]), ALU.mult))
                        wait(dve, halved, i * SLOTS + b + 1)
                        chain(dve.tensor_tensor(part[:, edges, :], halves[:, b, :, 0, :], halves[:, b, :, 1, :], ALU.add))
                        dve.tensor_tensor(part[:, edges, :], part[:, edges, :], third[:, b % 2],
                                          ALU.add).then_inc(slot_free[b], 1)
                    wait(dve, slot_free[SLOTS - 1], i + 1)
                    chain(dve.tensor_tensor(msg3[:, :, :, :], part[:, :, :].rearrange("p t (a f) -> p t a f", a=3),
                                            spread(coef[:, :, 1, :, None], [P, T, 3, D]), ALU.mult))
                    basis(i + 1)
                    chain(dve.tensor_tensor(msg[:, :, :], msg3[:, :, 0, :], msg3[:, :, 1, :], ALU.add))
                    chain(dve.tensor_tensor(msg[:, :, :], msg[:, :, :], msg3[:, :, 2, :], ALU.add))
                    wait(dve, stored, i * 16)
                    for f in range(D):
                        last = dve.tensor_tensor_scan(
                            running[:, 0, :, f], g.keep[:, bass.ds(i * T, T)], msg[:, :, f],
                            running[:, 1, T - 1, f:f + 1], ALU.mult, ALU.add)
                    last.then_inc(scanned, 1)
                    wait(dve, scanned, i + 1)
                    chain(dve.tensor_copy(running[:, 1, T - 1, :], running[:, 0, T - 1, :]))
                chain.end_loop(LOOPS1)
                chain(dve.tensor_copy(g.tail[:, 0:D], running[:, 1, T - 1, :]))


def spline_nodes(nc, g):
    with ExitStack() as stack:
        m = Pools(nc, stack, "spl_n")
        agg, table = m.sb("agg", [NP, NJ, D]), m.sb("table", [NP, NJ, D + 1])
        mean = m.sb("mean", [NP, NJ])
        wide = [NP, CJ, D]
        carry(nc, g, "sum", g.run, g.tail)

        def before(dve, chain, cols, made):
            chain(dve.tensor_scalar(mean[:, cols], g.deg[:, cols], 1.0, None, ALU.max))
            chain(dve.reciprocal(mean[:, cols], mean[:, cols]))
            chain(dve.tensor_tensor(mean[:, cols], mean[:, cols], g.mask[:, cols], ALU.mult))
            chain(dve.tensor_tensor(agg[:, cols, :], agg[:, cols, :], spread(mean[:, cols, None], wide), ALU.mult))

        def after(dve, chain, cols):
            chain(dve.tensor_tensor(agg[:, cols, :], agg[:, cols, :], g.rooted[:, cols, :], ALU.add))
            chain(dve.tensor_tensor(agg[:, cols, :], agg[:, cols, :], spread(g.bias[0:NP, 1:2, 0:D], wide), ALU.add))
            chain(dve.tensor_tensor(g.x[:, cols, :], g.x[:, cols, :], agg[:, cols, :], ALU.add))

        def finish(dve, chain, cols):
            chain(dve.tensor_copy(table[:, cols, 0:D], g.x[:, cols, :]))
            chain(dve.tensor_tensor(agg[:, cols, :], g.x[:, cols, :], spread(g.score_w[0:NP, None, :], wide), ALU.mult))
            return dve.tensor_reduce(table[:, cols, D:D + 1], agg[:, cols, :], AX.X, ALU.add)

        node_phase(nc, g, "spl_node", g.run[0:E + P, 0:D], agg, before, None, None, after, finish,
                   sends=[(g.att_rows, table)])


def attention_edges(nc, g):
    with ExitStack() as stack:
        m = Pools(nc, stack, "attn")
        idx = m.sb("idx", [P, SLOTS, T], I32)
        rows, running = m.sb("rows", [P, SLOTS, T, D + 1]), m.sb("running", [P, SLOTS, T, D + 2])
        top, drift, weighted = m.sb("top", [P, T + 1]), m.sb("drift", [P, 2, T]), m.sb("weighted", [P, T, D + 1])
        score = m.sb("score", [P, T])
        idx_ready, gathered, scanned, stored = (m.sems(n) for n in ("idx_ready", "gathered", "scanned", "stored"))
        link, exp_in, exp_out = m.sem("link"), m.sem("exp_in"), m.sem("exp_out")

        with nc.Block() as block:
            @block.scalar
            def _(act):
                for b in range(SLOTS):
                    stage_ahead(act, g, idx, idx_ready, T, 0, b)

                @repeat(act, LOOPS)
                def _(i):
                    for b in range(SLOTS):
                        wait(act, gathered[b], (i + 1) * (16 * T))
                        stage_ahead(act, g, idx, idx_ready, T, i + 1, b)
                        wait(act, exp_in, i * SLOTS + b + 1)
                        act.activation(drift[:, :, :], drift[:, :, :], ACT.Exp).then_inc(exp_out, 1)

            @block.gpsimd
            def _(pool):
                gather_rows(pool, g.att_rows, rows, idx, idx_ready, scanned, gathered, T, LOOPS)

            @block.sync
            def _(sp):
                store_running(sp, running, by_partition(g.run[0:E, 0:D + 2]), scanned, stored, LOOPS)
                finish_stores(sp, stored, LOOPS)

            @block.vector
            def _(dve):
                chain = Chain(dve, link)
                chain(dve.memset(running[:, SLOTS - 1, T - 1, 0:D + 1], 0.0))
                chain(dve.memset(top[:, T:T + 1], -BIG))
                chain(dve.memset(drift[:, :, :], 0.0))
                @repeat(dve, LOOPS)
                def _(i):
                    chain.loop(i, 8 * SLOTS)
                    for b in range(SLOTS):
                        at = i * (SLOTS * T) + b * T
                        before = (b - 1) % SLOTS
                        chain(dve.tensor_copy(top[:, 0:1], top[:, T:T + 1]))
                        wait(dve, gathered[b], (i + 1) * (16 * T))
                        chain(dve.tensor_scalar(score[:, :], rows[:, b, :, D], -1.0, None, ALU.mult))
                        chain(dve.tensor_tensor_scan(top[:, 1:T + 1], g.pen[:, bass.ds(at, T)], score[:, :],
                                                     top[:, 0:1], ALU.add, ALU.max))
                        chain(dve.tensor_tensor(drift[:, 0, :], top[:, 0:T], g.pen[:, bass.ds(at, T)], ALU.add))
                        chain(dve.tensor_tensor(drift[:, 0, :], drift[:, 0, :], top[:, 1:T + 1], ALU.subtract))
                        dve.tensor_tensor(drift[:, 1, :], score[:, :], top[:, 1:T + 1],
                                          ALU.subtract).then_inc(exp_in, 1)
                        wait(dve, exp_out, i * SLOTS + b + 1)
                        chain(dve.tensor_tensor(weighted[:, :, 0:D], rows[:, b, :, 0:D],
                                                spread(drift[:, 1, :, None], [P, T, D]), ALU.mult))
                        chain(dve.tensor_copy(weighted[:, :, D], drift[:, 1, :]))
                        wait(dve, stored[b], i * 16)
                        wait(dve, scanned[before], i + 1 if b else i)
                        chain(dve.tensor_copy(running[:, b, :, D + 1], top[:, 1:T + 1]))
                        for f in range(D + 1):
                            last = dve.tensor_tensor_scan(
                                running[:, b, :, f], drift[:, 0, :], weighted[:, :, f],
                                running[:, before, T - 1, f:f + 1], ALU.mult, ALU.add)
                        last.then_inc(scanned[b], 1)
                        wait(dve, scanned[b], i + 1)
                chain.end_loop(LOOPS)
                chain(dve.tensor_copy(g.tail[:, :], running[:, SLOTS - 1, T - 1, :]))


def attention_nodes(nc, g):
    with ExitStack() as stack:
        m = Pools(nc, stack, "att_n")
        state, agg, out = m.sb("state", [NP, NJ, D + 2]), m.sb("agg", [NP, NJ, D]), m.sb("out", [NP, NJ, D])
        share = m.sb("share", [NP, NJ])
        wide = [NP, CJ, D]
        carry(nc, g, "softmax", g.run, g.tail)

        def before(dve, chain, cols, made):
            chain(dve.tensor_tensor(share[:, cols], state[:, cols, D], g.mask[:, cols], ALU.mult))
            chain(dve.scalar_tensor_tensor(share[:, cols], share[:, cols], 1.0, g.mask[:, cols], ALU.add, ALU.subtract))
            chain(dve.reciprocal(share[:, cols], share[:, cols]))
            chain(dve.tensor_tensor(share[:, cols], share[:, cols], g.mask[:, cols], ALU.mult))
            dve.tensor_tensor(agg[:, cols, :], state[:, cols, 0:D], spread(share[:, cols, None], wide),
                              ALU.mult).then_inc(made, 1)

        def take(dve, ps, cols):
            return dve.tensor_tensor(out[:, cols, :], ps, spread(g.bias[0:NP, 2:3, 0:D], [NP, GJ, D]), ALU.add)

        def after(dve, chain, cols):
            chain(dve.tensor_tensor(agg[:, cols, :], spread(g.mask[:, cols, None], wide),
                                    spread(g.bias[0:NP, 3:4, 0:D], wide), ALU.mult))
            chain(dve.tensor_tensor(out[:, cols, :], out[:, cols, :], agg[:, cols, :], ALU.add))
            chain(dve.tensor_tensor(g.x[:, cols, :], g.x[:, cols, :], out[:, cols, :], ALU.add))

        node_phase(nc, g, "att_node", g.run[0:E + P, 0:D + 2], state, before, Linear([(agg, g.w_a), (g.x, g.w_s)], D),
                   take, after, table=(Linear([(g.x, g.w_p)], H), g.mlp_rows, g.bias[0:NP, 5:6, 0:H]),
                   sends=[(g.table, g.x)], place=g.fill_rows)


def mlp_edges(nc, g, a):
    GE = 5
    PER = T // GE
    GROUPS = SLOTS * PER
    with ExitStack() as stack:
        m = Pools(nc, stack, "edge_mlp")
        idx = m.sb("idx", [P, SLOTS, T], I32)
        rows = m.sb("rows", [P, SLOTS, T, H])
        first_rows, attr, x_dst = (m.sb(n, [P, SLOTS, T, D]) for n in ("first_rows", "attr", "x_dst"))
        value, running = m.sb("value", [P, 2, T, D]), m.sb("running", [P, SLOTS, T, D])
        in_t, hid = m.sb("in_t", [P, 2, 4, P]), m.sb("hid", [P, 2, GE * H])
        hid_t = m.sb("hid_t", [P, 2, 3, P])
        in_ps, hid_ps, hid_t_ps, val_ps = (m.ps(n, [P, 2, 512]) for n in ("in_ps", "hid_ps", "hid_t_ps", "val_ps"))
        idx_ready, gathered, scanned, stored = (m.sems(n) for n in ("idx_ready", "gathered", "scanned", "stored"))
        loaded, spread_ok = m.sems("loaded"), m.sems("spread_ok")
        (started, turned, turned_sb, product, summed, hid_turned, hid_turned_sb, valued, value_sb, first) = (
            m.sem(n) for n in ("started turned turned_sb product summed hid_turned hid_turned_sb valued value_sb "
                               "first").split())

        with nc.Block() as block:
            @block.sync
            def _(sp):
                places = by_partition(g.fill_rows[0:E, :])
                attrs = by_partition(a["edge_attr_32"])
                run_rows = by_partition(g.run[0:E, 0:D])

                def load(i, b, at):
                    sp.dma_start(first_rows[:, b], places[:, bass.ds(at, T), :]).then_inc(loaded[b], 16)
                    sp.dma_start(attr[:, b], attrs[:, bass.ds(at, T), :]).then_inc(loaded[b], 16)

                for b in range(SLOTS):
                    load(0, b, b * T)
                @repeat(sp, LOOPS - 1)
                def _(i):
                    for b in range(SLOTS):
                        wait(sp, scanned[b], i + 1)
                        sp.dma_start(run_rows[:, bass.ds(i * (SLOTS * T) + b * T, T), :],
                                     running[:, b]).then_inc(stored[b], 16)
                        load(i, b, (i + 1) * (SLOTS * T) + b * T)
                for b in range(SLOTS):
                    sp.wait_ge(scanned[b], LOOPS)
                    at = (LOOPS - 1) * SLOTS * T + b * T
                    sp.dma_start(run_rows[:, at:at + T, :], running[:, b]).then_inc(stored[b], 16)
                finish_stores(sp, stored, LOOPS)

            @block.gpsimd
            def _(pool):
                pool.indirect_dma_start(x_dst[:, SLOTS - 1, T - 1, :], None, g.table[:, 0:D],
                                        bass.IndirectOffsetOnAxis(ap=g.first_dst[:, 0:1], axis=0)).then_inc(first, 16)
                gather_rows(pool, g.mlp_rows, rows, idx, idx_ready, scanned, gathered, T, LOOPS)

            @block.scalar
            def _(act):
                for b in range(SLOTS):
                    stage_ahead(act, g, idx, idx_ready, T, 0, b)

                @repeat(act, LOOPS)
                def _(i):
                    n = i * GROUPS
                    for s in range(GROUPS + 3):
                        if s < GROUPS:
                            k = s % 2
                            wait(act, turned, n + s + 1)
                            wait(act, product, n + max(s - 1, 0))
                            act.activation(in_t[:, k, 0:2, :], in_ps[:, k, 0:2 * P].rearrange("p (c e) -> p c e", e=P),
                                           ACT.Copy)
                            act.activation(in_t[0:D, k, 2:4, :],
                                           in_ps[0:D, k, 2 * P:4 * P].rearrange("p (c e) -> p c e", e=P),
                                           ACT.Copy).then_inc(turned_sb, 1)
                        if 0 <= s - 2 < GROUPS:
                            u = s - 2
                            k = u % 2
                            wait(act, hid_turned, n + u + 1)
                            wait(act, valued, n + max(u - 1, 0))
                            act.activation(hid_t[:, k, 0:2, :], hid_t_ps[:, k, 0:2 * P].rearrange("p (c e) -> p c e", e=P),
                                           ACT.Relu)
                            act.activation(hid_t[0:H, k, 2, :], hid_t_ps[0:H, k, 2 * P:3 * P],
                                           ACT.Relu).then_inc(hid_turned_sb, 1)
                            if u % PER == 0:
                                wait(act, gathered[u // PER], (i + 1) * (16 * T))
                                stage_ahead(act, g, idx, idx_ready, T, i + 1, u // PER)
                        if 0 <= s - 3 < GROUPS:
                            u = s - 3
                            b, c = u // PER, u % PER
                            wait(act, valued, n + u + 1)
                            if c == 0 and b >= 2:
                                wait(act, scanned[b - 2], i + 1)
                            elif c == 0:
                                wait(act, scanned[SLOTS - 1], i)
                            act.activation(value[:, b % 2, c * GE:c * GE + GE, :],
                                           val_ps[:, u % 2, 0:GE * D].rearrange("p (t f) -> p t f", f=D),
                                           ACT.Copy).then_inc(value_sb, 1)

            @block.tensor
            def _(pe):
                @repeat(pe, LOOPS)
                def _(i):
                    n = i * GROUPS

                    def turn(s):
                        b, at, k = s // PER, s % PER * GE, s % 2
                        if s % PER == 0:
                            wait(pe, loaded[b], (i + 1) * 32)
                            wait(pe, spread_ok[b], i + 1)
                        wait(pe, turned_sb, n + max(s - 1, 0))
                        for c, (tile, lo, hi) in enumerate(((attr, 0, 4), (x_dst, 0, 4), (attr, 4, 5), (x_dst, 4, 5))):
                            last = pe.transpose(in_ps[0:(hi - lo) * D, k, c * P:c * P + P],
                                                tile[:, b, at + lo:at + hi, :].rearrange("p t f -> p (t f)"), g.ident[:, :])
                        last.then_inc(turned, 1)

                    def first_product(s):
                        k = s % 2
                        wait(pe, turned_sb, n + s + 1)
                        wait(pe, summed, n + max(s - 1, 0))
                        for lanes, t, c in ((slice(0, P), 0, 0), (slice(0, D), 4, 2)):
                            out = hid_ps[:, k, t * H:(t + 4) * H] if t == 0 else hid_ps[:, k, t * H:t * H + H]
                            wide = slice(0, 4 if t == 0 else 1)
                            pe.matmul(out, in_t[lanes, k, c, :], g.w_e[lanes, wide, :], start=True, stop=False)
                            last = pe.matmul(out, in_t[lanes, k, c + 1, :], g.w_d[lanes, wide, :],
                                             start=False, stop=True)
                        last.then_inc(product, 1)

                    def turn_hidden(s):
                        k = s % 2
                        wait(pe, summed, n + s + 1)
                        wait(pe, hid_turned_sb, n + max(s - 1, 0))
                        for c in range(3):
                            w = 2 * H if c < 2 else H
                            last = pe.transpose(hid_t_ps[0:w, k, c * P:c * P + P], hid[:, k, c * 2 * H:c * 2 * H + w],
                                                g.ident[:, :])
                        last.then_inc(hid_turned, 1)

                    def second_product(s):
                        k = s % 2
                        wait(pe, hid_turned_sb, n + s + 1)
                        wait(pe, value_sb, n + max(s - 1, 0))
                        for c in range(3):
                            lanes, wide = (slice(0, P), slice(0, 2)) if c < 2 else (slice(0, H), slice(0, 1))
                            at = 2 * c * D
                            last = pe.matmul(val_ps[:, k, at:at + (2 * D if c < 2 else D)], hid_t[lanes, k, c, :],
                                             g.w_v[lanes, wide, :], start=True, stop=True)
                        last.then_inc(valued, 1)

                    for s in range(GROUPS + 3):
                        for lag, stage in enumerate((turn, first_product, turn_hidden, second_product)):
                            if 0 <= s - lag < GROUPS:
                                stage(s - lag)

            @block.vector
            def _(dve):
                dve.memset(running[:, SLOTS - 1, T - 1, :], -BIG).then_inc(started, 1)
                dve.wait_ge(started, 1)
                dve.wait_ge(first, 16)
                @repeat(dve, LOOPS)
                def _(i):
                    n = i * GROUPS

                    def spread_rows(b):
                        at, before = i * (SLOTS * T) + b * T, (b - 1) % SLOTS
                        wait(dve, loaded[b], (i + 1) * 32)
                        wait(dve, spread_ok[before], i + 1 if b else i)
                        for f in range(D):
                            last = dve.tensor_tensor_scan(
                                x_dst[:, b, :, f], g.keep[:, bass.ds(at, T)], first_rows[:, b, :, f],
                                x_dst[:, before, T - 1, f:f + 1], ALU.mult, ALU.add)
                        last.then_inc(spread_ok[b], 1)

                    def add_source(s):
                        b, at, k = s // PER, s % PER * GE, s % 2
                        if s % PER == 0:
                            wait(dve, gathered[b], (i + 1) * (16 * T))
                        wait(dve, product, n + s + 1)
                        wait(dve, hid_turned, n + max(s - 1, 0))
                        dve.tensor_tensor(hid[:, k, :], hid_ps[:, k, 0:GE * H],
                                          rows[:, b, at:at + GE, :].rearrange("p t f -> p (t f)"),
                                          ALU.add).then_inc(summed, 1)

                    def maximum(b):
                        at, before = i * (SLOTS * T) + b * T, (b - 1) % SLOTS
                        wait(dve, value_sb, n + (b + 1) * PER)
                        wait(dve, stored[b], i * 16)
                        wait(dve, scanned[before], i + 1 if b else i)
                        for f in range(D):
                            last = dve.tensor_tensor_scan(
                                running[:, b, :, f], g.pen[:, bass.ds(at, T)], value[:, b % 2, :, f],
                                running[:, before, T - 1, f:f + 1], ALU.add, ALU.max)
                        last.then_inc(scanned[b], 1)

                    spread_rows(0)
                    for s in range(GROUPS + 5):
                        if s % PER == 0 and s // PER + 1 < SLOTS:
                            spread_rows(s // PER + 1)
                        if 0 <= s - 1 < GROUPS:
                            add_source(s - 1)
                        if 0 <= s - 5 < GROUPS and (s - 5) % PER == PER - 1:
                            maximum((s - 5) // PER)
                dve.wait_ge(scanned[SLOTS - 1], LOOPS)
                dve.tensor_copy(g.tail[:, 0:D], running[:, SLOTS - 1, T - 1, :])


def mlp_nodes(nc, g, out):
    with ExitStack() as stack:
        m = Pools(nc, stack, "mlp_n")
        top = m.sb("top", [NP, NJ, D])
        wide = [NP, CJ, D]
        carry(nc, g, "max", g.run, g.tail)

        def before(dve, chain, cols, made):
            chain(dve.tensor_tensor(top[:, cols, :], top[:, cols, :], spread(g.mask[:, cols, None], wide), ALU.mult))
            chain(dve.tensor_tensor(top[:, cols, :], top[:, cols, :], spread(g.pen_node[:, cols, None], wide), ALU.add))
            chain(dve.tensor_tensor(top[:, cols, :], top[:, cols, :], spread(g.bias[0:NP, 4:5, 0:D], wide), ALU.add))

        def after(dve, chain, cols):
            chain(dve.tensor_tensor(top[:, cols, :], top[:, cols, :], g.x[:, cols, :], ALU.max))
            chain(dve.tensor_tensor(g.x[:, cols, :], g.x[:, cols, :], top[:, cols, :], ALU.add))

        node_phase(nc, g, "mlp_node", g.run[0:E + P, 0:D], top, before, None, None, after, sends=[(out, g.x)])


class Globals:
    pass


def graph_layers(nc, a, out, stop=99):
    g = Globals()
    g.phase = 0
    Pools.live.clear()
    with ExitStack() as stack:
        m = Pools(nc, stack, "g")
        g.src = m.sb("src", [P, EPP + SLOTS * T], I32)
        g.keep, g.pen = m.sb("keep", [P, EPP]), m.sb("pen", [P, EPP])
        g.ident = m.sb("ident", [P, P])
        g.x = m.sb("x", [NP, NJ, D])
        g.rooted = m.sb("rooted", [NP, NJ, D])
        g.end_idx, g.start_idx, g.node_id = (m.sb(n, [NP, NJ], I32) for n in ("end_idx", "start_idx", "node_id"))
        g.mask, g.pen_node, g.deg = (m.sb(n, [NP, NJ]) for n in ("mask", "pen_node", "deg"))
        g.norm_src = m.sb("norm_src", [NP, NJ])
        g.stat = m.sb("stat", [NP, 2, NJ])
        g.head_idx, g.first_dst, g.iota_e = (m.sb(n, [P, 1], I32) for n in ("head_idx", "first_dst", "iota_e"))
        g.keep_row, g.pen_row = m.sb("keep_row", [D + 2, P]), m.sb("pen_row", [D + 2, P])
        g.tail = m.sb("tail", [P, D + 2])
        g.zeros = m.sb("zeros", [P, D + 2])
        g.score_w = m.sb("score_w", [P, D])
        g.bias = m.sb("bias", [P, 6, H])
        g.wg, g.w_s, g.w_a = (m.sb(n, [P, GJ, D]) for n in ("wg", "w_s", "w_a"))
        g.w_p, g.w_d, g.w_e = (m.sb(n, [P, GJ, H]) for n in ("w_p", "w_d", "w_e"))
        g.w_v = m.sb("w_v", [P, 2, D])
        g.w_y = m.sb("w_y", [P, GJ, (K1 + 1) * D])
        dram = lambda name, shape: nc.dram_tensor(name, shape, F32, kind="Internal").ap()
        g.table = dram("node_rows", (N, D))
        g.spline_rows = dram("spline_rows", (N, K1 * D))
        g.att_rows = dram("att_rows", (N, D + 1))
        g.mlp_rows = dram("mlp_rows", (N, H))
        g.fill_rows = dram("fill_rows", (E + N, D))
        runs = {w: dram(f"run{w}", (E + P, w)) for w in (D, D + 2)}
        with ExitStack() as first:
            f = Pools(nc, first, "f")
            g.h0 = f.sb("h0", [NP, NJ, D])
            g.m0 = g.rooted
            g.high, g.low = f.sb("high", [P, EPP], BF16), f.sb("low", [P, EPP], BF16)
            g.dst_i, g.dst_f = f.sb("dst_i", [P, EPP + 1], I32), f.sb("dst_f", [P, EPP + 1])
            g.next_i, g.spare_row = f.sb("next_i", [P, 1], I32), f.sb("spare_row", [P, 1], I32)
            g.steps = f.sb("steps", [P, NP, T], BF16)
            g.run = runs[D]
            prepare(nc, g, a, list(runs.values()))
            gcn_edges(nc, g)
            gcn_nodes(nc, g)
        clear_semaphores(nc)
        if stop > 1:
            spline_edges(nc, g, a)
            spline_nodes(nc, g)
        if stop > 2:
            g.run = runs[D + 2]
            attention_edges(nc, g)
            attention_nodes(nc, g)
        clear_semaphores(nc)
        if stop > 3:
            g.run = runs[D]
            mlp_edges(nc, g, a)
            mlp_nodes(nc, g, out)
        else:
            write_rows(nc, "result", [(out, g.x[:, :, :])])


_INS = ['x', 'src', 'dst', 'edge_attr_2', 'edge_attr_32', 'L0_gnn_W1', 'L0_gnn_b1', 'L0_gnn_W2', 'L0_gnn_b2',
        'L0_gnn_Wg', 'L0_gnn_bg', 'L1_gnn_weight', 'L1_gnn_root_w', 'L1_gnn_root_b', 'L2_gnn_w1_W', 'L2_gnn_w1_b',
        'L2_gnn_w2_W', 'L2_gnn_w2_b', 'L2_gnn_a', 'L3_gnn_W1', 'L3_gnn_b1', 'L3_gnn_W2', 'L3_gnn_b2']


def kernel(**inputs):
    import numpy as _np
    import concourse.bacc as _bacc
    from concourse.bass_utils import run_bass_kernel_spmd as _run

    nc = _bacc.Bacc("TRN2", target_bir_lowering=False, num_devices=1)
    arrays, aps = {}, {}
    for name in _INS:
        v = _np.ascontiguousarray(inputs[name])
        arrays[f"in_{name}"] = v
        aps[name] = nc.dram_tensor(f"in_{name}", v.shape, mybir.dt.from_np(v.dtype), kind="ExternalInput").ap()
    out = nc.dram_tensor("out_x", (N, D), F32, kind="ExternalOutput").ap()
    graph_layers(nc, aps, out)
    r = _run(nc, [arrays], core_ids=[0])
    return r.results[0]["out_x"]
```

```python
from contextlib import ExitStack

import concourse.bass as bass
from concourse import mybir

F32 = mybir.dt.float32
I32 = mybir.dt.int32
BF16 = mybir.dt.bfloat16
ALU = mybir.AluOpType
ACT = mybir.ActivationFunctionType
AX = mybir.AxisListType

N, E, D, H = 12500, 400000, 32, 64
P = 128
EPP = E // P
NP, NJ = 125, 100
T = 25
SLOTS = 5
LOOPS = EPP // (T * SLOTS)
T1 = 5
LOOPS1 = EPP // (T1 * SLOTS)
K1 = 9
HOT_PREP, HOT_GCN = 5, 2
GJ = 4
EARLY = 12
AT_EARLY = (SLOTS - 1) * T
LANES = 4
ENC = 5
CHUNKS = 5
CJ = NJ // CHUNKS
ROOT_AT = 2
GROUPS = CJ // GJ
BIG = 1e38
MAGIC = 12582912.0
EPS = 1e-5


def repeat(eng, count, start=0):
    def build(body):
        if start == 0:
            body(0)
        with eng.Fori(max(start, 1), count) as i:
            body(i)
    return build


def wait(eng, sem, value):
    if not isinstance(value, int) or value > 0:
        eng.wait_ge(sem, value)


def nth_use(i, b, ring):
    k = b % ring
    return k, i * len(range(k, SLOTS, ring)) + b // ring


class Chain:

    def __init__(self, eng, sem):
        self.eng, self.sem, self.n, self.base = eng, sem, 0, None

    def __call__(self, ins):
        ins.then_inc(self.sem, 1)
        self.n += 1
        self.eng.wait_ge(self.sem, self.n if self.base is None else self.base + self.n)

    def loop(self, i, per_iteration):
        if self.base is None:
            self.start = self.n
        self.n, self.per = 0, per_iteration
        self.base = i * per_iteration + self.start

    def end_loop(self, iterations):
        assert self.n == self.per, (self.n, self.per)
        self.n, self.base = self.start + iterations * self.per, None


class Pools:

    live = []

    def __init__(self, nc, stack, tag):
        self.nc, self.stack, self.tag = nc, stack, tag

    def sb(self, name, shape, dt=F32):
        return self.stack.enter_context(self.nc.sbuf_tensor(f"{self.tag}_{name}", shape, dt))

    def ps(self, name, shape):
        return self.stack.enter_context(self.nc.psum_tensor(f"{self.tag}_{name}", shape, F32))

    def sem(self, name):
        self.live.append(self.nc.alloc_semaphore(name=f"{self.tag}_{name}"))
        return self.live[-1]

    def sems(self, name, n=SLOTS):
        return [self.sem(f"{name}{k}") for k in range(n)]


def clear_semaphores(nc):
    nc.clear_and_free_semaphores(Pools.live)
    nc.all_engine_barrier()
    Pools.live.clear()


def by_partition(ap, parts=P):
    return ap.rearrange("(p t) f -> p t f", p=parts)


def spread(ap, shape):
    return ap.to_broadcast(shape)




def stage_indices(act, src, idx, idx_ready, gathered, tiles, loops):
    @repeat(act, loops)
    def _(i):
        for b in range(SLOTS):
            wait(act, gathered[b], i * (16 * tiles))
            act.activation(idx[:, b, :], src[:, bass.ds(i * (SLOTS * tiles) + b * tiles, tiles)],
                           ACT.Copy).then_inc(idx_ready[b], 1)


def stage_ahead(act, g, idx, idx_ready, tiles, i, b):
    act.activation(idx[:, b, :], g.src[:, bass.ds(i * (SLOTS * tiles) + b * tiles, tiles)],
                   ACT.Copy).then_inc(idx_ready[b], 1)


def gather_rows(pool, table, rows, idx, idx_ready, slot_free, gathered, tiles, loops, early=0):
    @repeat(pool, loops)
    def _(i):
        for b in range(SLOTS):
            wait(pool, idx_ready[b], i + 1)
            pool.nop(nofuse=True)
            wait(pool, slot_free[b], i)
            pool.nop(nofuse=True)
            for t in range(early if b == SLOTS - 1 else 0, tiles):
                pool.indirect_dma_start(
                    rows[:, b, t, :], None, table, bass.IndirectOffsetOnAxis(ap=idx[:, b, t:t + 1], axis=0)
                ).then_inc(gathered[b], 16)


def store_running(sp, running, run_rows, scanned, stored, loops):
    @repeat(sp, loops)
    def _(i):
        for b in range(SLOTS):
            wait(sp, scanned[b], i + 1)
            sp.dma_start(run_rows[:, bass.ds(i * (SLOTS * T) + b * T, T), :], running[:, b]).then_inc(stored[b], 16)


def finish_stores(sp, stored, loops):
    for b in range(SLOTS):
        sp.wait_ge(stored[b], 16 * loops)


def layer_norm(dve, chain, g, cols, tmp, var_ok, std_ok, n, done):
    wide = [NP, CJ, D]
    x, mean, var = g.x[:, cols, :], g.stat[:, 0, cols], g.stat[:, 1, cols]
    chain(dve.tensor_reduce(mean, x, AX.X, ALU.add))
    chain(dve.tensor_scalar(mean, mean, 1.0 / D, None, ALU.mult))
    chain(dve.tensor_tensor(x, x, spread(g.stat[:, 0, cols, None], wide), ALU.subtract))
    chain(dve.tensor_tensor(tmp[:, cols, 0:D], x, x, ALU.mult))
    chain(dve.tensor_reduce(var, tmp[:, cols, 0:D], AX.X, ALU.add))
    dve.tensor_scalar(var, var, 1.0 / D, EPS, ALU.mult, ALU.add).then_inc(var_ok, 1)
    dve.wait_ge(std_ok, n + 1)
    chain(dve.reciprocal(var, var))
    dve.tensor_tensor(x, x, spread(g.stat[:, 1, cols, None], wide), ALU.mult).then_inc(done, 1)


class Linear:

    def __init__(self, terms, width):
        self.terms, self.width, self.wide = terms, width, width * GJ > 512


def node_phase(nc, g, tag, run_rows, rows, before, linear, take, after, finish=None, table=None, sends=(),
               root_first=None, place=None):
    with ExitStack() as stack:
        m = Pools(nc, stack, tag)
        fetched, row_sent = m.sems("fetched", CHUNKS), m.sems("row_sent", 2)
        (link, made, var_ok, std_ok, normed, finished, staged, turned_ps, turned_sb, product, taken, taken_act,
         sent, root_in, root, placed, half, half_taken) = (m.sem(n) for n in (
             "link made var_ok std_ok normed finished staged turned_ps turned_sb product taken taken_act "
             "sent root_in root placed half half_taken").split())
        kinds = [k for k in (linear, table and table[0]) if k]
        nt = max([len(k.terms) for k in kinds], default=1)
        if kinds:
            stage, turned = m.sb("stage", [NP, 2, nt, GJ * D]), m.sb("turned", [P, 2, nt, NP])
            turn_ps, small_ps = m.ps("turn_ps", [P, 2, 512]), m.ps("small_ps", [NP, 2, 512])
        if table:
            row_stage = m.sb("row_stage", [NP, 2, GJ, table[1].shape[1]])
        if table and table[0].wide:
            wide_ps = m.ps("wide_ps", [NP, GJ, 512])
        turns = []
        for c in range(CHUNKS):
            turns += [(c, linear)] if linear else []
            turns += [(c - 1, table[0])] if table and c else []
        turns += [(CHUNKS - 1, table[0])] if table else []
        jobs = [(c, k, u) for c, k in turns for u in range(GROUPS)]

        def batch(c, kind):
            return [n for n, (c_, k, _) in enumerate(jobs) if c_ == c and k is kind]

        def cols_of(n):
            c, _, u = jobs[n]
            return slice(c * CJ + u * GJ, c * CJ + (u + 1) * GJ)

        def before_of(n, wide):
            return sum(1 for _, k, _ in jobs[:n] if k.wide == wide)

        def result(n):
            k = jobs[n][1]
            if k.wide:
                return wide_ps[:, :, 0:k.width]
            return small_ps[:, before_of(n, False) % 2, 0:GJ * k.width].rearrange("p (q w) -> p q w", q=GJ)

        def table_number(n):
            return sum(1 for _, k, _ in jobs[:n] if table and k is table[0])

        with nc.Block() as block:
            @block.gpsimd
            def _(pool):
                for c in range(CHUNKS):
                    for j in range(c * CJ, (c + 1) * CJ):
                        pool.indirect_dma_start(rows[:, j, :], None, run_rows, bass.IndirectOffsetOnAxis(
                            ap=g.end_idx[:, j:j + 1], axis=0)).then_inc(fetched[c], 16)
                if place is not None:
                    for c in range(CHUNKS):
                        pool.wait_ge(normed, c + 1)
                        for j in range(c * CJ, (c + 1) * CJ):
                            pool.indirect_dma_start(
                                place, bass.IndirectOffsetOnAxis(ap=g.start_idx[:, j:j + 1], axis=0),
                                g.x[:, j, :], None).then_inc(placed, 16)
                    pool.wait_ge(placed, 16 * NJ)

            @block.scalar
            def _(act):
                if root_first:
                    act.wait_ge(root_in, 1)
                    act.activation(root_first, root_first, ACT.Sqrt).then_inc(root, 1)

                def put(n):
                    act.wait_ge(turned_ps, n - 1) if n > 1 else None
                    for k, (tile, _) in enumerate(jobs[n][1].terms):
                        last = act.activation(stage[:, n % 2, k, :].rearrange("p (j f) -> p j f", f=D),
                                              tile[:, cols_of(n), :], ACT.Copy)
                    last.then_inc(staged, 1)

                def take_wide(n):
                    b, at = table_number(n), cols_of(n).start
                    if b >= 2:
                        act.wait_ge(row_sent[b % 2], 16 * (b // 2))
                    for q, ready, count, free in ((0, half, b, half_taken), (2, product, n, taken_act)):
                        act.wait_ge(ready, count + 1)
                        act.activation(row_stage[:, b % 2, q:q + 2, :], wide_ps[:, q:q + 2, 0:K1 * D], ACT.Copy)
                        act.activation(g.rooted[:, at + q:at + q + 2, :], wide_ps[:, q:q + 2, K1 * D:K1 * D + D],
                                       ACT.Copy).then_inc(free, 1)

                def root_of(c):
                    act.wait_ge(var_ok, c + 1)
                    cols = slice(c * CJ, (c + 1) * CJ)
                    act.activation(g.stat[:, 1, cols], g.stat[:, 1, cols], ACT.Sqrt).then_inc(std_ok, 1)

                def turn_rows(c, kind, root_after=None):
                    ns = batch(c, kind)
                    put(ns[0])
                    for n in ns:
                        if root_after is not None and n == ns[ROOT_AT]:
                            root_of(root_after)
                        if n + 1 in ns:
                            put(n + 1)
                        act.wait_ge(turned_ps, n + 1)
                        act.wait_ge(product, n - 1) if n > 1 else None
                        k = len(kind.terms)
                        act.activation(turned[:, n % 2, 0:k, :],
                                       turn_ps[:, n % 2, 0:k * NP].rearrange("p (k n) -> p k n", n=NP),
                                       ACT.Copy).then_inc(turned_sb, 1)
                        if kind.wide and n > ns[0]:
                            take_wide(n - 1)
                    if kind.wide:
                        take_wide(ns[-1])

                for c in range(CHUNKS):
                    if linear:
                        act.wait_ge(made, c + 1)
                        turn_rows(c, linear)
                    if table and table[0].wide and c:
                        act.wait_ge(normed, c)
                        turn_rows(c - 1, table[0], root_after=c)
                        continue
                    root_of(c)
                    if table and c:
                        act.wait_ge(normed, c)
                        turn_rows(c - 1, table[0])
                if table:
                    act.wait_ge(normed, CHUNKS)
                    turn_rows(CHUNKS - 1, table[0])

            @block.tensor
            def _(pe):
                def turn(n):
                    pe.wait_ge(staged, n + 1)
                    pe.wait_ge(turned_sb, n - 1) if n > 1 else None
                    for k in range(len(jobs[n][1].terms)):
                        last = pe.transpose(turn_ps[:, n % 2, k * NP:(k + 1) * NP], stage[:, n % 2, k, :],
                                            g.ident[0:NP, 0:NP])
                    last.then_inc(turned_ps, 1)

                for c, kind in turns:
                    ns = batch(c, kind)
                    turn(ns[0])
                    for n in ns:
                        if n + 1 in ns:
                            turn(n + 1)
                        pe.wait_ge(turned_sb, n + 1)
                        b = before_of(n, kind.wide)
                        last_term = len(kind.terms) - 1
                        if kind.wide:
                            for q in range(GJ):
                                if b and q == 0:
                                    pe.wait_ge(half_taken, b)
                                if b and q == 2:
                                    pe.wait_ge(taken_act, b)
                                lanes = slice(D * q, D * q + D)
                                for k, (_, w) in enumerate(kind.terms):
                                    last = pe.matmul(wide_ps[:, q, 0:kind.width], turned[lanes, n % 2, k, :],
                                                     w[lanes, q, :], start=(k == 0), stop=(k == last_term))
                                if q == 1:
                                    last.then_inc(half, 1)
                        else:
                            if b >= 2:
                                pe.wait_ge(taken, b - 1)
                            for k, (_, w) in enumerate(kind.terms):
                                last = pe.matmul(result(n), turned[:, n % 2, k, :], w[:, :, :],
                                                 start=(k == 0), stop=(k == last_term))
                        last.then_inc(product, 1)

            @block.vector
            def _(dve):
                chain = Chain(dve, link)
                if root_first:
                    dve.tensor_scalar(root_first, g.deg[:, :], 1.0, None, ALU.add).then_inc(root_in, 1)
                    dve.wait_ge(root, 1)
                    chain(dve.reciprocal(root_first, root_first))

                def tables(c):
                    if table[0].wide:
                        return
                    for n in batch(c, table[0]):
                        b = table_number(n)
                        dve.wait_ge(product, n + 1)
                        if b >= 2:
                            dve.wait_ge(row_sent[b % 2], 16 * (b // 2))
                        dve.tensor_tensor(row_stage[:, b % 2], result(n),
                                          spread(table[2], [NP, GJ, table[0].width]), ALU.add).then_inc(taken, 1)

                for c in range(CHUNKS):
                    cols = slice(c * CJ, (c + 1) * CJ)
                    dve.wait_ge(fetched[c], 16 * CJ)
                    before(dve, chain, cols, made)
                    if linear:
                        for n in batch(c, linear):
                            dve.wait_ge(product, n + 1)
                            take(dve, result(n), cols_of(n)).then_inc(taken, 1)
                        dve.wait_ge(taken, before_of(batch(c, linear)[-1], False) + 1)
                    after(dve, chain, cols)
                    layer_norm(dve, chain, g, cols, rows, var_ok, std_ok, c, normed)
                    if finish:
                        dve.wait_ge(normed, c + 1)
                        finish(dve, chain, cols).then_inc(finished, 1)
                    if table and c:
                        tables(c - 1)
                if table:
                    tables(CHUNKS - 1)

            @block.sync
            def _(sp):
                def tables(c):
                    for n in batch(c, table[0]):
                        b = table_number(n)
                        if table[0].wide:
                            sp.wait_ge(half_taken, b + 1)
                            sp.wait_ge(taken_act, b + 1)
                        else:
                            sp.wait_ge(taken, n + 1)
                        sp.dma_start(by_partition(table[1], NP)[:, cols_of(n), :],
                                     row_stage[:, b % 2]).then_inc(row_sent[b % 2], 16)

                for c in range(CHUNKS):
                    cols = slice(c * CJ, (c + 1) * CJ)
                    if sends:
                        sp.wait_ge(finished if finish else normed, c + 1)
                    for dram, tile in sends:
                        sp.dma_start(by_partition(dram, NP)[:, cols, :], tile[:, cols, :]).then_inc(sent, 16)
                    if table:
                        tables(c - 1) if c else None
                if table:
                    tables(CHUNKS - 1)
                if sends:
                    sp.wait_ge(sent, 16 * CHUNKS * len(sends))
                if table:
                    total = CHUNKS * GROUPS
                    sp.wait_ge(row_sent[0], 16 * ((total + 1) // 2))
                    sp.wait_ge(row_sent[1], 16 * (total // 2))


def carry(nc, g, kind, run_dram, tail):
    w = {"sum": D, "max": D, "softmax": D + 2}[kind]
    r = {"sum": D, "max": D, "softmax": D + 1}[kind]
    with ExitStack() as stack:
        m = Pools(nc, stack, f"carry{g.phase}")
        g.phase += 1
        ps = m.ps("ps", [P, 4, 512])
        tail_t, state = m.sb("tail_t", [r, P]), m.sb("state", [r, P + 1])
        head = m.sb("head", [P, w])
        tail_max, max_t = m.sb("tail_max", [P, r]), m.sb("max_t", [r, P])
        max_state, drift = m.sb("max_state", [r, P + 1]), m.sb("drift", [r, 2, P])
        new_max, fade = m.sb("new_max", [P, 1]), m.sb("fade", [P, 2])
        turned, scanned, back, exp_in, exp_out = (
            m.sem(x) for x in ("turned", "scanned", "back", "exp_in", "exp_out"))
        prepared, head_in, head_ok, head_out, link = (
            m.sem(x) for x in ("prepared", "head_in", "head_ok", "head_out", "link"))
        soft = kind == "softmax"

        with nc.Block() as block:
            @block.tensor
            def _(pe):
                if soft:
                    pe.wait_ge(prepared, 1)
                    pe.transpose(ps[0:r, 1, 0:P], tail_max[:, :], g.ident[:, :])
                pe.transpose(ps[0:r, 0, 0:P], tail[:, 0:r], g.ident[:, :]).then_inc(turned, 1)
                pe.wait_ge(scanned, 1)
                if soft:
                    pe.transpose(ps[:, 3, 0:r], max_state[:, 0:P], g.ident[0:r, 0:r])
                pe.transpose(ps[:, 2, 0:r], state[:, 0:P], g.ident[0:r, 0:r]).then_inc(back, 1)

            @block.scalar
            def _(act):
                if soft:
                    act.wait_ge(exp_in, 1)
                    act.activation(drift[:, :, :], drift[:, :, :], ACT.Exp).then_inc(exp_out, 1)
                    act.wait_ge(exp_in, 2)
                    act.activation(fade[:, :], fade[:, :], ACT.Exp).then_inc(exp_out, 1)

            @block.vector
            def _(dve):
                chain = Chain(dve, link)
                chain(dve.memset(state[:, 0:1], -BIG if kind == "max" else 0.0))
                if soft:
                    chain(dve.memset(max_state[:, 0:1], -BIG))
                    dve.tensor_copy(tail_max[:, :], spread(tail[:, D + 1:D + 2], [P, r])).then_inc(prepared, 1)
                dve.wait_ge(turned, 1)
                chain(dve.tensor_copy(tail_t[:, :], ps[0:r, 0, 0:P]))
                if kind == "sum":
                    dve.tensor_tensor_scan(state[:, 1:P + 1], g.keep_row[0:r, :], tail_t[:, :], 0.0,
                                           ALU.mult, ALU.add).then_inc(scanned, 1)
                elif kind == "max":
                    dve.tensor_tensor_scan(state[:, 1:P + 1], g.pen_row[0:r, :], tail_t[:, :], -BIG,
                                           ALU.add, ALU.max).then_inc(scanned, 1)
                else:
                    chain(dve.tensor_copy(max_t[:, :], ps[0:r, 1, 0:P]))
                    chain(dve.tensor_tensor_scan(max_state[:, 1:P + 1], g.pen_row[0:r, :], max_t[:, :], -BIG,
                                                 ALU.add, ALU.max))
                    chain(dve.tensor_tensor(drift[:, 0, :], max_state[:, 0:P], g.pen_row[0:r, :], ALU.add))
                    chain(dve.tensor_tensor(drift[:, 0, :], drift[:, 0, :], max_state[:, 1:P + 1], ALU.subtract))
                    dve.tensor_tensor(drift[:, 1, :], max_t[:, :], max_state[:, 1:P + 1],
                                      ALU.subtract).then_inc(exp_in, 1)
                    dve.wait_ge(exp_out, 1)
                    chain(dve.tensor_tensor(tail_t[:, :], tail_t[:, :], drift[:, 1, :], ALU.mult))
                    dve.tensor_tensor_scan(state[:, 1:P + 1], drift[:, 0, :], tail_t[:, :], 0.0,
                                           ALU.mult, ALU.add).then_inc(scanned, 1)
                dve.wait_ge(back, 1)
                dve.wait_ge(head_in, 16)
                if kind == "sum":
                    dve.tensor_tensor(head[:, :], head[:, :], ps[:, 2, 0:r], ALU.add).then_inc(head_ok, 1)
                elif kind == "max":
                    dve.tensor_tensor(head[:, :], head[:, :], ps[:, 2, 0:r], ALU.max).then_inc(head_ok, 1)
                else:
                    chain(dve.tensor_tensor(new_max[:, :], head[:, D + 1:D + 2], ps[:, 3, 0:1], ALU.max))
                    chain(dve.tensor_tensor(fade[:, 0:1], head[:, D + 1:D + 2], new_max[:, :], ALU.subtract))
                    dve.tensor_tensor(fade[:, 1:2], ps[:, 3, 0:1], new_max[:, :], ALU.subtract).then_inc(exp_in, 1)
                    dve.wait_ge(exp_out, 2)
                    chain(dve.tensor_scalar(head[:, 0:r], head[:, 0:r], fade[:, 0:1], None, ALU.mult))
                    chain(dve.tensor_copy(head[:, D + 1:D + 2], new_max[:, :]))
                    dve.scalar_tensor_tensor(head[:, 0:r], ps[:, 2, 0:r], fade[:, 1:2], head[:, 0:r],
                                             ALU.mult, ALU.add).then_inc(head_ok, 1)

            @block.gpsimd
            def _(pool):
                rows = run_dram[0:E + P, 0:w]
                pool.indirect_dma_start(head[:, :], None, rows, bass.IndirectOffsetOnAxis(
                    ap=g.head_idx[:, 0:1], axis=0)).then_inc(head_in, 16)
                pool.wait_ge(head_ok, 1)
                pool.indirect_dma_start(rows, bass.IndirectOffsetOnAxis(ap=g.head_idx[:, 0:1], axis=0),
                                        head[:, :], None).then_inc(head_out, 16)
                pool.wait_ge(head_out, 16)




def digits(dve, chain, ids, high, low, scratch):
    chain(dve.tensor_scalar(scratch[:, :], ids, 0.5, 1.0 / NJ, ALU.add, ALU.mult))
    chain(dve.tensor_scalar(scratch[:, :], scratch[:, :], -0.5, MAGIC, ALU.add, ALU.add))
    chain(dve.tensor_scalar(high[:, :], scratch[:, :], -MAGIC, None, ALU.add))
    chain(dve.scalar_tensor_tensor(low[:, :], high[:, :], -float(NJ), ids, ALU.mult, ALU.add))


def mark(dve, hot, b, steps, high, low, at):
    dve.tensor_tensor(hot[:, b, 0:NP, :], steps[:, :, :],
                      spread(high[:, None, bass.ds(at, T)], [P, NP, T]), ALU.is_equal)
    return dve.tensor_tensor(hot[:, b, NP:NP + NJ, :], steps[:, 0:NJ, :],
                             spread(low[:, None, bass.ds(at, T)], [P, NJ, T]), ALU.is_equal)


def count(pe, counts, hot, b):
    for t in range(T):
        last = pe.matmul(counts, hot[:, b, 0:NP, t], hot[:, b, NP:NP + NJ, t], start=False, stop=False,
                         skip_group_check=True)
    return last




def prepare(nc, g, a, spare):
    with ExitStack() as stack:
        m = Pools(nc, stack, "prep")
        dst_i, next_i = g.dst_i, g.next_i
        hot = m.sb("hot", [P, HOT_PREP, NP + NJ, T], BF16)
        nothing = m.sb("nothing", [P, NP], BF16)
        step_i, step_f = m.sb("step_i", [P, NP], I32), m.sb("step_f", [P, NP])
        w1, w2b, b1 = m.sb("w1", [P, GJ, H]), m.sb("w2b", [H + 1, D]), m.sb("b1", [H, 1])
        avec, w2l2 = m.sb("avec", [D, 1]), m.sb("w2l2", [D, D])
        acol = m.sb("acol", [D, P])
        stage, turned, hid = m.sb("stage", [NP, 2, GJ * D]), m.sb("turned", [P, 2, NP]), m.sb("hid", [H + 1, 2, GJ * NP])
        early_idx, early = m.sb("early_idx", [P, 2, EARLY // 2], I32), m.sb("early", [P, 2, EARLY // 2, D])
        counts, small_ps = m.ps("counts", [NP, 512]), m.ps("small_ps", [P, 512])
        turn_ps, hid_ps, h0_ps = (m.ps(n, [P, 2, 512]) for n in ("turn_ps", "hid_ps", "h0_ps"))
        names = ("src_in dst_in border x_in enc_in w_in filled link consts hid_one nothing_ok staged turned_ps "
                 "turned_sb hid_ready hid_sb h0_ready h0_out counted trash_ok rows_ok rows_ps ab_ok ab_ps root root_in "
                 "zero_out ident_zero score_sb weights_zero table_ok table_out encoded").split()
        s = {n: m.sem(n) for n in names}
        marked, used = m.sems("marked", HOT_PREP), m.sems("used", HOT_PREP)
        early_ready, early_in, early_out = (m.sems(n, 2) for n in ("early_ready", "early_in", "early_out"))

        across = [(q, slice(D * q, D * q + D)) for q in range(GJ)]
        encoder = [(w1[r, q, :], a["L0_gnn_W1"]) for q, r in across]
        encoder += [(w2b[0:H, :], a["L0_gnn_W2"]), (w2b[H:H + 1, :], a["L0_gnn_b2"][None, :]),
                    (b1[:, :], a["L0_gnn_b1"][:, None])]
        others = [(avec[:, :], a["L2_gnn_a"].rearrange("z i -> i z")), (w2l2[:, :], a["L2_gnn_w2_W"])]
        for q, r in across:
            others += [(g.wg[r, q, :], a["L0_gnn_Wg"]),
                       (g.w_p[r, q, :], a["L3_gnn_W1"][0:D, :]),
                       (g.w_d[r, q, :], a["L3_gnn_W1"][D:2 * D, :]),
                       (g.w_e[r, q, :], a["L3_gnn_W1"][2 * D:3 * D, :]),
                       (g.w_y[r, q, 0:K1 * D].rearrange("i (k o) -> i k o", k=K1),
                        a["L1_gnn_weight"].rearrange("k i o -> i k o")),
                       (g.w_y[r, q, K1 * D:K1 * D + D], a["L1_gnn_root_w"].rearrange("o i -> i o")),
                       (g.w_s[r, q, :], a["L2_gnn_w1_W"].rearrange("o i -> i o")),
                       (g.w_a[r, q, :], a["L2_gnn_w2_W"].rearrange("o i -> i o"))]
        others += [(g.w_v[H * q:H * q + H, q, :], a["L3_gnn_W2"]) for q in range(2)]
        others += [(g.bias[:, k, 0:v.shape[0]], v[None, :].to_broadcast([P, v.shape[0]])) for k, v in enumerate(
            a[n] for n in ("L0_gnn_bg", "L1_gnn_root_b", "L2_gnn_w1_b", "L2_gnn_w2_b", "L3_gnn_b2", "L3_gnn_b1"))]

        with nc.Block() as block:
            @block.sync
            def _(sp):
                sp.dma_start(g.src[:, 0:EPP], a["src"].rearrange("(p t) -> p t", p=P)).then_inc(s["src_in"], 16)
                sp.dma_start(dst_i[:, 1:EPP + 1], a["dst"].rearrange("(p t) -> p t", p=P)).then_inc(s["dst_in"], 16)
                sp.wait_ge(s["filled"], 1)
                col = a["dst"].rearrange("(p t) -> p t", p=P)
                sp.dma_start(dst_i[1:P, 0:1], col[0:P - 1, EPP - 1:EPP],
                             allow_slow_non_contiguous=True).then_inc(s["border"], 16)
                sp.dma_start(next_i[0:P - 1, :], col[1:P, 0:1],
                             allow_slow_non_contiguous=True).then_inc(s["border"], 16)
                sp.dma_start(g.x[:, :, :], by_partition(a["x"], NP)).then_inc(s["x_in"], 16)
                sp.wait_ge(s["weights_zero"], 1)
                for tile, dram in encoder:
                    sp.dma_start(tile, dram, allow_slow_non_contiguous=True).then_inc(s["enc_in"], 16)
                for tile, dram in others:
                    sp.dma_start(tile, dram, allow_slow_non_contiguous=True).then_inc(s["w_in"], 16)
                sp.wait_ge(s["h0_out"], NJ // GJ)
                sp.dma_start(by_partition(g.encoded, NP), g.h0[:, :, :]).then_inc(s["encoded"], 16)
                sp.wait_ge(s["nothing_ok"], 1)
                for run in spare:
                    sp.dma_start(run[E:E + P, :], g.zeros[:, 0:run.shape[1]]).then_inc(s["zero_out"], 16)
                sp.wait_ge(s["zero_out"], 16 * len(spare))
                sp.wait_ge(s["dst_in"], 16)
                sp.wait_ge(s["border"], 32)

                @repeat(sp, LOOPS)
                def _(i):
                    for k in range(2):
                        wait(sp, early_in[k], (i + 1) * (8 * EARLY))
                        sp.dma_start(g.early_rows[:, bass.ds(i * EARLY + k * (EARLY // 2), EARLY // 2), :],
                                     early[:, k]).then_inc(early_out[k], 16)
                for k in range(2):
                    sp.wait_ge(early_out[k], 16 * LOOPS)
                sp.wait_ge(s["table_ok"], 1)
                sp.dma_start(by_partition(g.table, NP), g.m0[:, :, :]).then_inc(s["table_out"], 16)
                sp.wait_ge(s["table_out"], 16)

            @block.scalar
            def _(act):
                act.wait_ge(s["enc_in"], 16 * len(encoder))
                act.wait_ge(s["x_in"], 16)
                act.wait_ge(s["hid_one"], 1)

                @repeat(act, NJ // GJ // ENC)
                def _(i):
                    for step in range(ENC + 3):
                        n = i * ENC + step
                        if step < ENC:
                            k = step % 2
                            act.activation(stage[:, k, :].rearrange("p (j f) -> p j f", f=D),
                                           g.x[:, bass.ds(n * GJ, GJ), :], ACT.Copy).then_inc(s["staged"], 1)
                        if 0 <= step - 1 < ENC:
                            k = (step - 1) % 2
                            act.wait_ge(s["turned_ps"], n)
                            act.activation(turned[:, k, :], turn_ps[:, k, 0:NP], ACT.Copy).then_inc(s["turned_sb"], 1)
                        if 0 <= step - 2 < ENC:
                            k = (step - 2) % 2
                            act.wait_ge(s["hid_ready"], n - 1)
                            act.activation(hid[0:H, k, :], hid_ps[0:H, k, 0:GJ * NP], ACT.Relu,
                                           bias=b1[:, 0:1]).then_inc(s["hid_sb"], 1)
                        if 0 <= step - 3 < ENC:
                            k = (step - 3) % 2
                            act.wait_ge(s["h0_ready"], n - 2)
                            act.activation(g.h0[:, bass.ds((n - 3) * GJ, GJ), :],
                                           h0_ps[0:NP, k, 0:GJ * D].rearrange("p (j f) -> p j f", f=D),
                                           ACT.Relu).then_inc(s["h0_out"], 1)
                act.wait_ge(s["src_in"], 16)

                @repeat(act, LOOPS)
                def _(i):
                    for k in range(2):
                        wait(act, early_in[k], i * (8 * EARLY))
                        act.activation(early_idx[:, k, :],
                                       g.src[:, bass.ds(i * (SLOTS * T) + (AT_EARLY + k * (EARLY // 2)), EARLY // 2)],
                                       ACT.Copy).then_inc(early_ready[k], 1)
                act.wait_ge(s["root_in"], 1)
                act.activation(g.norm_src[:, :], g.norm_src[:, :], ACT.Sqrt).then_inc(s["root"], 1)

            @block.gpsimd
            def _(pool):
                pool.memset(g.ident[:, :], 0.0).then_inc(s["ident_zero"], 1)
                pool.iota(step_i[:, :], [[1, NP]], base=0, channel_multiplier=0).then_inc(s["consts"], 1)
                pool.iota(g.spare_row[:, :], [[1, 1]], base=E, channel_multiplier=1).then_inc(s["trash_ok"], 1)
                pool.iota(g.iota_e[:, :], [[0, 1]], base=0, channel_multiplier=EPP).then_inc(s["trash_ok"], 1)
                pool.iota(g.node_id[:, :], [[1, NJ]], base=0, channel_multiplier=NJ).then_inc(s["trash_ok"], 1)
                pool.wait_ge(s["trash_ok"], 3)
                pool.wait_ge(s["ident_zero"], 1)
                pool.affine_select(out=g.ident[:, :], in_=g.ident[:, :], compare_op=ALU.not_equal, fill=1.0,
                                   base=0, pattern=[[-1, P]], channel_multiplier=1).then_inc(s["consts"], 1)
                pool.wait_ge(s["encoded"], 16)

                @repeat(pool, LOOPS)
                def _(i):
                    for k in range(2):
                        wait(pool, early_ready[k], i + 1)
                        pool.nop(nofuse=True)
                        wait(pool, early_out[k], i * 16)
                        pool.nop(nofuse=True)
                        for t in range(EARLY // 2):
                            pool.indirect_dma_start(early[:, k, t, :], None, g.encoded, bass.IndirectOffsetOnAxis(
                                ap=early_idx[:, k, t:t + 1], axis=0)).then_inc(early_in[k], 16)

            @block.tensor
            def _(pe):
                pe.wait_ge(s["nothing_ok"], 1)
                pe.matmul(counts[:, 0:NJ], nothing[:, 0:NP], nothing[:, 0:NJ], start=True, stop=False,
                          skip_group_check=True)
                pe.wait_ge(s["consts"], 2)
                def count_slot(i, b):
                    k, n = nth_use(i, b, HOT_PREP)
                    wait(pe, marked[k], n + 1)
                    count(pe, counts[:, 0:NJ], hot, k).then_inc(used[k], 1)

                @repeat(pe, NJ // GJ // ENC)
                def _(i):
                    for step in range(ENC + 2):
                        n = i * ENC + step
                        if step < ENC:
                            k = step % 2
                            pe.wait_ge(s["staged"], n + 1)
                            pe.transpose(turn_ps[:, k, 0:NP], stage[:, k, :], g.ident[0:NP, 0:NP]).then_inc(
                                s["turned_ps"], 1)
                        if 0 <= step - 1 < ENC:
                            k = (step - 1) % 2
                            pe.wait_ge(s["turned_sb"], n)
                            for q in range(GJ):
                                last = pe.matmul(hid_ps[0:H, k, q * NP:q * NP + NP], w1[:, q, :],
                                                 turned[:, k, :], start=True, stop=True)
                            last.then_inc(s["hid_ready"], 1)
                        if 0 <= step - 2 < ENC:
                            k = (step - 2) % 2
                            pe.wait_ge(s["hid_sb"], n - 1)
                            wait(pe, s["h0_out"], n - 3)
                            for q in range(GJ):
                                last = pe.matmul(h0_ps[0:NP, k, q * D:q * D + D], hid[:, k, q * NP:q * NP + NP],
                                                 w2b[:, :], start=True, stop=True)
                            last.then_inc(s["h0_ready"], 1)
                        if step < SLOTS:
                            count_slot(i, step)

                @repeat(pe, LOOPS, start=NJ // GJ // ENC)
                def _(i):
                    for b in range(SLOTS):
                        count_slot(i, b)
                pe.matmul(counts[:, 0:NJ], nothing[:, 0:NP], nothing[:, 0:NJ], start=False, stop=True,
                          skip_group_check=True).then_inc(s["counted"], 1)
                pe.wait_ge(s["w_in"], 16 * len(others))
                pe.wait_ge(s["ab_ok"], 1)
                pe.matmul(small_ps[:, 0:D], acol[:, :], w2l2[:, :], start=True, stop=True).then_inc(s["ab_ps"], 1)

            @block.vector
            def _(dve):
                chain = Chain(dve, s["link"])
                for w in (w1, g.wg, g.w_p, g.w_d, g.w_e, g.w_s, g.w_a, g.w_v):
                    dve.memset(w[:, :, :], 0.0)
                dve.memset(g.w_y[:, :, :], 0.0).then_inc(s["weights_zero"], 1)
                chain(dve.memset(dst_i[:, 0:1], -1))
                dve.memset(next_i[:, :], -1).then_inc(s["filled"], 1)
                chain(dve.memset(g.src[:, EPP:EPP + SLOTS * T], 0))
                chain(dve.memset(nothing[:, :], 0.0))
                dve.memset(g.zeros[:, :], 0.0).then_inc(s["nothing_ok"], 1)
                dve.memset(hid[H:H + 1, :, :], 1.0).then_inc(s["hid_one"], 1)
                dve.wait_ge(s["consts"], 2)
                chain(dve.tensor_copy(step_f[:, :], step_i[:, :]))
                chain(dve.tensor_copy(g.steps[:, :, :], spread(step_f[:, :, None], [P, NP, T])))
                dve.wait_ge(s["src_in"], 16)
                digits(dve, chain, g.src[:, 0:EPP], g.high, g.low, g.pen)
                @repeat(dve, EPP // (T * SLOTS))
                def _(i):
                    for b in range(SLOTS):
                        k, n = nth_use(i, b, HOT_PREP)
                        wait(dve, used[k], n)
                        mark(dve, hot, k, g.steps, g.high, g.low, i * (SLOTS * T) + b * T).then_inc(marked[k], 1)
                dve.wait_ge(s["w_in"], 16 * len(others))
                dve.tensor_copy(acol[:, :], spread(avec[:, :], [D, P])).then_inc(s["ab_ok"], 1)
                dve.wait_ge(s["ab_ps"], 1)
                dve.tensor_copy(g.score_w[:, :], small_ps[:, 0:D]).then_inc(s["score_sb"], 1)
                dve.wait_ge(s["counted"], 1)
                dve.tensor_scalar(g.norm_src[:, :], counts[:, 0:NJ], 1.0, None, ALU.add).then_inc(s["root_in"], 1)
                dve.wait_ge(s["root"], 1)
                chain(dve.reciprocal(g.norm_src[:, :], g.norm_src[:, :]))
                dve.wait_ge(s["h0_out"], NJ // GJ)
                dve.tensor_tensor(g.m0[:, :, :], g.h0[:, :, :], spread(g.norm_src[:, :, None], [NP, NJ, D]),
                                  ALU.mult).then_inc(s["table_ok"], 1)


def gcn_edges(nc, g):
    with ExitStack() as stack:
        m = Pools(nc, stack, "gcn")
        idx = m.sb("idx", [P, SLOTS, T], I32)
        rows, running = m.sb("rows", [P, SLOTS, T, D]), m.sb("running", [P, SLOTS, T, D])
        hot, nothing = m.sb("hot", [P, HOT_GCN, NP + NJ, T], BF16), m.sb("nothing", [P, NP], BF16)
        zero_slot = m.sb("zero_slot", [P, T * D])
        idx_ready, gathered, scanned, stored = (m.sems(n) for n in ("idx_ready", "gathered", "scanned", "stored"))
        marked, used = m.sems("marked", HOT_GCN), m.sems("used", HOT_GCN)
        prepared, counted, zeroed, link, ends_in = (m.sem(n) for n in ("prepared", "counted", "zeroed", "link", "ends_in"))
        tot = m.sb("tot", [NP, 1])
        early_high, early_low = m.sb("early_high", [P, LOOPS * EARLY], BF16), m.sb("early_low", [P, LOOPS * EARLY], BF16)
        ident_h = m.sb("ident_h", [P, P], BF16)
        hot_high, hot_high_t = m.sb("hot_high", [P, NP, EARLY], BF16), m.sb("hot_high_t", [NP, EARLY, P])
        hot_low, factor = m.sb("hot_low", [P, EARLY, NJ]), m.sb("factor", [P, EARLY])
        turn_ps, pick_ps = m.ps("turn_ps", [NP, EARLY // LANES, 512]), m.ps("pick_ps", [P, EARLY // LANES, 512])
        high_ok, low_ok, turned_ps, turned_sb, picked, masked, factor_ok, early_in, scaled = (m.sem(n) for n in (
            "high_ok low_ok turned_ps turned_sb picked masked factor_ok early_in scaled").split())
        below = m.sb("below", [NP, NP])
        below_ok, tot_ok, based = m.sem("below_ok"), m.sem("tot_ok"), m.sem("based")
        counts = m.ps("counts", [NP, 512])
        work, cum = hot_low[0:NP, 0, :], hot_low[0:NP, 1, :]
        next_f, edge, rows33 = m.sb("next_f", [P, 1]), m.sb("edge", [P, 8]), m.sb("rows33", [P, 2, D + 2])
        rows_ok, rows_ps = m.sem("rows_ok"), m.sem("rows_ps_ok")
        row_ps, tot_ps = pick_ps[:, 0, :], pick_ps[0:NP, 1, :]

        with nc.Block() as block:
            @block.scalar
            def _(act):
                @repeat(act, LOOPS)
                def _(i):
                    for b in range(SLOTS):
                        wait(act, gathered[b], i * (16 * (T - EARLY if b == SLOTS - 1 else T)))
                        stage_ahead(act, g, idx, idx_ready, T, i, b)
                    act.wait_ge(turned_ps, i + 1)
                    for k in range(EARLY // LANES):
                        last = act.activation(hot_high_t[:, k * LANES:(k + 1) * LANES, :],
                                              turn_ps[:, k, :].rearrange("p (t e) -> p t e", e=P), ACT.Copy)
                    last.then_inc(turned_sb, 1)

            @block.gpsimd
            def _(pool):
                pool.memset(below[:, :], 1.0).then_inc(below_ok, 1)
                pool.wait_ge(below_ok, 1)
                pool.affine_select(out=below[:, :], in_=below[:, :], compare_op=ALU.is_gt, fill=0.0,
                                   base=0, pattern=[[1, NP]], channel_multiplier=-1).then_inc(below_ok, 1)
                gather_rows(pool, g.table[:, 0:D], rows, idx, idx_ready, scanned, gathered, T, LOOPS, EARLY)

            @block.sync
            def _(sp):
                sp.wait_ge(prepared, 1)
                fill = g.fill_rows[0:E, :].rearrange("(p t) f -> p (t f)", p=P)
                run_rows = by_partition(g.run[0:E, 0:D])
                @repeat(sp, LOOPS)
                def _(i):
                    sp.dma_start(rows[:, SLOTS - 1, 0:EARLY, :],
                                 g.early_rows[:, bass.ds(i * EARLY, EARLY), :]).then_inc(early_in, 16)
                    for b in range(SLOTS):
                        sp.dma_start(fill[:, bass.ds(i * (SLOTS * T * D) + b * T * D, T * D)],
                                     zero_slot[:, :]).then_inc(zeroed, 16)
                        wait(sp, scanned[b], i + 1)
                        sp.dma_start(run_rows[:, bass.ds(i * (SLOTS * T) + b * T, T), :],
                                     running[:, b]).then_inc(stored[b], 16)
                finish_stores(sp, stored, LOOPS)
                sp.wait_ge(zeroed, 16 * LOOPS * SLOTS)

            @block.tensor
            def _(pe):
                pe.wait_ge(prepared, 1)
                pe.matmul(counts[:, 0:NJ], nothing[:, 0:NP], nothing[:, 0:NJ], start=True, stop=False,
                          skip_group_check=True)
                @repeat(pe, LOOPS)
                def _(i):
                    for b in range(SLOTS):
                        k, n = nth_use(i, b, HOT_GCN)
                        wait(pe, marked[k], n + 1)
                        count(pe, counts[:, 0:NJ], hot, k).then_inc(used[k], 1)
                        if b == 0:
                            pe.wait_ge(high_ok, i + 1)
                            for t in range(EARLY):
                                at = t % LANES * P
                                last = pe.matmul(turn_ps[:, t // LANES, at:at + P], hot_high[:, :, t],
                                                 ident_h[:, :], start=True, stop=True)
                            last.then_inc(turned_ps, 1)
                        if b == 1:
                            pe.wait_ge(turned_sb, i + 1)
                            wait(pe, masked, i)
                            for t in range(EARLY):
                                at = t % LANES * NJ
                                last = pe.matmul(pick_ps[:, t // LANES, at:at + NJ], hot_high_t[:, t, :],
                                                 g.norm_src[:, :], start=True, stop=True)
                            last.then_inc(picked, 1)
                pe.matmul(counts[:, 0:NJ], nothing[:, 0:NP], nothing[:, 0:NJ], start=False, stop=True,
                          skip_group_check=True).then_inc(counted, 1)
                pe.wait_ge(rows_ok, 1)
                pe.transpose(row_ps[0:D + 2, 0:P], rows33[:, 0, :], g.ident[:, :])
                pe.transpose(row_ps[0:D + 2, P:2 * P], rows33[:, 1, :], g.ident[:, :]).then_inc(rows_ps, 1)
                pe.wait_ge(below_ok, 2)
                pe.wait_ge(tot_ok, 1)
                pe.matmul(tot_ps[:, 0:1], below[:, :], tot[:, :], start=True, stop=True).then_inc(based, 1)

            @block.vector
            def _(dve):
                chain = Chain(dve, link)
                chain(dve.memset(nothing[:, :], 0.0))
                chain(dve.memset(running[:, SLOTS - 1, T - 1, :], 0.0))
                dve.memset(zero_slot[:, :], 0.0).then_inc(prepared, 1)
                chain(dve.tensor_copy(g.dst_f[:, :], g.dst_i[:, :]))
                chain(dve.tensor_copy(next_f[:, :], g.next_i[:, :]))
                chain(dve.tensor_tensor(g.keep[:, :], g.dst_f[:, 1:EPP + 1], g.dst_f[:, 0:EPP], ALU.is_equal))
                chain(dve.tensor_copy(ident_h[:, :], g.ident[:, :]))
                for kept, digit in ((early_high, g.high), (early_low, g.low)):
                    chain(dve.tensor_copy(kept[:, :].rearrange("p (i t) -> p i t", t=EARLY),
                                          digit[:, :].rearrange("p (i t) -> p i t", t=SLOTS * T)[
                                              :, :, AT_EARLY:AT_EARLY + EARLY]))
                digits(dve, chain, g.dst_f[:, 1:EPP + 1], g.high, g.low, g.pen)
                chain(dve.tensor_scalar(g.pen[:, :], g.dst_f[:, 1:EPP + 1], g.dst_f[:, 1:2], None, ALU.is_equal))
                chain(dve.tensor_reduce(edge[:, 3:4], g.pen[:, :], AX.X, ALU.add))
                chain(dve.tensor_scalar(g.pen[:, :], g.keep[:, :], BIG, -BIG, ALU.mult, ALU.add))
                chain(dve.tensor_copy(g.first_dst[:, :], g.dst_i[:, 1:2]))

                @repeat(dve, LOOPS)
                def _(i):
                    for b in range(SLOTS):
                        at = i * (SLOTS * T) + b * T
                        k, n = nth_use(i, b, HOT_GCN)
                        wait(dve, used[k], n)
                        mark(dve, hot, k, g.steps, g.high, g.low, at).then_inc(marked[k], 1)
                        if b == 0:
                            dve.tensor_tensor(hot_high[:, :, :], g.steps[:, :, 0:EARLY],
                                              spread(early_high[:, None, bass.ds(i * EARLY, EARLY)], [P, NP, EARLY]),
                                              ALU.is_equal).then_inc(high_ok, 1)
                            dve.tensor_tensor(hot_low[:, :, :],
                                              spread(g.steps[:, 0:NJ, 0][:, None, :], [P, EARLY, NJ]),
                                              spread(early_low[:, bass.ds(i * EARLY, EARLY)][:, :, None],
                                                     [P, EARLY, NJ]), ALU.is_equal).then_inc(low_ok, 1)
                        if b == SLOTS - 1:
                            dve.wait_ge(low_ok, i + 1)
                            dve.wait_ge(picked, i + 1)
                            dve.tensor_tensor(hot_low[:, :, :].rearrange("p (k t) j -> p k (t j)", t=LANES),
                                              pick_ps[:, :, 0:LANES * NJ],
                                              hot_low[:, :, :].rearrange("p (k t) j -> p k (t j)", t=LANES),
                                              ALU.mult).then_inc(masked, 1)
                            dve.wait_ge(masked, i + 1)
                            dve.tensor_reduce(factor[:, :], hot_low[:, :, :], AX.X, ALU.add).then_inc(factor_ok, 1)
                            dve.wait_ge(factor_ok, i + 1)
                            dve.wait_ge(early_in, (i + 1) * 16)
                            dve.tensor_tensor(rows[:, b, 0:EARLY, :], rows[:, b, 0:EARLY, :],
                                              spread(factor[:, :, None], [P, EARLY, D]),
                                              ALU.mult).then_inc(scaled, 1)
                            dve.wait_ge(scaled, i + 1)
                        wait(dve, gathered[b], (i + 1) * (16 * (T - EARLY if b == SLOTS - 1 else T)))
                        wait(dve, stored[b], i * 16)
                        before = (b - 1) % SLOTS
                        wait(dve, scanned[before], i + 1 if b else i)
                        for f in range(D):
                            last = dve.tensor_tensor_scan(
                                running[:, b, :, f], g.keep[:, bass.ds(at, T)], rows[:, b, :, f],
                                running[:, before, T - 1, f:f + 1], ALU.mult, ALU.add)
                        last.then_inc(scanned[b], 1)
                dve.wait_ge(scanned[SLOTS - 1], LOOPS)
                chain(dve.tensor_copy(g.tail[:, 0:D], running[:, SLOTS - 1, T - 1, :]))
                chain(dve.tensor_tensor(edge[:, 0:1], g.dst_f[:, EPP:EPP + 1], next_f[:, :], ALU.is_equal))
                chain(dve.tensor_tensor(edge[:, 1:2], g.dst_f[:, 1:2], g.dst_f[:, EPP:EPP + 1], ALU.is_equal))
                chain(dve.tensor_copy(edge[:, 2:3], g.keep[:, 0:1]))
                chain(dve.tensor_tensor(edge[:, 4:5], edge[:, 0:1], edge[:, 1:2], ALU.mult))
                chain(dve.tensor_scalar(edge[:, 4:5], edge[:, 4:5], -1.0, 1.0, ALU.mult, ALU.add))
                chain(dve.tensor_tensor(edge[:, 4:5], edge[:, 4:5], edge[:, 2:3], ALU.mult))
                chain(dve.tensor_copy(edge[:, 5:6], g.iota_e[:, :]))
                chain(dve.tensor_copy(edge[:, 6:7], g.spare_row[:, :]))
                chain(dve.scalar_tensor_tensor(edge[:, 5:6], edge[:, 5:6], -1.0, edge[:, 3:4], ALU.add, ALU.add))
                chain(dve.tensor_tensor(edge[:, 5:6], edge[:, 5:6], edge[:, 6:7], ALU.subtract))
                chain(dve.tensor_tensor(edge[:, 5:6], edge[:, 5:6], edge[:, 4:5], ALU.mult))
                chain(dve.tensor_tensor(edge[:, 5:6], edge[:, 5:6], edge[:, 6:7], ALU.add))
                chain(dve.tensor_copy(g.head_idx[:, :], edge[:, 5:6]))
                chain(dve.tensor_tensor(edge[:, 7:8], edge[:, 1:2], edge[:, 2:3], ALU.mult))
                chain(dve.tensor_copy(rows33[:, 0, :], spread(edge[:, 7:8], [P, D + 2])))
                dve.tensor_scalar(rows33[:, 1, :], rows33[:, 0, :], BIG, -BIG, ALU.mult, ALU.add).then_inc(rows_ok, 1)
                dve.wait_ge(rows_ps, 1)
                chain(dve.tensor_copy(g.keep_row[:, :], row_ps[0:D + 2, 0:P]))
                chain(dve.tensor_copy(g.pen_row[:, :], row_ps[0:D + 2, P:2 * P]))
                dve.wait_ge(counted, 1)
                chain(dve.tensor_copy(g.deg[:, :], counts[:, 0:NJ]))
                chain(dve.tensor_scalar(g.mask[:, :], g.deg[:, :], 0.0, None, ALU.is_gt))
                chain(dve.tensor_scalar(g.pen_node[:, :], g.mask[:, :], BIG, -BIG, ALU.mult, ALU.add))
                chain(dve.memset(work[:, :], 1.0))
                chain(dve.tensor_tensor_scan(cum[:, :], work[:, :], g.deg[:, :], 0.0, ALU.mult, ALU.add))
                dve.tensor_copy(tot[:, :], cum[:, NJ - 1:NJ]).then_inc(tot_ok, 1)
                dve.wait_ge(based, 1)
                chain(dve.tensor_copy(tot[:, :], tot_ps[:, 0:1]))
                chain(dve.tensor_scalar(cum[:, :], cum[:, :], tot[:, 0:1], None, ALU.add))
                chain(dve.tensor_scalar(work[:, :], cum[:, :], -1.0, 0.0, ALU.add, ALU.max))
                chain(dve.tensor_copy(g.end_idx[:, :], work[:, :]))
                chain(dve.tensor_copy(work[:, :], g.node_id[:, :]))
                chain(dve.tensor_scalar(work[:, :], work[:, :], float(E), None, ALU.add))
                chain(dve.tensor_tensor(cum[:, :], cum[:, :], g.deg[:, :], ALU.subtract))
                chain(dve.tensor_tensor(cum[:, :], cum[:, :], work[:, :], ALU.subtract))
                chain(dve.tensor_tensor(cum[:, :], cum[:, :], g.mask[:, :], ALU.mult))
                chain(dve.tensor_tensor(cum[:, :], cum[:, :], work[:, :], ALU.add))
                chain(dve.tensor_copy(g.start_idx[:, :], cum[:, :]))


def gcn_nodes(nc, g):
    with ExitStack() as stack:
        m = Pools(nc, stack, "gcn_n")
        agg, out = m.sb("agg", [NP, NJ, D]), m.sb("out", [NP, NJ, D])
        norm_dst = m.sb("norm_dst", [NP, NJ])
        wide = [NP, CJ, D]
        carry(nc, g, "sum", g.run, g.tail)

        def before(dve, chain, cols, made):
            chain(dve.tensor_tensor(agg[:, cols, :], agg[:, cols, :], spread(g.mask[:, cols, None], wide), ALU.mult))
            chain(dve.tensor_tensor(agg[:, cols, :], agg[:, cols, :], g.m0[:, cols, :], ALU.add))
            dve.tensor_tensor(agg[:, cols, :], agg[:, cols, :], spread(norm_dst[:, cols, None], wide),
                              ALU.mult).then_inc(made, 1)

        def take(dve, ps, cols):
            return dve.tensor_tensor(out[:, cols, :], ps, spread(g.bias[0:NP, 0:1, 0:D], [NP, GJ, D]), ALU.add)

        def after(dve, chain, cols):
            chain(dve.scalar_tensor_tensor(out[:, cols, :], out[:, cols, :], 0.0, g.h0[:, cols, :], ALU.max, ALU.add))
            chain(dve.tensor_tensor(g.x[:, cols, :], g.x[:, cols, :], out[:, cols, :], ALU.add))

        node_phase(nc, g, "gcn_node", g.run[0:E + P, 0:D], agg, before, Linear([(agg, g.wg)], D), take, after,
                   table=(Linear([(g.x, g.w_y)], (K1 + 1) * D), g.spline_rows, None), root_first=norm_dst[:, :])


def spline_edges(nc, g, a):
    with ExitStack() as stack:
        m = Pools(nc, stack, "spln")
        idx = m.sb("idx", [P, SLOTS, T1], I32)
        rows = m.sb("rows", [P, SLOTS, T1, K1 * D])
        halves = m.sb("halves", [P, SLOTS, T1, 2, 3 * D])
        third, part = m.sb("third", [P, 2, T1, 3 * D]), m.sb("part", [P, T, 3 * D])
        msg3, msg, running = m.sb("msg3", [P, T, 3, D]), m.sb("msg", [P, T, D]), m.sb("running", [P, 2, T, D])
        place = m.sb("place", [P, EPP + T, 2])
        coef = m.sb("coef", [P, T, 2, 3])
        placed, link, scanned, stored, based, halved = (
            m.sem(n) for n in ("placed", "link", "scanned", "stored", "based", "halved"))
        idx_ready, gathered, slot_free = (m.sems(n) for n in ("idx_ready", "gathered", "slot_free"))

        with nc.Block() as block:
            @block.scalar
            def _(act):
                for b in range(SLOTS):
                    stage_ahead(act, g, idx, idx_ready, T1, 0, b)

                @repeat(act, LOOPS1)
                def _(i):
                    wait(act, based, i + 1)
                    for b in range(SLOTS):
                        wait(act, gathered[b], (i + 1) * (16 * T1))
                        stage_ahead(act, g, idx, idx_ready, T1, i + 1, b)
                        wait(act, slot_free[b], i)
                        for t in range(T1):
                            for c in range(2):
                                last = act.activation(
                                    halves[:, b, t, c, :], rows[:, b, t, c * 3 * D:(c + 1) * 3 * D], ACT.Copy,
                                    scale=coef[:, b * T1 + t, 0, c:c + 1])
                        last.then_inc(halved, 1)

            @block.gpsimd
            def _(pool):
                gather_rows(pool, g.spline_rows, rows, idx, idx_ready, slot_free, gathered, T1, LOOPS1)

            @block.sync
            def _(sp):
                sp.dma_start(place[:, 0:EPP, :],
                             a["edge_attr_2"].rearrange("(p t) c -> p t c", p=P)).then_inc(placed, 16)
                run_rows = by_partition(g.run[0:E, 0:D])

                @repeat(sp, LOOPS1)
                def _(i):
                    wait(sp, scanned, i + 1)
                    sp.dma_start(run_rows[:, bass.ds(i * T, T), :], running[:, 0]).then_inc(stored, 16)
                sp.wait_ge(stored, 16 * LOOPS1)

            @block.vector
            def _(dve):
                chain = Chain(dve, link)

                def basis(i):
                    chain(dve.tensor_scalar(coef[:, :, :, 1], place[:, bass.ds(i * T, T), :], 0.0, 1.0,
                                            ALU.max, ALU.min))
                    dve.tensor_scalar(coef[:, :, :, 0], coef[:, :, :, 1], -2.0, 1.0, ALU.mult, ALU.add)
                    chain(dve.tensor_scalar(coef[:, :, :, 2], coef[:, :, :, 1], 2.0, -1.0, ALU.mult, ALU.add))
                    chain(dve.tensor_tensor(coef[:, :, :, 1], coef[:, :, :, 0], coef[:, :, :, 2], ALU.max))
                    dve.tensor_scalar(coef[:, :, :, 1], coef[:, :, :, 1], -1.0, 1.0, ALU.mult, ALU.add)
                    dve.tensor_scalar(coef[:, :, :, 0], coef[:, :, :, 0], 0.0, None, ALU.max)
                    dve.tensor_scalar(coef[:, :, :, 2], coef[:, :, :, 2], 0.0, None, ALU.max).then_inc(based, 1)

                chain(dve.memset(running[:, 1, T - 1, :], 0.0))
                chain(dve.memset(place[:, EPP:EPP + T, :], 0.0))
                dve.wait_ge(placed, 16)
                basis(0)

                @repeat(dve, LOOPS1)
                def _(i):
                    chain.loop(i, 2 * SLOTS + 1 + 3 + 2 + 1)
                    wait(dve, based, i + 1)
                    for b in range(SLOTS):
                        wait(dve, gathered[b], (i + 1) * (16 * T1))
                        edges = slice(b * T1, b * T1 + T1)
                        chain(dve.tensor_tensor(third[:, b % 2], rows[:, b, :, 6 * D:9 * D],
                                                spread(coef[:, edges, 0, 2:3], [P, T1, 3 * D]), ALU.mult))
                        wait(dve, halved, i * SLOTS + b + 1)
                        chain(dve.tensor_tensor(part[:, edges, :], halves[:, b, :, 0, :], halves[:, b, :, 1, :], ALU.add))
                        dve.tensor_tensor(part[:, edges, :], part[:, edges, :], third[:, b % 2],
                                          ALU.add).then_inc(slot_free[b], 1)
                    wait(dve, slot_free[SLOTS - 1], i + 1)
                    chain(dve.tensor_tensor(msg3[:, :, :, :], part[:, :, :].rearrange("p t (a f) -> p t a f", a=3),
                                            spread(coef[:, :, 1, :, None], [P, T, 3, D]), ALU.mult))
                    basis(i + 1)
                    chain(dve.tensor_tensor(msg[:, :, :], msg3[:, :, 0, :], msg3[:, :, 1, :], ALU.add))
                    chain(dve.tensor_tensor(msg[:, :, :], msg[:, :, :], msg3[:, :, 2, :], ALU.add))
                    wait(dve, stored, i * 16)
                    for f in range(D):
                        last = dve.tensor_tensor_scan(
                            running[:, 0, :, f], g.keep[:, bass.ds(i * T, T)], msg[:, :, f],
                            running[:, 1, T - 1, f:f + 1], ALU.mult, ALU.add)
                    last.then_inc(scanned, 1)
                    wait(dve, scanned, i + 1)
                    chain(dve.tensor_copy(running[:, 1, T - 1, :], running[:, 0, T - 1, :]))
                chain.end_loop(LOOPS1)
                chain(dve.tensor_copy(g.tail[:, 0:D], running[:, 1, T - 1, :]))


def spline_nodes(nc, g):
    with ExitStack() as stack:
        m = Pools(nc, stack, "spl_n")
        agg, table = m.sb("agg", [NP, NJ, D]), m.sb("table", [NP, NJ, D + 1])
        mean = m.sb("mean", [NP, NJ])
        wide = [NP, CJ, D]
        carry(nc, g, "sum", g.run, g.tail)

        def before(dve, chain, cols, made):
            chain(dve.tensor_scalar(mean[:, cols], g.deg[:, cols], 1.0, None, ALU.max))
            chain(dve.reciprocal(mean[:, cols], mean[:, cols]))
            chain(dve.tensor_tensor(mean[:, cols], mean[:, cols], g.mask[:, cols], ALU.mult))
            chain(dve.tensor_tensor(agg[:, cols, :], agg[:, cols, :], spread(mean[:, cols, None], wide), ALU.mult))

        def after(dve, chain, cols):
            chain(dve.tensor_tensor(agg[:, cols, :], agg[:, cols, :], g.rooted[:, cols, :], ALU.add))
            chain(dve.tensor_tensor(agg[:, cols, :], agg[:, cols, :], spread(g.bias[0:NP, 1:2, 0:D], wide), ALU.add))
            chain(dve.tensor_tensor(g.x[:, cols, :], g.x[:, cols, :], agg[:, cols, :], ALU.add))

        def finish(dve, chain, cols):
            chain(dve.tensor_copy(table[:, cols, 0:D], g.x[:, cols, :]))
            chain(dve.tensor_tensor(agg[:, cols, :], g.x[:, cols, :], spread(g.score_w[0:NP, None, :], wide), ALU.mult))
            return dve.tensor_reduce(table[:, cols, D:D + 1], agg[:, cols, :], AX.X, ALU.add)

        node_phase(nc, g, "spl_node", g.run[0:E + P, 0:D], agg, before, None, None, after, finish,
                   sends=[(g.att_rows, table)])


def attention_edges(nc, g):
    with ExitStack() as stack:
        m = Pools(nc, stack, "attn")
        idx = m.sb("idx", [P, SLOTS, T], I32)
        rows, running = m.sb("rows", [P, SLOTS, T, D + 1]), m.sb("running", [P, SLOTS, T, D + 2])
        top, drift, weighted = m.sb("top", [P, T + 1]), m.sb("drift", [P, 2, T]), m.sb("weighted", [P, T, D + 1])
        score = m.sb("score", [P, T])
        idx_ready, gathered, scanned, stored = (m.sems(n) for n in ("idx_ready", "gathered", "scanned", "stored"))
        link, exp_in, exp_out = m.sem("link"), m.sem("exp_in"), m.sem("exp_out")

        with nc.Block() as block:
            @block.scalar
            def _(act):
                for b in range(SLOTS):
                    stage_ahead(act, g, idx, idx_ready, T, 0, b)

                @repeat(act, LOOPS)
                def _(i):
                    for b in range(SLOTS):
                        wait(act, gathered[b], (i + 1) * (16 * T))
                        stage_ahead(act, g, idx, idx_ready, T, i + 1, b)
                        wait(act, exp_in, i * SLOTS + b + 1)
                        act.activation(drift[:, :, :], drift[:, :, :], ACT.Exp).then_inc(exp_out, 1)

            @block.gpsimd
            def _(pool):
                gather_rows(pool, g.att_rows, rows, idx, idx_ready, scanned, gathered, T, LOOPS)

            @block.sync
            def _(sp):
                store_running(sp, running, by_partition(g.run[0:E, 0:D + 2]), scanned, stored, LOOPS)
                finish_stores(sp, stored, LOOPS)

            @block.vector
            def _(dve):
                chain = Chain(dve, link)
                chain(dve.memset(running[:, SLOTS - 1, T - 1, 0:D + 1], 0.0))
                chain(dve.memset(top[:, T:T + 1], -BIG))
                chain(dve.memset(drift[:, :, :], 0.0))
                @repeat(dve, LOOPS)
                def _(i):
                    chain.loop(i, 8 * SLOTS)
                    for b in range(SLOTS):
                        at = i * (SLOTS * T) + b * T
                        before = (b - 1) % SLOTS
                        chain(dve.tensor_copy(top[:, 0:1], top[:, T:T + 1]))
                        wait(dve, gathered[b], (i + 1) * (16 * T))
                        chain(dve.tensor_scalar(score[:, :], rows[:, b, :, D], -1.0, None, ALU.mult))
                        chain(dve.tensor_tensor_scan(top[:, 1:T + 1], g.pen[:, bass.ds(at, T)], score[:, :],
                                                     top[:, 0:1], ALU.add, ALU.max))
                        chain(dve.tensor_tensor(drift[:, 0, :], top[:, 0:T], g.pen[:, bass.ds(at, T)], ALU.add))
                        chain(dve.tensor_tensor(drift[:, 0, :], drift[:, 0, :], top[:, 1:T + 1], ALU.subtract))
                        dve.tensor_tensor(drift[:, 1, :], score[:, :], top[:, 1:T + 1],
                                          ALU.subtract).then_inc(exp_in, 1)
                        wait(dve, exp_out, i * SLOTS + b + 1)
                        chain(dve.tensor_tensor(weighted[:, :, 0:D], rows[:, b, :, 0:D],
                                                spread(drift[:, 1, :, None], [P, T, D]), ALU.mult))
                        chain(dve.tensor_copy(weighted[:, :, D], drift[:, 1, :]))
                        wait(dve, stored[b], i * 16)
                        wait(dve, scanned[before], i + 1 if b else i)
                        chain(dve.tensor_copy(running[:, b, :, D + 1], top[:, 1:T + 1]))
                        for f in range(D + 1):
                            last = dve.tensor_tensor_scan(
                                running[:, b, :, f], drift[:, 0, :], weighted[:, :, f],
                                running[:, before, T - 1, f:f + 1], ALU.mult, ALU.add)
                        last.then_inc(scanned[b], 1)
                        wait(dve, scanned[b], i + 1)
                chain.end_loop(LOOPS)
                chain(dve.tensor_copy(g.tail[:, :], running[:, SLOTS - 1, T - 1, :]))


def attention_nodes(nc, g):
    with ExitStack() as stack:
        m = Pools(nc, stack, "att_n")
        state, agg, out = m.sb("state", [NP, NJ, D + 2]), m.sb("agg", [NP, NJ, D]), m.sb("out", [NP, NJ, D])
        share = m.sb("share", [NP, NJ])
        wide = [NP, CJ, D]
        carry(nc, g, "softmax", g.run, g.tail)

        def before(dve, chain, cols, made):
            chain(dve.tensor_tensor(share[:, cols], state[:, cols, D], g.mask[:, cols], ALU.mult))
            chain(dve.scalar_tensor_tensor(share[:, cols], share[:, cols], 1.0, g.mask[:, cols], ALU.add, ALU.subtract))
            chain(dve.reciprocal(share[:, cols], share[:, cols]))
            chain(dve.tensor_tensor(share[:, cols], share[:, cols], g.mask[:, cols], ALU.mult))
            dve.tensor_tensor(agg[:, cols, :], state[:, cols, 0:D], spread(share[:, cols, None], wide),
                              ALU.mult).then_inc(made, 1)

        def take(dve, ps, cols):
            return dve.tensor_tensor(out[:, cols, :], ps, spread(g.bias[0:NP, 2:3, 0:D], [NP, GJ, D]), ALU.add)

        def after(dve, chain, cols):
            chain(dve.tensor_tensor(agg[:, cols, :], spread(g.mask[:, cols, None], wide),
                                    spread(g.bias[0:NP, 3:4, 0:D], wide), ALU.mult))
            chain(dve.tensor_tensor(out[:, cols, :], out[:, cols, :], agg[:, cols, :], ALU.add))
            chain(dve.tensor_tensor(g.x[:, cols, :], g.x[:, cols, :], out[:, cols, :], ALU.add))

        node_phase(nc, g, "att_node", g.run[0:E + P, 0:D + 2], state, before, Linear([(agg, g.w_a), (g.x, g.w_s)], D),
                   take, after, table=(Linear([(g.x, g.w_p)], H), g.mlp_rows, g.bias[0:NP, 5:6, 0:H]),
                   sends=[(g.table, g.x)], place=g.fill_rows)


def mlp_edges(nc, g, a):
    GE = 5
    PER = T // GE
    GROUPS = SLOTS * PER
    with ExitStack() as stack:
        m = Pools(nc, stack, "edge_mlp")
        idx = m.sb("idx", [P, SLOTS, T], I32)
        rows = m.sb("rows", [P, SLOTS, T, H])
        first_rows, attr, x_dst = (m.sb(n, [P, SLOTS, T, D]) for n in ("first_rows", "attr", "x_dst"))
        value, running = m.sb("value", [P, 2, T, D]), m.sb("running", [P, SLOTS, T, D])
        in_t, hid = m.sb("in_t", [P, 2, 4, P]), m.sb("hid", [P, 2, GE * H])
        hid_t = m.sb("hid_t", [P, 2, 3, P])
        in_ps, hid_ps, hid_t_ps, val_ps = (m.ps(n, [P, 2, 512]) for n in ("in_ps", "hid_ps", "hid_t_ps", "val_ps"))
        idx_ready, gathered, scanned, stored = (m.sems(n) for n in ("idx_ready", "gathered", "scanned", "stored"))
        loaded, spread_ok = m.sems("loaded"), m.sems("spread_ok")
        (started, turned, turned_sb, product, summed, hid_turned, hid_turned_sb, valued, value_sb, first) = (
            m.sem(n) for n in ("started turned turned_sb product summed hid_turned hid_turned_sb valued value_sb "
                               "first").split())

        with nc.Block() as block:
            @block.sync
            def _(sp):
                places = by_partition(g.fill_rows[0:E, :])
                attrs = by_partition(a["edge_attr_32"])
                run_rows = by_partition(g.run[0:E, 0:D])

                def load(i, b, at):
                    sp.dma_start(first_rows[:, b], places[:, bass.ds(at, T), :]).then_inc(loaded[b], 16)
                    sp.dma_start(attr[:, b], attrs[:, bass.ds(at, T), :]).then_inc(loaded[b], 16)

                for b in range(SLOTS):
                    load(0, b, b * T)
                @repeat(sp, LOOPS - 1)
                def _(i):
                    for b in range(SLOTS):
                        wait(sp, scanned[b], i + 1)
                        sp.dma_start(run_rows[:, bass.ds(i * (SLOTS * T) + b * T, T), :],
                                     running[:, b]).then_inc(stored[b], 16)
                        load(i, b, (i + 1) * (SLOTS * T) + b * T)
                for b in range(SLOTS):
                    sp.wait_ge(scanned[b], LOOPS)
                    at = (LOOPS - 1) * SLOTS * T + b * T
                    sp.dma_start(run_rows[:, at:at + T, :], running[:, b]).then_inc(stored[b], 16)
                finish_stores(sp, stored, LOOPS)

            @block.gpsimd
            def _(pool):
                pool.indirect_dma_start(x_dst[:, SLOTS - 1, T - 1, :], None, g.table[:, 0:D],
                                        bass.IndirectOffsetOnAxis(ap=g.first_dst[:, 0:1], axis=0)).then_inc(first, 16)
                gather_rows(pool, g.mlp_rows, rows, idx, idx_ready, scanned, gathered, T, LOOPS)

            @block.scalar
            def _(act):
                for b in range(SLOTS):
                    stage_ahead(act, g, idx, idx_ready, T, 0, b)

                @repeat(act, LOOPS)
                def _(i):
                    n = i * GROUPS
                    for s in range(GROUPS + 3):
                        if s < GROUPS:
                            k = s % 2
                            wait(act, turned, n + s + 1)
                            wait(act, product, n + max(s - 1, 0))
                            act.activation(in_t[:, k, 0:2, :], in_ps[:, k, 0:2 * P].rearrange("p (c e) -> p c e", e=P),
                                           ACT.Copy)
                            act.activation(in_t[0:D, k, 2:4, :],
                                           in_ps[0:D, k, 2 * P:4 * P].rearrange("p (c e) -> p c e", e=P),
                                           ACT.Copy).then_inc(turned_sb, 1)
                        if 0 <= s - 2 < GROUPS:
                            u = s - 2
                            k = u % 2
                            wait(act, hid_turned, n + u + 1)
                            wait(act, valued, n + max(u - 1, 0))
                            act.activation(hid_t[:, k, 0:2, :], hid_t_ps[:, k, 0:2 * P].rearrange("p (c e) -> p c e", e=P),
                                           ACT.Relu)
                            act.activation(hid_t[0:H, k, 2, :], hid_t_ps[0:H, k, 2 * P:3 * P],
                                           ACT.Relu).then_inc(hid_turned_sb, 1)
                            if u % PER == 0:
                                wait(act, gathered[u // PER], (i + 1) * (16 * T))
                                stage_ahead(act, g, idx, idx_ready, T, i + 1, u // PER)
                        if 0 <= s - 3 < GROUPS:
                            u = s - 3
                            b, c = u // PER, u % PER
                            wait(act, valued, n + u + 1)
                            if c == 0 and b >= 2:
                                wait(act, scanned[b - 2], i + 1)
                            elif c == 0:
                                wait(act, scanned[SLOTS - 1], i)
                            act.activation(value[:, b % 2, c * GE:c * GE + GE, :],
                                           val_ps[:, u % 2, 0:GE * D].rearrange("p (t f) -> p t f", f=D),
                                           ACT.Copy).then_inc(value_sb, 1)

            @block.tensor
            def _(pe):
                @repeat(pe, LOOPS)
                def _(i):
                    n = i * GROUPS

                    def turn(s):
                        b, at, k = s // PER, s % PER * GE, s % 2
                        if s % PER == 0:
                            wait(pe, loaded[b], (i + 1) * 32)
                            wait(pe, spread_ok[b], i + 1)
                        wait(pe, turned_sb, n + max(s - 1, 0))
                        for c, (tile, lo, hi) in enumerate(((attr, 0, 4), (x_dst, 0, 4), (attr, 4, 5), (x_dst, 4, 5))):
                            last = pe.transpose(in_ps[0:(hi - lo) * D, k, c * P:c * P + P],
                                                tile[:, b, at + lo:at + hi, :].rearrange("p t f -> p (t f)"), g.ident[:, :])
                        last.then_inc(turned, 1)

                    def first_product(s):
                        k = s % 2
                        wait(pe, turned_sb, n + s + 1)
                        wait(pe, summed, n + max(s - 1, 0))
                        for lanes, t, c in ((slice(0, P), 0, 0), (slice(0, D), 4, 2)):
                            out = hid_ps[:, k, t * H:(t + 4) * H] if t == 0 else hid_ps[:, k, t * H:t * H + H]
                            wide = slice(0, 4 if t == 0 else 1)
                            pe.matmul(out, in_t[lanes, k, c, :], g.w_e[lanes, wide, :], start=True, stop=False)
                            last = pe.matmul(out, in_t[lanes, k, c + 1, :], g.w_d[lanes, wide, :],
                                             start=False, stop=True)
                        last.then_inc(product, 1)

                    def turn_hidden(s):
                        k = s % 2
                        wait(pe, summed, n + s + 1)
                        wait(pe, hid_turned_sb, n + max(s - 1, 0))
                        for c in range(3):
                            w = 2 * H if c < 2 else H
                            last = pe.transpose(hid_t_ps[0:w, k, c * P:c * P + P], hid[:, k, c * 2 * H:c * 2 * H + w],
                                                g.ident[:, :])
                        last.then_inc(hid_turned, 1)

                    def second_product(s):
                        k = s % 2
                        wait(pe, hid_turned_sb, n + s + 1)
                        wait(pe, value_sb, n + max(s - 1, 0))
                        for c in range(3):
                            lanes, wide = (slice(0, P), slice(0, 2)) if c < 2 else (slice(0, H), slice(0, 1))
                            at = 2 * c * D
                            last = pe.matmul(val_ps[:, k, at:at + (2 * D if c < 2 else D)], hid_t[lanes, k, c, :],
                                             g.w_v[lanes, wide, :], start=True, stop=True)
                        last.then_inc(valued, 1)

                    for s in range(GROUPS + 3):
                        for lag, stage in enumerate((turn, first_product, turn_hidden, second_product)):
                            if 0 <= s - lag < GROUPS:
                                stage(s - lag)

            @block.vector
            def _(dve):
                dve.memset(running[:, SLOTS - 1, T - 1, :], -BIG).then_inc(started, 1)
                dve.wait_ge(started, 1)
                dve.wait_ge(first, 16)
                @repeat(dve, LOOPS)
                def _(i):
                    n = i * GROUPS

                    def spread_rows(b):
                        at, before = i * (SLOTS * T) + b * T, (b - 1) % SLOTS
                        wait(dve, loaded[b], (i + 1) * 32)
                        wait(dve, spread_ok[before], i + 1 if b else i)
                        for f in range(D):
                            last = dve.tensor_tensor_scan(
                                x_dst[:, b, :, f], g.keep[:, bass.ds(at, T)], first_rows[:, b, :, f],
                                x_dst[:, before, T - 1, f:f + 1], ALU.mult, ALU.add)
                        last.then_inc(spread_ok[b], 1)

                    def add_source(s):
                        b, at, k = s // PER, s % PER * GE, s % 2
                        if s % PER == 0:
                            wait(dve, gathered[b], (i + 1) * (16 * T))
                        wait(dve, product, n + s + 1)
                        wait(dve, hid_turned, n + max(s - 1, 0))
                        dve.tensor_tensor(hid[:, k, :], hid_ps[:, k, 0:GE * H],
                                          rows[:, b, at:at + GE, :].rearrange("p t f -> p (t f)"),
                                          ALU.add).then_inc(summed, 1)

                    def maximum(b):
                        at, before = i * (SLOTS * T) + b * T, (b - 1) % SLOTS
                        wait(dve, value_sb, n + (b + 1) * PER)
                        wait(dve, stored[b], i * 16)
                        wait(dve, scanned[before], i + 1 if b else i)
                        for f in range(D):
                            last = dve.tensor_tensor_scan(
                                running[:, b, :, f], g.pen[:, bass.ds(at, T)], value[:, b % 2, :, f],
                                running[:, before, T - 1, f:f + 1], ALU.add, ALU.max)
                        last.then_inc(scanned[b], 1)

                    spread_rows(0)
                    for s in range(GROUPS + 5):
                        if s % PER == 0 and s // PER + 1 < SLOTS:
                            spread_rows(s // PER + 1)
                        if 0 <= s - 1 < GROUPS:
                            add_source(s - 1)
                        if 0 <= s - 5 < GROUPS and (s - 5) % PER == PER - 1:
                            maximum((s - 5) // PER)
                dve.wait_ge(scanned[SLOTS - 1], LOOPS)
                dve.tensor_copy(g.tail[:, 0:D], running[:, SLOTS - 1, T - 1, :])


def mlp_nodes(nc, g, out):
    with ExitStack() as stack:
        m = Pools(nc, stack, "mlp_n")
        top = m.sb("top", [NP, NJ, D])
        wide = [NP, CJ, D]
        carry(nc, g, "max", g.run, g.tail)

        def before(dve, chain, cols, made):
            chain(dve.tensor_tensor(top[:, cols, :], top[:, cols, :], spread(g.mask[:, cols, None], wide), ALU.mult))
            chain(dve.tensor_tensor(top[:, cols, :], top[:, cols, :], spread(g.pen_node[:, cols, None], wide), ALU.add))
            chain(dve.tensor_tensor(top[:, cols, :], top[:, cols, :], spread(g.bias[0:NP, 4:5, 0:D], wide), ALU.add))

        def after(dve, chain, cols):
            chain(dve.tensor_tensor(top[:, cols, :], top[:, cols, :], g.x[:, cols, :], ALU.max))
            chain(dve.tensor_tensor(g.x[:, cols, :], g.x[:, cols, :], top[:, cols, :], ALU.add))

        node_phase(nc, g, "mlp_node", g.run[0:E + P, 0:D], top, before, None, None, after, sends=[(out, g.x)])


class Globals:
    pass


def graph_layers(nc, a, out):
    g = Globals()
    g.phase = 0
    Pools.live.clear()
    with ExitStack() as stack:
        m = Pools(nc, stack, "g")
        g.src = m.sb("src", [P, EPP + SLOTS * T], I32)
        g.keep, g.pen = m.sb("keep", [P, EPP]), m.sb("pen", [P, EPP])
        g.ident = m.sb("ident", [P, P])
        g.x = m.sb("x", [NP, NJ, D])
        g.rooted = m.sb("rooted", [NP, NJ, D])
        g.end_idx, g.start_idx, g.node_id = (m.sb(n, [NP, NJ], I32) for n in ("end_idx", "start_idx", "node_id"))
        g.mask, g.pen_node, g.deg = (m.sb(n, [NP, NJ]) for n in ("mask", "pen_node", "deg"))
        g.norm_src = m.sb("norm_src", [NP, NJ])
        g.stat = m.sb("stat", [NP, 2, NJ])
        g.head_idx, g.first_dst, g.iota_e = (m.sb(n, [P, 1], I32) for n in ("head_idx", "first_dst", "iota_e"))
        g.keep_row, g.pen_row = m.sb("keep_row", [D + 2, P]), m.sb("pen_row", [D + 2, P])
        g.tail = m.sb("tail", [P, D + 2])
        g.zeros = m.sb("zeros", [P, D + 2])
        g.score_w = m.sb("score_w", [P, D])
        g.bias = m.sb("bias", [P, 6, H])
        g.wg, g.w_s, g.w_a = (m.sb(n, [P, GJ, D]) for n in ("wg", "w_s", "w_a"))
        g.w_p, g.w_d, g.w_e = (m.sb(n, [P, GJ, H]) for n in ("w_p", "w_d", "w_e"))
        g.w_v = m.sb("w_v", [P, 2, D])
        g.w_y = m.sb("w_y", [P, GJ, (K1 + 1) * D])
        dram = lambda name, shape: nc.dram_tensor(name, shape, F32, kind="Internal").ap()
        g.table = dram("node_rows", (N, D))
        g.encoded = dram("encoded", (N, D))
        g.early_rows = dram("early_rows", (P, LOOPS * EARLY, D))
        g.spline_rows = dram("spline_rows", (N, K1 * D))
        g.att_rows = dram("att_rows", (N, D + 1))
        g.mlp_rows = dram("mlp_rows", (N, H))
        g.fill_rows = dram("fill_rows", (E + N, D))
        runs = {w: dram(f"run{w}", (E + P, w)) for w in (D, D + 2)}
        with ExitStack() as first:
            f = Pools(nc, first, "f")
            g.h0 = f.sb("h0", [NP, NJ, D])
            g.m0 = g.rooted
            g.high, g.low = f.sb("high", [P, EPP], BF16), f.sb("low", [P, EPP], BF16)
            g.dst_i, g.dst_f = f.sb("dst_i", [P, EPP + 1], I32), f.sb("dst_f", [P, EPP + 1])
            g.next_i, g.spare_row = f.sb("next_i", [P, 1], I32), f.sb("spare_row", [P, 1], I32)
            g.steps = f.sb("steps", [P, NP, T], BF16)
            g.run = runs[D]
            prepare(nc, g, a, list(runs.values()))
            gcn_edges(nc, g)
            gcn_nodes(nc, g)
        clear_semaphores(nc)
        spline_edges(nc, g, a)
        spline_nodes(nc, g)
        g.run = runs[D + 2]
        attention_edges(nc, g)
        attention_nodes(nc, g)
        clear_semaphores(nc)
        g.run = runs[D]
        mlp_edges(nc, g, a)
        mlp_nodes(nc, g, out)


_INS = ['x', 'src', 'dst', 'edge_attr_2', 'edge_attr_32', 'L0_gnn_W1', 'L0_gnn_b1', 'L0_gnn_W2', 'L0_gnn_b2',
        'L0_gnn_Wg', 'L0_gnn_bg', 'L1_gnn_weight', 'L1_gnn_root_w', 'L1_gnn_root_b', 'L2_gnn_w1_W', 'L2_gnn_w1_b',
        'L2_gnn_w2_W', 'L2_gnn_w2_b', 'L2_gnn_a', 'L3_gnn_W1', 'L3_gnn_b1', 'L3_gnn_W2', 'L3_gnn_b2']


def kernel(**inputs):
    import numpy as _np
    import concourse.bacc as _bacc
    from concourse.bass_utils import run_bass_kernel_spmd as _run

    nc = _bacc.Bacc("TRN2", target_bir_lowering=False, num_devices=1)
    arrays, aps = {}, {}
    for name in _INS:
        v = _np.ascontiguousarray(inputs[name])
        arrays[f"in_{name}"] = v
        aps[name] = nc.dram_tensor(f"in_{name}", v.shape, mybir.dt.from_np(v.dtype), kind="ExternalInput").ap()
    out = nc.dram_tensor("out_x", (N, D), F32, kind="ExternalOutput").ap()
    graph_layers(nc, aps, out)
    r = _run(nc, [arrays], core_ids=[0])
    return r.results[0]["out_x"]
```
